# Optimizing a Trainium2 kernel written in Bass

```python
import numpy as np
import jax
import jax.numpy as jnp

def _softmax(x, axis=-1):
    return jax.nn.softmax(x, axis=axis)

def _gelu(x):
    return jax.nn.gelu(x, approximate=True)

def _silu(x):
    return jax.nn.silu(x)

def _sigmoid(x):
    return jax.nn.sigmoid(x)

def _layernorm(x, axis=-1, eps=1e-05):
    m = jnp.mean(x, axis=axis, keepdims=True)
    v = jnp.var(x, axis=axis, keepdims=True)
    return (x - m) / jnp.sqrt(v + eps)

def _scatter_add(tgt, idx, src, axis=0):
    return tgt.at[idx].add(src)

def _segment_sum(src, seg, n):
    return jax.ops.segment_sum(src, seg, n)
kernel_name = 'mk_gnn_preln_d2_gnn_r8_460af6'

def setup_inputs(seed: int=0):
    np.random.seed(seed)
    _w = jnp.asarray

    def _rec_inputs():
        import jax
        import jax.numpy as jnp
        _gk = jax.random.key(seed)
        x = -0.0002949 + 1 * jax.random.normal(jax.random.fold_in(_gk, 1), (1250, 512), jnp.float32)
        _s = jax.random.randint(jax.random.fold_in(_gk, 2), (10000,), 0, 1250, jnp.int32)
        _d = jax.random.randint(jax.random.fold_in(_gk, 3), (10000,), 0, 1250, jnp.int32)
        _loop = jnp.arange(1250, dtype=jnp.int32)
        src = jnp.concatenate([_s, _d, _loop])
        dst = jnp.concatenate([_d, _s, _loop])
        _o = jnp.argsort(dst, stable=True)
        src = src[_o]
        dst = dst[_o]
        node_vec1 = jax.random.uniform(jax.random.fold_in(_gk, 12), (1250, 1), jnp.float32, 0.0, 0.999957)
        return (x, src, dst, node_vec1)
    x, src, dst, node_vec1 = _rec_inputs()

    def _L0_gnn_setup():
        import jax, jax.numpy as jnp
        import numpy as np
        N_NODES = 40962
        LATENT_DIM = 512
        N_EDGES = 81924
        NUM_BLOCKS = 4
        NUM_HEADS = 4
        NUM_FREQ = 32
        BASE_PERIOD = 16
        NOISE_EMB_DIM = 16
        EPS = 1e-05

        def _cond_layer_norm(x, cond, sw, sb, bw, bb):
            mu = jnp.mean(x, axis=-1, keepdims=True)
            var = jnp.var(x, axis=-1, keepdims=True)
            xn = (x - mu) * jax.lax.rsqrt(var + EPS)
            scale = cond @ sw + sb
            bias = cond @ bw + bb
            return xn * (1.0 + scale) + bias

        def _sparse_attention(x, src, dst, wq, bq, wk, bk, wv, bv, wo, bo):
            N, D = x.shape
            H, Dh = (NUM_HEADS, D // NUM_HEADS)
            q = (x @ wq + bq).reshape(N, H, Dh) * Dh ** (-0.5)
            k = (x @ wk + bk).reshape(N, H, Dh)
            v = (x @ wv + bv).reshape(N, H, Dh)
            scores = jnp.einsum('ehd,ehd->eh', q[src], k[dst])
            smax = jax.ops.segment_max(scores, src, num_segments=N)
            ex = jnp.exp(scores - smax[src])
            denom = jax.ops.segment_sum(ex, src, num_segments=N)
            attn = ex / denom[src]
            out = jax.ops.segment_sum(attn[:, :, None] * v[dst], src, num_segments=N)
            return out.reshape(N, D) @ wo + bo

        def _forward(x, edge_index, noise_levels, f_w1, f_b1, f_w2, f_b2, s1_w, s1_b, b1_w, b1_b, wq, bq, wk, bk, wv, bv, wo, bo, s2_w, s2_b, b2_w, b2_b, m_w1, m_b1, m_w2, m_b2):
            src, dst = (edge_index[0], edge_index[1])
            freqs = jnp.arange(1, NUM_FREQ + 1, dtype=x.dtype) * (2.0 * np.pi / BASE_PERIOD)
            ph = noise_levels * freqs
            emb = jnp.concatenate([jnp.sin(ph), jnp.cos(ph)], axis=-1)
            cond = jax.nn.silu(emb @ f_w1 + f_b1) @ f_w2 + f_b2
            for i in range(NUM_BLOCKS):
                y = _cond_layer_norm(x, cond, s1_w[i], s1_b[i], b1_w[i], b1_b[i])
                y = _sparse_attention(y, src, dst, wq[i], bq[i], wk[i], bk[i], wv[i], bv[i], wo[i], bo[i])
                x = x + y
                y = _cond_layer_norm(x, cond, s2_w[i], s2_b[i], b2_w[i], b2_b[i])
                y = jax.nn.relu(y @ m_w1[i] + m_b1[i]) @ m_w2[i] + m_b2[i]
                x = x + y
            return x
        key = jax.random.key(seed)
        ks = jax.random.split(key, 20)

        def w(k, shape, s=0.02):
            return jax.random.normal(k, shape, dtype=jnp.float32) * s
        D, B, C = (LATENT_DIM, NUM_BLOCKS, NOISE_EMB_DIM)
        z = lambda *s: jnp.zeros(s, jnp.float32)
        return {'latent_mesh_nodes': jax.random.normal(ks[0], (N_NODES, D), dtype=jnp.float32), 'edge_index': jax.random.randint(ks[1], (2, N_EDGES), 0, N_NODES, dtype=jnp.int32), 'noise_levels': jax.random.uniform(ks[2], (N_NODES, 1), dtype=jnp.float32), 'f_w1': w(ks[3], (2 * NUM_FREQ, C)), 'f_b1': z(C), 'f_w2': w(ks[4], (C, C)), 'f_b2': z(C), 's1_w': w(ks[5], (B, C, D)), 's1_b': z(B, D), 'b1_w': w(ks[6], (B, C, D)), 'b1_b': z(B, D), 'wq': w(ks[7], (B, D, D)), 'bq': z(B, D), 'wk': w(ks[8], (B, D, D)), 'bk': z(B, D), 'wv': w(ks[9], (B, D, D)), 'bv': z(B, D), 'wo': w(ks[10], (B, D, D)), 'bo': z(B, D), 's2_w': w(ks[11], (B, C, D)), 's2_b': z(B, D), 'b2_w': w(ks[12], (B, C, D)), 'b2_b': z(B, D), 'm_w1': w(ks[13], (B, D, D)), 'm_b1': z(B, D), 'm_w2': w(ks[14], (B, D, D)), 'm_b2': z(B, D)}
    _L0_gnn_all = _L0_gnn_setup()
    _L0_gnn_in = {k: v for k, v in _L0_gnn_all.items() if k in ('f_w1', 'f_b1', 'f_w2', 'f_b2', 's1_w', 's1_b', 'b1_w', 'b1_b', 'wq', 'bq', 'wk', 'bk', 'wv', 'bv', 'wo', 'bo', 's2_w', 's2_b', 'b2_w', 'b2_b', 'm_w1', 'm_b1', 'm_w2', 'm_b2')}
    del _L0_gnn_all

    def _L1_gnn_setup():
        import jax, jax.numpy as jnp
        import numpy as np
        N, E, D = (6250, 18750, 512)

        def _gcn_conv(x, src, dst, W, b, n):
            h = x @ W
            deg = jax.ops.segment_sum(jnp.ones_like(dst, dtype=x.dtype), dst, num_segments=n)
            dis = jnp.where(deg > 0, jax.lax.rsqrt(jnp.maximum(deg, 1.0)), 0.0)
            norm = dis[src] * dis[dst]
            msg = h[src] * norm[:, None]
            out = jax.ops.segment_sum(msg, dst, num_segments=n)
            return out + b
        key = jax.random.key(seed)
        k = jax.random.split(key, 6)
        x = jax.random.normal(k[0], (N, D), dtype=jnp.float32)
        edge_index = jax.random.randint(k[1], (2, E), 0, N, dtype=jnp.int64)
        s = 1.0 / np.sqrt(D)
        W1 = jax.random.uniform(k[2], (D, D), dtype=jnp.float32, minval=-s, maxval=s)
        b1 = jnp.zeros((D,), dtype=jnp.float32)
        W2 = jax.random.uniform(k[3], (D, D), dtype=jnp.float32, minval=-s, maxval=s)
        b2 = jnp.zeros((D,), dtype=jnp.float32)
        return {'x': x, 'edge_index': edge_index, 'W1': W1, 'b1': b1, 'W2': W2, 'b2': b2}
    _L1_gnn_all = _L1_gnn_setup()
    _L1_gnn_in = {k: v for k, v in _L1_gnn_all.items() if k in ('W1', 'b1', 'W2', 'b2')}
    del _L1_gnn_all
    return {'x': x, 'src': src, 'dst': dst, 'node_vec1': node_vec1, 'L0_gnn_f_w1': _L0_gnn_in['f_w1'], 'L0_gnn_f_b1': _L0_gnn_in['f_b1'], 'L0_gnn_f_w2': _L0_gnn_in['f_w2'], 'L0_gnn_f_b2': _L0_gnn_in['f_b2'], 'L0_gnn_s1_w': _L0_gnn_in['s1_w'], 'L0_gnn_s1_b': _L0_gnn_in['s1_b'], 'L0_gnn_b1_w': _L0_gnn_in['b1_w'], 'L0_gnn_b1_b': _L0_gnn_in['b1_b'], 'L0_gnn_wq': _L0_gnn_in['wq'], 'L0_gnn_bq': _L0_gnn_in['bq'], 'L0_gnn_wk': _L0_gnn_in['wk'], 'L0_gnn_bk': _L0_gnn_in['bk'], 'L0_gnn_wv': _L0_gnn_in['wv'], 'L0_gnn_bv': _L0_gnn_in['bv'], 'L0_gnn_wo': _L0_gnn_in['wo'], 'L0_gnn_bo': _L0_gnn_in['bo'], 'L0_gnn_s2_w': _L0_gnn_in['s2_w'], 'L0_gnn_s2_b': _L0_gnn_in['s2_b'], 'L0_gnn_b2_w': _L0_gnn_in['b2_w'], 'L0_gnn_b2_b': _L0_gnn_in['b2_b'], 'L0_gnn_m_w1': _L0_gnn_in['m_w1'], 'L0_gnn_m_b1': _L0_gnn_in['m_b1'], 'L0_gnn_m_w2': _L0_gnn_in['m_w2'], 'L0_gnn_m_b2': _L0_gnn_in['m_b2'], 'L1_gnn_W1': _L1_gnn_in['W1'], 'L1_gnn_b1': _L1_gnn_in['b1'], 'L1_gnn_W2': _L1_gnn_in['W2'], 'L1_gnn_b2': _L1_gnn_in['b2']}

def reference(x, src, dst, node_vec1, L0_gnn_f_w1, L0_gnn_f_b1, L0_gnn_f_w2, L0_gnn_f_b2, L0_gnn_s1_w, L0_gnn_s1_b, L0_gnn_b1_w, L0_gnn_b1_b, L0_gnn_wq, L0_gnn_bq, L0_gnn_wk, L0_gnn_bk, L0_gnn_wv, L0_gnn_bv, L0_gnn_wo, L0_gnn_bo, L0_gnn_s2_w, L0_gnn_s2_b, L0_gnn_b2_w, L0_gnn_b2_b, L0_gnn_m_w1, L0_gnn_m_b1, L0_gnn_m_w2, L0_gnn_m_b2, L1_gnn_W1, L1_gnn_b1, L1_gnn_W2, L1_gnn_b2):
    import jax
    import jax.numpy as jnp

    def _L0_gnn_ref(latent_mesh_nodes, edge_index, noise_levels, f_w1, f_b1, f_w2, f_b2, s1_w, s1_b, b1_w, b1_b, wq, bq, wk, bk, wv, bv, wo, bo, s2_w, s2_b, b2_w, b2_b, m_w1, m_b1, m_w2, m_b2):
        import jax, jax.numpy as jnp
        import numpy as np
        N_NODES = 40962
        LATENT_DIM = 512
        N_EDGES = 81924
        NUM_BLOCKS = 4
        NUM_HEADS = 4
        NUM_FREQ = 32
        BASE_PERIOD = 16
        NOISE_EMB_DIM = 16
        EPS = 1e-05

        def _cond_layer_norm(x, cond, sw, sb, bw, bb):
            mu = jnp.mean(x, axis=-1, keepdims=True)
            var = jnp.var(x, axis=-1, keepdims=True)
            xn = (x - mu) * jax.lax.rsqrt(var + EPS)
            scale = cond @ sw + sb
            bias = cond @ bw + bb
            return xn * (1.0 + scale) + bias

        def _sparse_attention(x, src, dst, wq, bq, wk, bk, wv, bv, wo, bo):
            N, D = x.shape
            H, Dh = (NUM_HEADS, D // NUM_HEADS)
            q = (x @ wq + bq).reshape(N, H, Dh) * Dh ** (-0.5)
            k = (x @ wk + bk).reshape(N, H, Dh)
            v = (x @ wv + bv).reshape(N, H, Dh)
            scores = jnp.einsum('ehd,ehd->eh', q[src], k[dst])
            smax = jax.ops.segment_max(scores, src, num_segments=N)
            ex = jnp.exp(scores - smax[src])
            denom = jax.ops.segment_sum(ex, src, num_segments=N)
            attn = ex / denom[src]
            out = jax.ops.segment_sum(attn[:, :, None] * v[dst], src, num_segments=N)
            return out.reshape(N, D) @ wo + bo

        def _forward(x, edge_index, noise_levels, f_w1, f_b1, f_w2, f_b2, s1_w, s1_b, b1_w, b1_b, wq, bq, wk, bk, wv, bv, wo, bo, s2_w, s2_b, b2_w, b2_b, m_w1, m_b1, m_w2, m_b2):
            src, dst = (edge_index[0], edge_index[1])
            freqs = jnp.arange(1, NUM_FREQ + 1, dtype=x.dtype) * (2.0 * np.pi / BASE_PERIOD)
            ph = noise_levels * freqs
            emb = jnp.concatenate([jnp.sin(ph), jnp.cos(ph)], axis=-1)
            cond = jax.nn.silu(emb @ f_w1 + f_b1) @ f_w2 + f_b2
            for i in range(NUM_BLOCKS):
                y = _cond_layer_norm(x, cond, s1_w[i], s1_b[i], b1_w[i], b1_b[i])
                y = _sparse_attention(y, src, dst, wq[i], bq[i], wk[i], bk[i], wv[i], bv[i], wo[i], bo[i])
                x = x + y
                y = _cond_layer_norm(x, cond, s2_w[i], s2_b[i], b2_w[i], b2_b[i])
                y = jax.nn.relu(y @ m_w1[i] + m_b1[i]) @ m_w2[i] + m_b2[i]
                x = x + y
            return x
        return _forward(latent_mesh_nodes, edge_index, noise_levels, f_w1, f_b1, f_w2, f_b2, s1_w, s1_b, b1_w, b1_b, wq, bq, wk, bk, wv, bv, wo, bo, s2_w, s2_b, b2_w, b2_b, m_w1, m_b1, m_w2, m_b2)

    def _L1_gnn_ref(x, edge_index, W1, b1, W2, b2):
        import jax, jax.numpy as jnp
        import numpy as np
        N, E, D = (6250, 18750, 512)

        def _gcn_conv(x, src, dst, W, b, n):
            h = x @ W
            deg = jax.ops.segment_sum(jnp.ones_like(dst, dtype=x.dtype), dst, num_segments=n)
            dis = jnp.where(deg > 0, jax.lax.rsqrt(jnp.maximum(deg, 1.0)), 0.0)
            norm = dis[src] * dis[dst]
            msg = h[src] * norm[:, None]
            out = jax.ops.segment_sum(msg, dst, num_segments=n)
            return out + b
        n = x.shape[0]
        loops = jnp.arange(n, dtype=edge_index.dtype)
        src = jnp.concatenate([edge_index[0], loops])
        dst = jnp.concatenate([edge_index[1], loops])
        h = _gcn_conv(x, src, dst, W1, b1, n)
        h = jax.nn.relu(h)
        return _gcn_conv(h, src, dst, W2, b2, n)
    edge_index = jnp.stack([src, dst])
    h = jnp.maximum(_layernorm(x, axis=-1), 0.0)
    x = x + _L0_gnn_ref(h, edge_index, node_vec1, L0_gnn_f_w1, L0_gnn_f_b1, L0_gnn_f_w2, L0_gnn_f_b2, L0_gnn_s1_w, L0_gnn_s1_b, L0_gnn_b1_w, L0_gnn_b1_b, L0_gnn_wq, L0_gnn_bq, L0_gnn_wk, L0_gnn_bk, L0_gnn_wv, L0_gnn_bv, L0_gnn_wo, L0_gnn_bo, L0_gnn_s2_w, L0_gnn_s2_b, L0_gnn_b2_w, L0_gnn_b2_b, L0_gnn_m_w1, L0_gnn_m_b1, L0_gnn_m_w2, L0_gnn_m_b2)
    h = jnp.maximum(_layernorm(x, axis=-1), 0.0)
    x = x + _L1_gnn_ref(h, edge_index, L1_gnn_W1, L1_gnn_b1, L1_gnn_W2, L1_gnn_b2)
    return x

_drawn_inputs = setup_inputs


def setup_inputs(seed=0):
    import zlib

    import numpy as np

    out = dict(_drawn_inputs(seed))
    spreads = {'L0_gnn_f_b1': (0.0, 0.8),
     'L0_gnn_f_b2': (0.0, 0.8),
     'L0_gnn_s1_b': (0.0, 0.744),
     'L0_gnn_b1_b': (0.0, 0.289),
     'L0_gnn_bq': (0.0, 0.8),
     'L0_gnn_bk': (0.0, 0.8),
     'L0_gnn_bv': (0.0, 0.1),
     'L0_gnn_bo': (0.0, 0.1),
     'L0_gnn_s2_b': (0.0, 0.45),
     'L0_gnn_b2_b': (0.0, 0.432),
     'L0_gnn_m_b1': (0.0, 0.1),
     'L0_gnn_m_b2': (0.0, 0.1),
     'L1_gnn_b1': (0.0, 0.341),
     'L1_gnn_b2': (0.0, 0.1)}
    factors = {'node_vec1': 8.0,
     'L0_gnn_f_w1': 8.0,
     'L0_gnn_f_w2': 8.0,
     'L0_gnn_s1_w': 8.0,
     'L0_gnn_b1_w': 8.0,
     'L0_gnn_wq': 4.653,
     'L0_gnn_wk': 4.522,
     'L0_gnn_s2_w': 8.0,
     'L0_gnn_b2_w': 8.0}
    for name, (base, spread) in spreads.items():
        noise = np.random.default_rng([zlib.crc32(name.encode()), seed]).standard_normal(out[name].shape)
        drawn = base * np.exp(spread * noise) if base else spread * noise
        out[name] = jnp.asarray(drawn.astype(out[name].dtype))
    for name, factor in factors.items():
        out[name] = (out[name] * factor).astype(out[name].dtype)
    return out
```

```python
from contextlib import ExitStack

import concourse.bass as bass
from concourse import mybir

ALU = mybir.AluOpType
ACT = mybir.ActivationFunctionType
F32 = mybir.dt.float32
F16 = mybir.dt.float16
BF16 = mybir.dt.bfloat16
I32 = mybir.dt.int32
AX_X = mybir.AxisListType.X

N = 1250
D = 512
E = 21250
L = 4
H = 4
DH = D // H
C = 16
NFREQ = 32
T = 125
NT = N // T
W = 2 * T
NC = NT // 2
KD = D // 128
EC = E // T
ECP = EC + 2
UNITS = 2 * H
EPS = 1e-5
SCALE = DH ** -0.5
BIG = 1e38
FLOOR = 1e30
MAGIC = 1.5 * 2.0 ** 23
COLS = [(0, 512), (512, 1024), (1024, N)]
PIECES = [(0, 4), (4, 8), (8, NT)]
AHEAD = 1
AHEAD_OF = "sb y yT yTp zC v_e ct ct_t ct_deg ct_e bst_out ttr Te zB k_e Tp oh_used".split()
LOW_ROWS = 112


def build(nc, x, src, dst, node_vec1, f_w1, f_b1, f_w2, f_b2, s1_w, s1_b, b1_w, b1_b, wq, bq, wk, bk, wv, bv,
          wo, bo, s2_w, s2_b, b2_w, b2_b, m_w1, m_b1, m_w2, m_b2, g_W1, g_b1, g_W2, g_b2, out):
    counts_dram = nc.dram_tensor("counts_scratch", [N, N], F32, kind="Internal").ap()
    bias_dram = nc.dram_tensor("edge_bias_scratch", [N, N], F32, kind="Internal").ap()

    with ExitStack() as ctx:
        def sb(name, shape, dt=F32):
            return ctx.enter_context(nc.sbuf_tensor(name, shape, dt))

        def sem(name):
            return ctx.enter_context(nc.semaphore(name))

        z = sb("z", [T, NT, D])
        arena = sb("arena", [128, 2 * KD * N + NT * D])
        qT = arena[:, 0:KD * N].rearrange("p (f n) -> p f n", f=KD)
        kT = arena[:, KD * N:2 * KD * N].rearrange("p (f n) -> p f n", f=KD)
        V = arena[0:T, 2 * KD * N:2 * KD * N + NT * D].rearrange("p (t d) -> p t d", t=NT)
        counts = arena[0:T, 0:NT * N].rearrange("p (t n) -> p t n", t=NT)
        pbuf = sb("pbuf", [T, 2 * N])
        P = pbuf[:, :].rearrange("p (b n) -> p b n", b=2)
        xn = pbuf[:, 0:2 * D].rearrange("p (u d) -> p u d", u=2)
        y = pbuf[:, 2 * D:4 * D].rearrange("p (u d) -> p u d", u=2)
        ptbuf = sb("ptbuf", [128, 2 * NT * W])
        PT = ptbuf[0:T, :].rearrange("p (b t n) -> p b t n", b=2, t=NT)
        yTc = ptbuf[:, 0:KD * W].rearrange("p (k n) -> p k n", k=KD)
        hTc = ptbuf[:, KD * W:2 * KD * W].rearrange("p (k n) -> p k n", k=KD)
        aggT = ptbuf[:, 0:KD * N].rearrange("p (k n) -> p k n", k=KD)
        edge_bias = sb("edge_bias", [T, 2 * N])
        bt = edge_bias[:, :].rearrange("p (u n) -> p u n", u=2)
        bias_stage = sb("bias_stage", [T, 2 * N])
        bst = bias_stage[:, :].rearrange("p (u n) -> p u n", u=2)
        weights = sb("weights", [128, 6, KD, D])
        WQ, WK, WV, WO, M1, M2 = (weights[:, i] for i in range(6))
        hs = weights[0:T, 2:5].rearrange("p a k d -> p (a k) d")[:, 0:NT, :]
        lnw = sb("lnw", [C + 1, 2, D])
        bvb = sb("bvb", [T, D])
        bob = sb("bob", [T, D])
        b2b = sb("b2b", [T, D])
        outTg = sb("outTg", [128, KD, W])
        qg = sb("qg", [128, KD, W])
        condT = sb("condT", [C + 1, N])
        condc = sb("condc", [C + 1, W])
        ident = sb("ident", [128, 128])
        cols = sb("cols", [128, 3 * L * KD + KD])
        eps = sb("eps", [T, 1])
        stats = sb("stats", [T, 2, 6])
        mv = sb("mv", [T, 2, 2])
        lnv = sb("lnv", [T, 2])
        r0 = sb("r0", [T, 2])
        nt_a = sb("nt_a", [T, 2])
        nt_b = sb("nt_b", [T, 2])
        nt_c = sb("nt_c", [T, 2])
        rstd = sb("rstd", [T, 2])
        ztmp = sb("ztmp", [T, 2, D])
        nmx = sb("nmx", [T, 2])
        den = sb("den", [T, 2])
        dmx = sb("dmx", [T, 2])
        rden = sb("rden", [T, 2])
        deg = sb("deg", [T, NT])
        dis = sb("dis", [T, NT])
        dis0 = sb("dis0", [T, NT])
        dis_a = sb("dis_a", [T, NT])
        dis_b = sb("dis_b", [T, NT])
        ones = sb("ones", [T, 128])
        diags = bias_stage[:, 0:N]
        disb = arena[:, NT * N:NT * N + N]
        oh_src = ptbuf[0:T, 0:N].bitcast(BF16).rearrange("p (b n) -> p b n", b=2)
        oh_dst = bias_stage[:, 2100:2100 + T + 1].bitcast(BF16).rearrange("p (b n) -> p b n", b=2)
        iota16 = ptbuf[0:T, N:N + N // 2].bitcast(F16)
        iota_i = ptbuf[0:T, 2 * N:3 * N].bitcast(I32)
        ln_count = ptbuf[0:T, 0:N]
        zeros16 = bias_stage[:, 1800:1800 + D // 2].bitcast(BF16)
        ct = pbuf[:, 0:N]
        edge_i = outTg[:, :, 0:T].bitcast(I32)
        edge_f = qg[:, :, 0:T]
        edgeT = bias_stage[:, 1400:1400 + 2 * ECP].rearrange("p (a e) -> p a e", a=2)
        nb = arena[0:2 * NFREQ, 12500:12500 + N]
        ph = arena[0:2 * NFREQ, 13750:13750 + N]
        phr = bias_stage[0:2 * NFREQ, 0:N]
        embT = edge_bias[0:2 * NFREQ, 0:N]
        h1T = edge_bias[0:C, N:2 * N]
        fw1 = sb("fw1", [2 * NFREQ, C])
        fw2 = sb("fw2", [C, C])
        fb = sb("fb", [C, 2])
        freq_i = sb("freq_i", [2 * NFREQ, 1], I32)
        freq = sb("freq", [2 * NFREQ, 1])
        offs = sb("offs", [2 * NFREQ, 1])
        brow = bias_stage[0:3 * L * KD + KD, N:N + 128]
        low_i = sb("low_i", [128, NT + 1], I32)
        low = sb("low", [128, NT + 1])
        mm_ = sb("mm_", [128, 2, 6])
        cand = sb("cand", [128, 2, 2 * NT])
        rel = sb("rel", [128, 2, 2 * NT])
        red = sb("red", [2 * NT, 1])
        rtab = sb("rtab", [1, 6 * NT])
        tab = sb("tab", [1, 3 * NT], I32)
        tab0 = sb("tab0", [1, NT], I32)

        ps = ctx.enter_context(nc.psum_tensor("ps", [128, 8, 512], F32))
        psf = ps[:, :, :].rearrange("p b n -> p (b n)")
        ps_S = psf[0:T, 0:N]
        ps_sb = ps[0:T, 0:4, :].rearrange("p (u a) n -> p u a n", u=2)
        ps_T = ps[:, 3:6, :]
        ps_yT = ps[:, 4:6, :]
        ps_q = ps[:, 6:8, :]

        s = {}
        for name in ("x_ld edge_ld small_ld brow_ld ident consts edge_f edge_t edgeT brow_t cols emb_u emb_r emb_f emb emb_h "
                     "h1 cond_mm condT rm rel cand cand_t red red_t tab prefix tabi onehot oh_used ct_mm ct ct_deg ct_t ct_e "
                     "bmax bln bmask bdone bst_out cnt_out ln_w0 "
                     "bn stats lnv r0 nw xn sb ysc y yTp yT condc condc_used "
                     "ldA ldLN ldO ldM q_mm q_e k_mm k_e v_mm v_e "
                     "S ttr exp dmx rden P Tp Te PV oT wo_mm zt zB st0 st1 bt qg "
                     "h_mm h_e o_mm zct zC "
                     "g_cnt g_x g_xz g_A g_dg g_diag g_bc g_disb g_hs_mm g_hs g_ag g_agd g_agT g_ft g_fin g_fz g_out z0 settled").split():
            s[name] = sem(name)
        block = ctx.enter_context(nc.Block())

        def rows(ap2):
            return ((0, LOW_ROWS), (LOW_ROWS, T))

        def settled(eng):
            eng.sem_inc(s["settled"], 1)

        @block.sync
        def _(sp):
            sp.dma_start(edge_i[0:128, 0, :], src[0:128 * T].rearrange("(j p) -> j p", p=T)).then_inc(s["edge_ld"], 16)
            sp.dma_start(edge_i[0:EC - 128, 1, :], src[128 * T:E].rearrange("(j p) -> j p", p=T)).then_inc(s["edge_ld"], 16)
            sp.dma_start(edge_i[0:128, 2, :], dst[0:128 * T].rearrange("(j p) -> j p", p=T)).then_inc(s["edge_ld"], 16)
            sp.dma_start(edge_i[0:EC - 128, 3, :], dst[128 * T:E].rearrange("(j p) -> j p", p=T)).then_inc(s["edge_ld"], 16)
            sp.dma_start(nb, node_vec1.rearrange("n a -> a n").to_broadcast([2 * NFREQ, N])).then_inc(s["small_ld"], 16)
            sp.dma_start(fw1[:, :], f_w1).then_inc(s["small_ld"], 16)
            sp.dma_start(fw2[:, :], f_w2).then_inc(s["small_ld"], 16)
            sp.dma_start(fb[:, 0:1], f_b1.rearrange("(c a) -> c a", a=1)).then_inc(s["small_ld"], 16)
            sp.dma_start(fb[:, 1:2], f_b2.rearrange("(c a) -> c a", a=1)).then_inc(s["small_ld"], 16)
            for i, b in enumerate((bq, bk, m_b1)):
                sp.dma_start(brow[i * L * KD:(i + 1) * L * KD, :], b.rearrange("l (k p) -> (l k) p", p=128)).then_inc(s["brow_ld"], 16)
            sp.dma_start(brow[3 * L * KD:3 * L * KD + KD, :], g_b1.rearrange("(k p) -> k p", p=128)).then_inc(s["brow_ld"], 16)
            for t in range(NT):
                sp.dma_start(z[:, t, :], x[t * T:(t + 1) * T, :]).then_inc(s["x_ld"], 16)

            def load_w(slot, w, name):
                sp.dma_start(slot, w.rearrange("(k p) n -> p k n", p=128)).then_inc(s[name], 16)

            def lay(w, l):
                return w[bass.ds(l, 1)].rearrange("a k n -> (a k) n") if not isinstance(l, int) else w[l]

            def row(b, l):
                return b[bass.ds(l, 1), :] if not isinstance(l, int) else b[l:l + 1, :]

            def load_attn(l):
                load_w(WQ, lay(wq, l), "ldA")
                load_w(WK, lay(wk, l), "ldA")
                load_w(WV, lay(wv, l), "ldA")
                sp.dma_start(bvb[:, :], row(bv, l).to_broadcast([T, D])).then_inc(s["ldA"], 16)

            def load_ln(l, sw, sbias, bw, bbias):
                sp.dma_start(lnw[0:C, 0, :], lay(sw, l)).then_inc(s["ldLN"], 16)
                sp.dma_start(lnw[C:C + 1, 0, :], row(sbias, l)).then_inc(s["ldLN"], 16)
                sp.dma_start(lnw[0:C, 1, :], lay(bw, l)).then_inc(s["ldLN"], 16)
                sp.dma_start(lnw[C:C + 1, 1, :], row(bbias, l)).then_inc(s["ldLN"], 16)

            def load_o(l):
                load_w(WO, lay(wo, l), "ldO")
                sp.dma_start(bob[:, :], row(bo, l).to_broadcast([T, D])).then_inc(s["ldO"], 16)

            def load_m(l):
                load_w(M1, lay(m_w1, l), "ldM")
                load_w(M2, lay(m_w2, l), "ldM")
                sp.dma_start(b2b[:, :], row(m_b2, l).to_broadcast([T, D])).then_inc(s["ldM"], 16)

            def load_stage(g, u):
                for a, b in ((0, LOW_ROWS), (LOW_ROWS, T)):
                    start = g * W + u * T + a
                    view = bias_dram[bass.ds(start, b - a), :] if not isinstance(g, int) else bias_dram[start:start + b - a, :]
                    sp.dma_start(bst[a:b, u, :], view).then_inc(s[f"st{u}"], 16)

            load_attn(0)
            load_ln(0, s1_w, s1_b, b1_w, b1_b)
            load_o(0)
            load_m(0)
            sp.wait_ge(s["ct_e"], AHEAD + 3 * NT)
            for t in range(NT):
                sp.dma_start(counts_dram[t * T:(t + 1) * T, :], counts[:, t, :]).then_inc(s["cnt_out"], 16)
            with sp.Fori(0, NT) as t:
                sp.wait_ge(s["bdone"], t + 1)
                sp.dma_start(bias_dram[bass.ds(t * T, T), :], P[:, 0, :]).then_inc(s["bst_out"], 16)
            sp.wait_ge(s["bst_out"], AHEAD + 16 * NT)
            load_stage(0, 0)
            load_stage(0, 1)

            def layer(l, last):
                sp.wait_ge(s["v_e"], AHEAD + 2 * NC * (l + 1))
                settled(sp)
                sp.wait_ge(s["v_mm"], NC * (l + 1))
                settled(sp)
                sp.wait_ge(s["sb"], AHEAD + 2 * NC * l + NC)
                if not last:
                    load_attn(l + 1)
                else:
                    load_w(WQ, g_W1, "ldA")
                    load_w(WK, g_W2, "ldA")
                    sp.dma_start(bvb[:, :], g_b2.rearrange("(a n) -> a n", a=1).to_broadcast([T, D])).then_inc(s["ldA"], 16)
                load_ln(l, s2_w, s2_b, b2_w, b2_b)
                with sp.Fori(0, NC - 1) as g:
                    for u in range(2):
                        sp.wait_ge(s["bt"], (l * NC + g) * 2 + u + 1)
                        load_stage(g + 1, u)
                for u in range(2):
                    sp.wait_ge(s["bt"], (l * NC + NC - 1) * 2 + u + 1)
                    if not last:
                        load_stage(0, u)
                sp.wait_ge(s["zB"], AHEAD + 2 * NC * (l + 1))
                if not last:
                    load_o(l + 1)
                else:
                    sp.wait_ge(s["cnt_out"], 16 * NT)
                    for t in range(NT):
                        sp.dma_start(counts[:, t, :], counts_dram[t * T:(t + 1) * T, :]).then_inc(s["g_cnt"], 16)
                sp.wait_ge(s["sb"], AHEAD + 2 * NC * (l + 1))
                if not last:
                    load_ln(l + 1, s1_w, s1_b, b1_w, b1_b)
                sp.wait_ge(s["zC"], AHEAD + 2 * NC * (l + 1))
                if not last:
                    load_m(l + 1)

            with sp.Fori(0, L - 1) as l:
                layer(l, False)
            layer(L - 1, True)
            xs = edge_bias[:, 0:2 * D].rearrange("p (u d) -> p u d", u=2)
            for c in range(NC):
                if c:
                    sp.wait_ge(s["g_xz"], c)
                for u in range(2):
                    sp.dma_start(xs[:, u, :], x[(2 * c + u) * T:(2 * c + u + 1) * T, :]).then_inc(s["g_x"], 16)
            for t in range(NT):
                sp.wait_ge(s["g_fz"], t + 1)
                sp.dma_start(out[t * T:(t + 1) * T, :], z[:, t, :]).then_inc(s["g_out"], 16)
            sp.wait_ge(s["g_out"], 16 * NT)

        @block.gpsimd
        def _(pool):
            g = nc.gpsimd
            for name in AHEAD_OF:
                pool.sem_inc(s[name], AHEAD)
            g.memset(ident[:, :], 0.0).then_inc(s["ident"], 1)
            pool.wait_ge(s["ident"], 1)
            g.affine_select(out=ident[:, :], in_=ident[:, :], compare_op=ALU.not_equal, fill=1.0, base=0,
                            pattern=[[-1, 128]], channel_multiplier=1).then_inc(s["ident"], 1)
            g.iota(iota_i, pattern=[[1, N]], base=0, channel_multiplier=0).then_inc(s["consts"], 1)
            pool.wait_ge(s["consts"], 1)
            g.iota(low_i[:, 0:NT], pattern=[[T, NT]], base=0, channel_multiplier=0).then_inc(s["consts"], 1)
            pool.wait_ge(s["consts"], 2)
            g.iota(low_i[:, NT:NT + 1], pattern=[[0, 1]], base=0, channel_multiplier=1).then_inc(s["consts"], 1)
            pool.wait_ge(s["consts"], 3)
            g.iota(freq_i[0:NFREQ, :], pattern=[[0, 1]], base=1, channel_multiplier=1).then_inc(s["consts"], 1)
            pool.wait_ge(s["consts"], 4)
            g.iota(freq_i[NFREQ:2 * NFREQ, :], pattern=[[0, 1]], base=1, channel_multiplier=1).then_inc(s["consts"], 1)
            pool.wait_ge(s["consts"], 5)
            g.memset(offs[0:NFREQ, :], 0.0).then_inc(s["consts"], 1)
            pool.wait_ge(s["consts"], 6)
            g.memset(offs[NFREQ:2 * NFREQ, :], 0.25).then_inc(s["consts"], 1)
            pool.wait_ge(s["consts"], 7)
            g.memset(zeros16[:, :], 0.0).then_inc(s["consts"], 1)
            pool.wait_ge(s["consts"], 8)
            g.memset(eps[:, :], EPS).then_inc(s["consts"], 1)
            pool.wait_ge(s["consts"], 9)
            g.memset(condT[:, :], 1.0).then_inc(s["consts"], 1)
            pool.wait_ge(s["consts"], 10)
            g.memset(edgeT[:, :, EC:ECP], -1.0).then_inc(s["consts"], 1)
            pool.wait_ge(s["consts"], 11)
            g.memset(ones[:, :], 1.0).then_inc(s["consts"], 1)
            pool.wait_ge(s["consts"], 12)

            def cond_chunk(f, c):
                pool.wait_ge(s["sb"], AHEAD + f)
                settled(pool)
                g.tensor_copy(condc[:, :], condT[:, bass.ds(c * W, W)]).then_inc(s["condc"], 1)

            def q_head(G, g_next, h):
                settled(pool)
                g.tensor_copy(qg[:, h, :], qT[:, h, bass.ds(g_next * W, W)]).then_inc(s["qg"], 1)

            def bias_tile(G, u):
                pool.wait_ge(s[f"st{u}"], 32 * (G + 1))
                settled(pool)
                g.tensor_copy(bt[:, u, :], bst[:, u, :]).then_inc(s["bt"], 1)

            pool.wait_ge(s["condT"], 3)
            with pool.Fori(0, L) as l:
                with pool.Fori(0, NC) as c:
                    cond_chunk(2 * NC * l + c, c)
                pool.wait_ge(s["q_e"], KD * NC * (l + 1))
                for h in range(H):
                    q_head(l * NC, 0, h)
                for u in range(2):
                    bias_tile(l * NC, u)
                with pool.Fori(0, NC - 1) as g_:
                    G = l * NC + g_
                    for h in range(3):
                        pool.wait_ge(s["S"], UNITS * G + 2 * h + 2)
                        q_head(G + 1, g_ + 1, h)
                    pool.wait_ge(s["ttr"], AHEAD + (UNITS * G + UNITS - 1))
                    bias_tile(G + 1, 0)
                    pool.wait_ge(s["S"], UNITS * G + UNITS)
                    q_head(G + 1, g_ + 1, 3)
                    pool.wait_ge(s["ttr"], AHEAD + UNITS * G + UNITS)
                    bias_tile(G + 1, 1)
                with pool.Fori(0, NC) as c:
                    cond_chunk(2 * NC * l + NC + c, c)

        @block.scalar
        def _(act):
            sc = nc.scalar
            act.wait_ge(s["consts"], 12)
            act.wait_ge(s["emb_f"], 1)
            sc.activation(embT, phr, ACT.Sin, scale=6.2831850).then_inc(s["emb"], 1)
            act.wait_ge(s["emb_h"], 3)
            act.wait_ge(s["small_ld"], 16 * 5)
            sc.activation(h1T, psf[0:C, 0:N], ACT.Silu, bias=fb[:, 0:1]).then_inc(s["h1"], 1)
            sc.preload_act_table_set("natural_log_exp_and_others")
            for i, (a, b) in enumerate(COLS):
                act.wait_ge(s["cond_mm"], 3)
                sc.activation(condT[0:C, a:b], psf[0:C, 2048 + a:2048 + b], ACT.Identity, bias=fb[:, 1:2]).then_inc(s["condT"], 1)
            with act.Fori(0, NT) as t:
                act.wait_ge(s["ct_mm"], t + 1)
                act.wait_ge(s["ct_t"], AHEAD + 3 * t)
                act.wait_ge(s["ct_deg"], AHEAD + t)
                sc.activation(ct, ps_S, ACT.Copy).then_inc(s["ct"], 1)
            with act.Fori(0, NT) as t:
                act.wait_ge(s["bmax"], t + 1)
                sc.activation(ln_count, P[:, 1, :], ACT.Ln).then_inc(s["bln"], 1)

            def rsqrt0(f):
                act.wait_ge(s["stats"], f + 1)
                sc.activation(lnv[:, :], mv[:, :, 1], ACT.Ln, bias=eps[:, :]).then_inc(s["lnv"], 1)
                act.wait_ge(s["lnv"], f + 1)
                sc.activation(r0[:, :], lnv[:, :], ACT.Exp, scale=-0.5).then_inc(s["r0"], 1)

            def yT_out(f):
                act.wait_ge(s["yTp"], AHEAD + f + 1)
                sc.activation(yTc.rearrange("p (a k) n -> p a (k n)", a=2), ps_yT[:, :, 0:2 * W], ACT.Copy).then_inc(s["yT"], 1)

            def q_out(l, c):
                act.wait_ge(s["q_mm"], l * NC + c + 1)
                for j in range(KD):
                    sc.activation(qT[:, j, bass.ds(c * W, W)], ps_q[:, j // 2, (j % 2) * W:(j % 2 + 1) * W], ACT.Identity,
                                  bias=cols[:, bass.ds(l * KD + j, 1)], scale=SCALE).then_inc(s["q_e"], 1)

            def h_out(l, c):
                act.wait_ge(s["h_mm"], l * NC + c + 1)
                for j in range(KD):
                    sc.activation(hTc[:, j, :], ps_q[:, j // 2, (j % 2) * W:(j % 2 + 1) * W], ACT.Relu,
                                  bias=cols[:, bass.ds(2 * L * KD + l * KD + j, 1)]).then_inc(s["h_e"], 1)

            def exp_unit(U, u):
                act.wait_ge(s["ttr"], AHEAD + U + 1)
                if u is not None:
                    sc.activation(P[:, u, :], P[:, u, :], ACT.Exp, bias=nmx[:, u:u + 1], scale=-1.0,
                                  accum_out=den[:, u:u + 1]).then_inc(s["exp"], 1)

            def turn_out(U, h, u):
                for i, (a, b) in enumerate(PIECES):
                    act.wait_ge(s["Tp"], AHEAD + 3 * U + i + 1)
                    sc.activation(PT[:, h % 2, a:b, u * T:(u + 1) * T],
                                  ps_T[0:T, i, 0:(b - a) * T].rearrange("p (t n) -> p t n", n=T), ACT.Copy).then_inc(s["Te"], 1)

            def attn_out(G, h):
                act.wait_ge(s["PV"], H * G + h + 1)
                sc.activation(outTg[:, h, :], ps_q[:, h % 2, 0:W], ACT.Copy).then_inc(s["oT"], 1)

            def attn_group(G, last):
                for k in range(UNITS):
                    h, u = k // 2, k % 2
                    turn_out(UNITS * G + k, h, u)
                    if k + 2 < UNITS or not last:
                        exp_unit(UNITS * G + k + 2, u)
                    if u == 1 and h >= 1:
                        attn_out(G, h - 1)
                attn_out(G, H - 1)

            for c in range(NC):
                rsqrt0(c)

            F0 = NC
            with act.Fori(0, L) as l:
                f = 2 * NC * l
                rsqrt0(F0 + f)
                with act.Fori(0, NC - 1) as c:
                    yT_out(f + c)
                    rsqrt0(F0 + f + c + 1)
                    q_out(l, c)
                yT_out(f + NC - 1)
                q_out(l, NC - 1)
                exp_unit(UNITS * NC * l, 0)
                exp_unit(UNITS * NC * l + 1, 1)
                with act.Fori(0, NC - 1) as g_:
                    attn_group(l * NC + g_, False)
                attn_group(l * NC + NC - 1, True)
                f2 = 2 * NC * l + NC
                rsqrt0(F0 + f2)
                with act.Fori(0, NC - 1) as c:
                    yT_out(f2 + c)
                    rsqrt0(F0 + f2 + c + 1)
                    h_out(l, c)
                yT_out(f2 + NC - 1)
                h_out(l, NC - 1)
            fg = 2 * NC * L
            act.wait_ge(s["g_dg"], 1)
            sc.activation(dis_a[:, :], dis_b[:, :], ACT.Ln).then_inc(s["g_dg"], 1)
            act.wait_ge(s["g_dg"], 2)
            sc.activation(dis0[:, :], dis_a[:, :], ACT.Exp, scale=-0.5).then_inc(s["g_dg"], 1)
            for c in range(NC):
                rsqrt0(F0 + fg + c)
                yT_out(fg + c)
            for j in range(KD):
                act.wait_ge(s["g_agd"], j + 1)
                sc.activation(aggT[:, j, :], aggT[:, j, :], ACT.Relu,
                              bias=cols[:, 3 * L * KD + j:3 * L * KD + j + 1]).then_inc(s["g_agT"], 1)

        @block.vector
        def _(dve):
            v = nc.vector
            dve.wait_ge(s["edge_ld"], 16 * 4)
            for i, r in ((0, 128), (1, EC - 128), (2, 128), (3, EC - 128)):
                e = v.tensor_copy(edge_f[0:r, i, :], edge_i[0:r, i, :])
            e.then_inc(s["edge_f"], 1)
            dve.wait_ge(s["consts"], 12)
            v.tensor_copy(low[:, :], low_i[:, :]).then_inc(s["prefix"], 1)
            v.tensor_copy(iota16, iota_i)
            v.tensor_scalar(freq[:, :], freq_i[:, :], 1.0 / 16, None, ALU.mult).then_inc(s["prefix"], 1)
            dve.wait_ge(s["prefix"], 2)
            dve.wait_ge(s["small_ld"], 16 * 5)
            v.tensor_scalar(ph, nb, freq[:, 0:1], offs[:, 0:1], ALU.mult, ALU.add).then_inc(s["emb_u"], 1)
            dve.wait_ge(s["emb_u"], 1)
            v.tensor_scalar(phr, ph, MAGIC, -MAGIC, ALU.add, ALU.add).then_inc(s["emb_r"], 1)
            dve.wait_ge(s["emb_r"], 1)
            v.tensor_tensor(phr, ph, phr, ALU.subtract).then_inc(s["emb_f"], 1)
            dve.wait_ge(s["edge_f"], 1)
            for hf, r in ((0, 128), (1, EC - 128)):
                v.tensor_reduce(mm_[0:r, hf, 0:1], edge_f[0:r, 2 + hf, :], AX_X, ALU.max)
                v.tensor_reduce(mm_[0:r, hf, 1:2], edge_f[0:r, 2 + hf, :], AX_X, ALU.min)
                v.tensor_scalar(mm_[0:r, hf, 4:5], low[0:r, NT:NT + 1], -1.0, float(ECP - 128 * hf), ALU.mult, ALU.add)
                e = v.tensor_scalar(mm_[0:r, hf, 5:6], low[0:r, NT:NT + 1], float(1 + 128 * hf), None, ALU.add)
            e.then_inc(s["rm"], 1)
            dve.wait_ge(s["rm"], 1)
            for hf, r in ((0, 128), (1, EC - 128)):
                v.tensor_scalar(mm_[0:r, hf, 2:3], mm_[0:r, hf, 1:2], float(-T), None, ALU.add)
                e = v.tensor_scalar(rel[0:r, hf, NT:2 * NT], low[0:r, 0:NT], mm_[0:r, hf, 0:1], None, ALU.is_le)
            e.then_inc(s["rel"], 1)
            dve.wait_ge(s["rel"], 1)
            for hf, r in ((0, 128), (1, EC - 128)):
                e = v.scalar_tensor_tensor(out=rel[0:r, hf, 0:NT], in0=low[0:r, 0:NT], scalar=mm_[0:r, hf, 2:3],
                                           in1=rel[0:r, hf, NT:2 * NT], op0=ALU.is_gt, op1=ALU.mult)
            e.then_inc(s["rel"], 1)
            dve.wait_ge(s["rel"], 2)
            for hf, r in ((0, 128), (1, EC - 128)):
                v.tensor_scalar(cand[0:r, hf, 0:NT], rel[0:r, hf, 0:NT], mm_[0:r, hf, 4:5], None, ALU.mult)
                e = v.tensor_scalar(cand[0:r, hf, NT:2 * NT], rel[0:r, hf, 0:NT], mm_[0:r, hf, 5:6], None, ALU.mult)
            e.then_inc(s["cand"], 1)
            dve.wait_ge(s["edge_t"], 1)
            v.tensor_copy(edgeT[:, :, 0:EC], ps[0:T, 7, 0:2 * EC].rearrange("p (a e) -> p a e", a=2)).then_inc(s["edgeT"], 1)
            dve.wait_ge(s["brow_t"], 1)
            v.tensor_scalar(cols[:, 0:L * KD], ps[:, 6, 0:L * KD], SCALE, None, ALU.mult)
            v.tensor_copy(cols[:, L * KD:], ps[:, 6, L * KD:3 * L * KD + KD]).then_inc(s["cols"], 1)
            dve.wait_ge(s["cand_t"], 1)
            v.tensor_reduce(red[:, :], ps[0:2 * NT, 5, 0:EC], AX_X, ALU.max).then_inc(s["red"], 1)
            dve.wait_ge(s["red_t"], 1)
            n_tab = [0]

            def tab_step(ins):
                n_tab[0] += 1
                ins.then_inc(s["tab"], 1)
                dve.wait_ge(s["tab"], n_tab[0])

            R = [rtab[:, i * NT:(i + 1) * NT] for i in range(6)]
            tab_step(v.tensor_copy(rtab[:, 0:2 * NT], ps[0:1, 5, 256:256 + 2 * NT]))
            tab_step(v.tensor_tensor(R[3], R[0], R[1], ALU.add))
            tab_step(v.tensor_scalar(R[4], R[3], float(-ECP), 1.0, ALU.add, ALU.max))
            tab_step(v.tensor_scalar(R[2], R[0], -1.0, float(ECP), ALU.mult, ALU.add))
            tab_step(v.tensor_scalar(tab[:, 0:NT], R[2], float(ECP - 4), None, ALU.min))
            tab_step(v.tensor_scalar(tab0[:, :], R[4], 1.0, None, ALU.add))
            tab_step(v.tensor_scalar(tab[:, NT:2 * NT], tab0[:, :], 1, None, ALU.arith_shift_right))
            tab_step(v.tensor_copy(R[5], tab[:, NT:2 * NT]))
            tab_step(v.memset(rtab[:, 0:1], 0.0))
            for t in range(1, NT):
                tab_step(v.tensor_tensor(rtab[:, t:t + 1], rtab[:, t - 1:t], R[5][:, t - 1:t], ALU.add))
            v.tensor_copy(tab[:, 2 * NT:3 * NT], R[0]).then_inc(s["tabi"], 1)
            dve.wait_ge(s["tabi"], 1)
            dve.wait_ge(s["edgeT"], 1)

            with dve.Fori(0, NT) as t:
                first = dve.value_load(tab[0:1, bass.ds(t, 1)], min_val=0, max_val=ECP - 4)
                pairs = dve.value_load(tab[0:1, bass.ds(t + NT, 1)], min_val=1, max_val=EC // 2)
                before = dve.value_load(tab[0:1, bass.ds(t + 2 * NT, 1)], min_val=0, max_val=EC // 2 * NT)
                with dve.Fori(0, pairs) as i:
                    for b in range(2):
                        chunk = (first + i * 2 + b).with_bounds(min_val=0, max_val=ECP - 1)
                        dve.wait_ge(s["oh_used"], AHEAD + (before + i) * 2 + b)
                        v.tensor_scalar(oh_dst[:, b, 0:T], iota16[:, bass.ds(t * T, T)],
                                        edgeT[:, 1, bass.ds(chunk, 1)], None, ALU.is_equal)
                        v.tensor_scalar(oh_src[:, b, :], iota16, edgeT[:, 0, bass.ds(chunk, 1)], None,
                                        ALU.is_equal).then_inc(s["onehot"], 1)
                dve.wait_ge(s["ct"], AHEAD + t + 1)
                v.tensor_reduce(deg[:, bass.ds(t, 1)], ct, AX_X, ALU.add).then_inc(s["ct_deg"], 1)
                for p, (a, b) in enumerate(PIECES):
                    dve.wait_ge(s["ct_t"], AHEAD + t * 3 + p + 1)
                    v.tensor_copy(counts[:, a:b, bass.ds(t * T, T)],
                                  ps_T[0:T, p, 0:(b - a) * T].rearrange("p (t n) -> p t n", n=T)).then_inc(s["ct_e"], 1)

            dve.wait_ge(s["ct_e"], AHEAD + 3 * NT)
            with dve.Fori(0, NT) as t:
                v.tensor_scalar(P[:, 1, :], counts[:, bass.ds(t, 1), :].rearrange("p a n -> p (a n)"), 1.0, None,
                                ALU.max).then_inc(s["bmax"], 1)
                dve.wait_ge(s["bst_out"], AHEAD + t * 16)
                v.tensor_scalar(P[:, 0, :], counts[:, bass.ds(t, 1), :].rearrange("p a n -> p (a n)"), 0.0, -BIG,
                                ALU.is_equal, ALU.mult).then_inc(s["bmask"], 1)
                dve.wait_ge(s["bln"], t + 1)
                dve.wait_ge(s["bmask"], t + 1)
                v.tensor_tensor(P[:, 0, :], P[:, 0, :], ln_count, ALU.add).then_inc(s["bdone"], 1)

            def front_stats(f, c):
                for u in range(2):
                    e = v.bn_stats(stats[:, u, :], tile_of(c, u))
                e.then_inc(s["bn"], 1)
                dve.wait_ge(s["bn"], f + 1)
                settled(dve)
                for u in range(2):
                    e = v.bn_aggr(mv[:, u, :], stats[:, u, :])
                e.then_inc(s["stats"], 1)

            def tile_of(c, u):
                i = 2 * c + u
                return z[:, i, :] if isinstance(i, int) else z[:, bass.ds(i, 1), :].rearrange("p a d -> p (a d)")

            def front_norm(f, c):
                dve.wait_ge(s["r0"], f + 1)
                dve.wait_ge(s["stats"], f + 1)
                v.scalar_tensor_tensor(out=nt_a[:, :], in0=mv[:, :, 1], scalar=EPS, in1=r0[:, :], op0=ALU.add,
                                       op1=ALU.mult).then_inc(s["nw"], 1)
                dve.wait_ge(s["nw"], 4 * f + 1)
                v.tensor_tensor(nt_b[:, :], nt_a[:, :], r0[:, :], ALU.mult).then_inc(s["nw"], 1)
                dve.wait_ge(s["nw"], 4 * f + 2)
                v.tensor_scalar(nt_c[:, :], nt_b[:, :], -0.5, 1.5, ALU.mult, ALU.add).then_inc(s["nw"], 1)
                dve.wait_ge(s["nw"], 4 * f + 3)
                v.tensor_tensor(rstd[:, :], nt_c[:, :], r0[:, :], ALU.mult).then_inc(s["nw"], 1)
                dve.wait_ge(s["nw"], 4 * f + 4)
                for u in range(2):
                    e = v.tensor_scalar(xn[:, u, :], tile_of(c, u), mv[:, u, 0:1], rstd[:, u:u + 1], ALU.subtract, ALU.mult)
                e.then_inc(s["xn"], 1)

            def front_mod(f):
                dve.wait_ge(s["sb"], AHEAD + f + 1)
                dve.wait_ge(s["xn"], F0 + f + 1)
                dve.wait_ge(s["yTp"], AHEAD + f)
                for u in range(2):
                    e = v.scalar_tensor_tensor(out=y[:, u, :], in0=ps_sb[:, u, 0, :], scalar=1.0, in1=xn[:, u, :],
                                               op0=ALU.add, op1=ALU.mult)
                e.then_inc(s["ysc"], 1)
                dve.wait_ge(s["ysc"], f + 1)
                for u in range(2):
                    e = v.tensor_tensor(y[:, u, :], y[:, u, :], ps_sb[:, u, 1, :], ALU.add)
                e.then_inc(s["y"], 1)

            F0 = NC
            dve.wait_ge(s["x_ld"], 16 * NT)
            dve.wait_ge(s["bst_out"], AHEAD + 16 * NT)
            for c in range(NC):
                front_stats(c, c)
                front_norm(c, c)
                dve.wait_ge(s["xn"], c + 1)
                v.tensor_scalar(z[:, 2 * c:2 * c + 2, :], xn, 0.0, None, ALU.max).then_inc(s["z0"], 1)

            def k_out(l, c):
                dve.wait_ge(s["k_mm"], l * NC + c + 1)
                for j in range(KD):
                    v.tensor_scalar(kT[:, j, bass.ds(c * W, W)], ps_yT[:, j // 2, (j % 2) * W:(j % 2 + 1) * W],
                                    cols[:, bass.ds(l * KD + (L * KD + j), 1)], None, ALU.add).then_inc(s["k_e"], 1)

            def v_out(l, c):
                dve.wait_ge(s["ldA"], 64 * (l + 1))
                dve.wait_ge(s["v_mm"], l * NC + c + 1)
                for u in range(2):
                    v.tensor_tensor(V[:, bass.ds(2 * c + u, 1), :].rearrange("p a d -> p (a d)"), ps_q[0:T, u, :], bvb[:, :],
                                    ALU.add).then_inc(s["v_e"], 1)

            def softmax(G, U, u, first):
                dve.wait_ge(s["S"], U + 1)
                dve.wait_ge(s["bt"], 2 * G + u + 1)
                if not first:
                    dve.wait_ge(s["Tp"], AHEAD + (3 * (U - 1)))
                settled(dve)
                v.tensor_tensor_reduce(out=P[:, u, :], in0=ps_S, in1=bt[:, u, :], scale=-1.0, scalar=FLOOR,
                                       op0=ALU.add, op1=ALU.min, accum_out=nmx[:, u:u + 1]).then_inc(s["ttr"], 1)
                dve.wait_ge(s["exp"], U + 1)
                v.tensor_scalar(dmx[:, u:u + 1], den[:, u:u + 1], 1e-30, None, ALU.max).then_inc(s["dmx"], 1)
                dve.wait_ge(s["dmx"], U + 1)
                v.reciprocal(rden[:, u:u + 1], dmx[:, u:u + 1]).then_inc(s["rden"], 1)
                dve.wait_ge(s["rden"], U + 1)
                v.tensor_scalar(P[:, u, :], P[:, u, :], rden[:, u:u + 1], None, ALU.mult).then_inc(s["P"], 1)

            def attn_add(l, g_):
                dve.wait_ge(s["ldO"], 32 * (l + 1))
                G = l * NC + g_
                for u in range(2):
                    dve.wait_ge(s["wo_mm"], 2 * G + u + 1)
                    v.tensor_tensor(ztmp[:, u, :], ps_q[0:T, u, :], bob[:, :], ALU.add).then_inc(s["zt"], 1)
                for u in range(2):
                    dve.wait_ge(s["zt"], 2 * G + u + 1)
                    v.tensor_tensor(tile_of(g_, u), tile_of(g_, u), ztmp[:, u, :], ALU.add).then_inc(s["zB"], 1)

            def mlp_add(l, c):
                dve.wait_ge(s["ldM"], 48 * (l + 1))
                a = l * NC + c
                for u in range(2):
                    dve.wait_ge(s["o_mm"], 2 * a + u + 1)
                    v.tensor_tensor(ztmp[:, u, :], ps_q[0:T, u, :], b2b[:, :], ALU.add).then_inc(s["zct"], 1)
                for u in range(2):
                    dve.wait_ge(s["zct"], 2 * a + u + 1)
                    v.tensor_tensor(tile_of(c, u), tile_of(c, u), ztmp[:, u, :], ALU.add).then_inc(s["zC"], 1)

            def attn_chunk(l, g_, last):
                G = l * NC + g_
                for k in range(2, UNITS if last else UNITS + 2):
                    softmax(G + k // UNITS, UNITS * G + k, k % 2, False)
                attn_add(l, g_)

            dve.wait_ge(s["z0"], NC)
            with dve.Fori(0, L) as l:
                f = 2 * NC * l
                dve.wait_ge(s["zC"], AHEAD + f)
                front_stats(F0 + f, 0)
                front_norm(F0 + f, 0)
                front_mod(f)
                with dve.Fori(0, NC - 1) as c:
                    front_stats(F0 + f + c + 1, c + 1)
                    k_out(l, c)
                    front_norm(F0 + f + c + 1, c + 1)
                    front_mod(f + c + 1)
                    v_out(l, c)
                k_out(l, NC - 1)
                v_out(l, NC - 1)
                for u in range(2):
                    softmax(l * NC, UNITS * NC * l + u, u, True)
                with dve.Fori(0, NC - 1) as g_:
                    attn_chunk(l, g_, False)
                attn_chunk(l, NC - 1, True)
                dve.wait_ge(s["zB"], AHEAD + f + 2 * NC)
                dve.wait_ge(s["Tp"], AHEAD + 3 * UNITS * NC * (l + 1))
                f2 = 2 * NC * l + NC
                front_stats(F0 + f2, 0)
                front_norm(F0 + f2, 0)
                front_mod(f2)
                with dve.Fori(0, NC - 1) as c:
                    front_stats(F0 + f2 + c + 1, c + 1)
                    front_norm(F0 + f2 + c + 1, c + 1)
                    front_mod(f2 + c + 1)
                    mlp_add(l, c)
                mlp_add(l, NC - 1)

            xs = edge_bias[:, 0:2 * D].rearrange("p (u d) -> p u d", u=2)
            v.tensor_scalar(dis_b[:, :], deg[:, :], 1.0, None, ALU.add).then_inc(s["g_dg"], 1)
            dve.wait_ge(s["g_dg"], 3)
            v.tensor_tensor(dis_a[:, :], dis_b[:, :], dis0[:, :], ALU.mult).then_inc(s["g_dg"], 1)
            dve.wait_ge(s["g_dg"], 4)
            v.tensor_tensor(dis_a[:, :], dis_a[:, :], dis0[:, :], ALU.mult).then_inc(s["g_dg"], 1)
            dve.wait_ge(s["g_dg"], 5)
            v.tensor_scalar(dis_b[:, :], dis_a[:, :], -0.5, 1.5, ALU.mult, ALU.add).then_inc(s["g_dg"], 1)
            dve.wait_ge(s["g_dg"], 6)
            v.tensor_tensor(dis[:, :], dis_b[:, :], dis0[:, :], ALU.mult).then_inc(s["g_dg"], 1)
            dve.wait_ge(s["g_dg"], 7)
            for t in range(NT):
                e = v.tensor_scalar(diags[:, t * T:(t + 1) * T], ident[0:T, 0:T], dis[:, t:t + 1], None, ALU.mult)
            e.then_inc(s["g_diag"], 1)
            dve.wait_ge(s["g_cnt"], 16 * NT)
            for t in range(NT):
                e = v.tensor_tensor(counts[:, t, t * T:(t + 1) * T], counts[:, t, t * T:(t + 1) * T], ident[0:T, 0:T], ALU.add)
            e.then_inc(s["g_A"], 1)
            fg = 2 * NC * L
            dve.wait_ge(s["zC"], AHEAD + fg)
            for c in range(NC):
                dve.wait_ge(s["g_x"], 32 * (c + 1))
                v.tensor_tensor(z[:, 2 * c:2 * c + 2, :], z[:, 2 * c:2 * c + 2, :], xs, ALU.add).then_inc(s["g_xz"], 1)
                dve.wait_ge(s["g_xz"], c + 1)
                front_stats(F0 + fg + c, c)
                front_norm(F0 + fg + c, c)
                dve.wait_ge(s["xn"], F0 + fg + c + 1)
                dve.wait_ge(s["yTp"], AHEAD + fg + c)
                v.tensor_scalar(y, xn, 0.0, None, ALU.max).then_inc(s["y"], 1)
                for u in range(2):
                    dve.wait_ge(s["g_hs_mm"], 2 * c + u + 1)
                    v.tensor_scalar(hs[:, 2 * c + u, :], ps_q[0:T, u, :], dis[:, 2 * c + u:2 * c + u + 1], None,
                                    ALU.mult).then_inc(s["g_hs"], 1)
            dve.wait_ge(s["g_bc"], 1)
            v.tensor_copy(disb, psf[:, 0:N]).then_inc(s["g_disb"], 1)
            dve.wait_ge(s["g_disb"], 1)
            for j in range(KD):
                dve.wait_ge(s["g_ag"], j + 1)
                o = 1536 * (j % 2)
                v.tensor_tensor(aggT[:, j, :], psf[:, o:o + N], disb, ALU.mult).then_inc(s["g_agd"], 1)
            for t in range(NT):
                dve.wait_ge(s["g_hs_mm"], NT + t + 1)
                v.tensor_scalar(hs[:, t, :], ps_q[0:T, t % 2, :], dis[:, t:t + 1], None, ALU.mult).then_inc(s["g_hs"], 1)
            for t in range(NT):
                dve.wait_ge(s["g_ft"], t + 1)
                v.scalar_tensor_tensor(out=ztmp[:, t % 2, :], in0=ps[0:T, t % 2, :], scalar=dis[:, t:t + 1], in1=bvb[:, :],
                                       op0=ALU.mult, op1=ALU.add).then_inc(s["g_fin"], 1)
                dve.wait_ge(s["g_fin"], t + 1)
                v.tensor_tensor(z[:, t, :], z[:, t, :], ztmp[:, t % 2, :], ALU.add).then_inc(s["g_fz"], 1)

        @block.tensor
        def _(pe):
            mm = nc.tensor.matmul
            turn = nc.tensor.transpose
            pe.wait_ge(s["ident"], 2)
            pe.wait_ge(s["edge_f"], 1)
            off = 0
            for i, r in ((0, 128), (1, EC - 128), (2, 128), (3, EC - 128)):
                e = turn(ps[0:T, 7, off:off + r], edge_f[0:r, i, :], ident[0:r, 0:r])
                off += r
            e.then_inc(s["edge_t"], 1)
            pe.wait_ge(s["brow_ld"], 16 * 4)
            nb_ = 3 * L * KD + KD
            turn(ps[:, 6, 0:nb_], brow, ident[0:nb_, 0:nb_]).then_inc(s["brow_t"], 1)
            pe.wait_ge(s["cand"], 1)
            turn(ps[0:2 * NT, 5, 0:128], cand[:, 0, :], ident[:, :])
            turn(ps[0:2 * NT, 5, 128:EC], cand[0:EC - 128, 1, :], ident[0:EC - 128, 0:EC - 128]).then_inc(s["cand_t"], 1)
            pe.wait_ge(s["red"], 1)
            turn(ps[0:1, 5, 256:256 + 2 * NT], red[:, 0:1], ident[0:2 * NT, 0:2 * NT]).then_inc(s["red_t"], 1)
            pe.wait_ge(s["emb"], 1)
            pe.wait_ge(s["small_ld"], 16 * 5)
            for a, b in COLS:
                mm(psf[0:C, a:b], fw1[:, :], embT[:, a:b], start=True, stop=True).then_inc(s["emb_h"], 1)
            pe.wait_ge(s["h1"], 1)
            pe.wait_ge(s["cols"], 1)
            pe.wait_ge(s["tabi"], 1)
            pe.wait_ge(s["edgeT"], 1)
            for a, b in COLS:
                mm(psf[0:C, 2048 + a:2048 + b], fw2[:, :], h1T[:, a:b], start=True, stop=True).then_inc(s["cond_mm"], 1)
            pe.wait_ge(s["consts"], 12)
            pe.wait_ge(s["condT"], 3)
            mm(ps[0:T, 7, :], zeros16[:, 0:T], zeros16[:, :], start=True, stop=True).then_inc(s["oh_used"], 1)
            with pe.Fori(0, NT) as t:
                pairs = pe.value_load(tab[0:1, bass.ds(t + NT, 1)], min_val=1, max_val=EC // 2)
                before = pe.value_load(tab[0:1, bass.ds(t + 2 * NT, 1)], min_val=0, max_val=EC // 2 * NT)
                pe.wait_ge(s["ct"], AHEAD + t)
                for a, b in COLS:
                    mm(psf[0:T, a:b], zeros16[:, 0:T], zeros16[:, 0:b - a], start=True, stop=False, skip_group_check=True)
                with pe.Fori(0, pairs) as i:
                    for q in range(2):
                        pe.wait_ge(s["onehot"], (before + i) * 2 + q + 1)
                        for a, b in COLS:
                            e = mm(psf[0:T, a:b], oh_dst[:, q, 0:T], oh_src[:, q, a:b], start=False, stop=False,
                                   skip_group_check=True)
                        e.then_inc(s["oh_used"], 1)
                for a, b in COLS:
                    e = mm(psf[0:T, a:b], zeros16[:, 0:T], zeros16[:, 0:b - a], start=False, stop=True, skip_group_check=True)
                e.then_inc(s["ct_mm"], 1)
                pe.wait_ge(s["ct"], AHEAD + t + 1)
                pe.wait_ge(s["ct_e"], AHEAD + 3 * t)
                for p, (a, b) in enumerate(PIECES):
                    for m in range(a, b):
                        e = turn(ps_T[0:T, p, (m - a) * T:(m - a + 1) * T], ct[:, m * T:(m + 1) * T], ident[0:T, 0:T])
                    e.then_inc(s["ct_t"], 1)

            def scale_bias(f, ld):
                pe.wait_ge(s["condc"], f + 1)
                pe.wait_ge(s["ldLN"], ld)
                pe.wait_ge(s["y"], AHEAD + f)
                for u in range(2):
                    for a in range(2):
                        e = mm(ps_sb[:, u, a, :], condc[:, u * T:(u + 1) * T], lnw[:, a, :], start=True, stop=True)
                e.then_inc(s["sb"], 1)

            def turn_y(f, k_e=None):
                pe.wait_ge(s["y"], AHEAD + f + 1)
                pe.wait_ge(s["yT"], AHEAD + f)
                if k_e is not None:
                    pe.wait_ge(s["k_e"], AHEAD + k_e)
                for k in range(KD):
                    for u in range(2):
                        o = (k % 2) * W + u * T
                        e = turn(ps_yT[:, k // 2, o:o + T], y[:, u, k * 128:(k + 1) * 128], ident[0:T, 0:T])
                e.then_inc(s["yTp"], 1)

            def features(out_banks, w, rhs):
                for j in range(KD):
                    for k in range(KD):
                        e = mm(out_banks[:, j // 2, (j % 2) * W:(j % 2 + 1) * W], w[:, k, j * 128:(j + 1) * 128], rhs[:, k, :],
                               start=(k == 0), stop=(k == KD - 1))
                return e

            def nodes(u, lhs, w):
                for k in range(KD):
                    e = mm(ps_q[0:T, u, :], lhs[:, k, u * T:(u + 1) * T], w[:, k, :], start=(k == 0), stop=(k == KD - 1))
                return e

            def project(l, c, more):
                a, f = l * NC + c, 2 * NC * l + c
                pe.wait_ge(s["yT"], AHEAD + f + 1)
                pe.wait_ge(s["ldA"], 64 * (l + 1))
                pe.wait_ge(s["v_e"], AHEAD + 2 * a)
                features(ps_q, WQ, yTc).then_inc(s["q_mm"], 1)
                features(ps_yT, WK, yTc).then_inc(s["k_mm"], 1)
                if more:
                    scale_bias(f + 1, 64 * (2 * l + 1))
                pe.wait_ge(s["q_e"], KD * (a + 1))
                for u in range(2):
                    e = nodes(u, yTc, WV)
                e.then_inc(s["v_mm"], 1)
                if more:
                    turn_y(f + 1, KD * (a + 1))

            def mlp(l, c, more):
                a, f = l * NC + c, 2 * NC * l + NC + c
                pe.wait_ge(s["yT"], AHEAD + f + 1)
                pe.wait_ge(s["ldM"], 48 * (l + 1))
                pe.wait_ge(s["zC"], AHEAD + 2 * a)
                features(ps_q, M1, yTc).then_inc(s["h_mm"], 1)
                if more:
                    scale_bias(f + 1, 64 * (2 * l + 2))
                pe.wait_ge(s["h_e"], KD * (a + 1))
                for u in range(2):
                    nodes(u, hTc, M2).then_inc(s["o_mm"], 1)
                if more:
                    turn_y(f + 1)

            def scores(G, U, h, u):
                pe.wait_ge(s["qg"], H * G + h + 1)
                pe.wait_ge(s["ttr"], AHEAD + U)
                for a, b in COLS:
                    e = mm(psf[0:T, a:b], qg[:, h, u * T:(u + 1) * T], kT[:, h, a:b], start=True, stop=True)
                e.then_inc(s["S"], 1)

            def turn_probs(U, u):
                pe.wait_ge(s["P"], U + 1)
                pe.wait_ge(s["Te"], AHEAD + 3 * U)
                for p, (a, b) in enumerate(PIECES):
                    for m in range(a, b):
                        e = turn(ps_T[0:T, p, (m - a) * T:(m - a + 1) * T], P[:, u, m * T:(m + 1) * T], ident[0:T, 0:T])
                    e.then_inc(s["Tp"], 1)

            def attend(G, h, part):
                ms = (range(0, NT // 2), range(NT // 2, NT), range(NT))[part]
                if part != 1:
                    pe.wait_ge(s["Te"], AHEAD + 3 * UNITS * G + 3 * (2 * h + 2))
                    if h < 2:
                        pe.wait_ge(s["zB"], AHEAD + 2 * G)
                    else:
                        pe.wait_ge(s["oT"], H * G + h - 1)
                for m in ms:
                    e = mm(ps_q[:, h % 2, 0:W], V[:, m, h * DH:(h + 1) * DH], PT[:, h % 2, m, :],
                           start=(m == 0), stop=(m == NT - 1))
                if part != 0:
                    e.then_inc(s["PV"], 1)

            def attn_group(l, g_, last):
                G = l * NC + g_
                for k in range(UNITS):
                    n = k + 2
                    if n < UNITS or not last:
                        scores(G + n // UNITS, UNITS * G + n, n % UNITS // 2, n % 2)
                    turn_probs(UNITS * G + k, k % 2)
                    if k >= 2:
                        attend(G, k // 2 - 1, k % 2)
                attend(G, H - 1, 2)
                pe.wait_ge(s["oT"], H * (G + 1))
                pe.wait_ge(s["ldO"], 32 * (l + 1))
                for u in range(2):
                    nodes(u, outTg, WO).then_inc(s["wo_mm"], 1)

            pe.wait_ge(s["ct_e"], AHEAD + 3 * NT)
            with pe.Fori(0, L) as l:
                scale_bias(2 * NC * l, 64 * (2 * l + 1))
                pe.wait_ge(s["zC"], AHEAD + 2 * NC * l)
                settled(pe)
                turn_y(2 * NC * l)
                with pe.Fori(0, NC - 1) as c:
                    project(l, c, True)
                project(l, NC - 1, False)
                pe.wait_ge(s["k_e"], AHEAD + KD * NC * (l + 1))
                pe.wait_ge(s["v_e"], AHEAD + 2 * NC * (l + 1))
                for u in range(2):
                    scores(l * NC, UNITS * NC * l + u, 0, u)
                with pe.Fori(0, NC - 1) as g_:
                    attn_group(l, g_, False)
                attn_group(l, NC - 1, True)
                pe.wait_ge(s["ttr"], AHEAD + UNITS * NC * (l + 1))
                pe.wait_ge(s["Te"], AHEAD + 3 * UNITS * NC * (l + 1))
                scale_bias(2 * NC * l + NC, 64 * (2 * l + 2))
                turn_y(2 * NC * l + NC)
                pe.wait_ge(s["zB"], AHEAD + 2 * NC * (l + 1))
                settled(pe)
                with pe.Fori(0, NC - 1) as c:
                    mlp(l, c, True)
                mlp(l, NC - 1, False)

            fg = 2 * NC * L
            pe.wait_ge(s["ldA"], 64 * L + 48)
            pe.wait_ge(s["zC"], AHEAD + 2 * NC * L)
            for c in range(NC):
                turn_y(fg + c)
                pe.wait_ge(s["yT"], AHEAD + fg + c + 1)
                pe.wait_ge(s["g_hs"], 2 * c)
                for u in range(2):
                    nodes(u, yTc, WQ).then_inc(s["g_hs_mm"], 1)
            pe.wait_ge(s["g_diag"], 1)
            for a, b in COLS:
                e = mm(psf[:, a:b], ones[:, :], diags[:, a:b], start=True, stop=True)
            e.then_inc(s["g_bc"], 1)
            pe.wait_ge(s["g_disb"], 1)
            pe.wait_ge(s["g_A"], 1)
            pe.wait_ge(s["g_hs"], NT)
            for j in range(KD):
                if j >= 2:
                    pe.wait_ge(s["g_agd"], j - 1)
                o = 1536 * (j % 2)
                for a, b in COLS:
                    for m in range(NT):
                        e = mm(psf[:, o + a:o + b], hs[:, m, j * 128:(j + 1) * 128], counts[:, m, a:b],
                               start=(m == 0), stop=(m == NT - 1))
                e.then_inc(s["g_ag"], 1)
            pe.wait_ge(s["g_agT"], KD)
            for t in range(NT):
                if t >= 2:
                    pe.wait_ge(s["g_hs"], NT + t - 1)
                for k in range(KD):
                    e = mm(ps_q[0:T, t % 2, :], aggT[:, k, t * T:(t + 1) * T], WK[:, k, :], start=(k == 0), stop=(k == KD - 1))
                e.then_inc(s["g_hs_mm"], 1)
            pe.wait_ge(s["g_hs"], 2 * NT)
            for t in range(NT):
                if t >= 2:
                    pe.wait_ge(s["g_fin"], t - 1)
                for m in range(NT):
                    e = mm(ps[0:T, t % 2, :], counts[:, m, t * T:(t + 1) * T], hs[:, m, :], start=(m == 0), stop=(m == NT - 1))
                e.then_inc(s["g_ft"], 1)


_P = "L0_gnn_"
_INS = ["x", "src", "dst", "node_vec1"] + [_P + n for n in (
    "f_w1 f_b1 f_w2 f_b2 s1_w s1_b b1_w b1_b wq bq wk bk wv bv wo bo s2_w s2_b b2_w b2_b m_w1 m_b1 m_w2 m_b2").split()] + [
    "L1_gnn_W1", "L1_gnn_b1", "L1_gnn_W2", "L1_gnn_b2"]


def kernel(**inputs):
    import numpy as _np
    import concourse.bacc as _bacc
    from concourse import mybir as _mybir
    from concourse.bass_utils import run_bass_kernel_spmd as _run

    nc = _bacc.Bacc("TRN2", target_bir_lowering=False, num_devices=1)
    arrays, args = {}, []
    for name in _INS:
        a = _np.ascontiguousarray(inputs[name])
        arrays[f"in_{name}_dram"] = a
        args.append(nc.dram_tensor(f"in_{name}_dram", a.shape, _mybir.dt.from_np(a.dtype), kind="ExternalInput").ap())
    args.append(nc.dram_tensor("out_0_dram", (N, D), F32, kind="ExternalOutput").ap())
    build(nc, *args)
    r = _run(nc, [arrays], core_ids=[0])
    return r.results[0]["out_0_dram"]
```

```python
from contextlib import ExitStack

import concourse.bass as bass
from concourse import mybir

ALU = mybir.AluOpType
ACT = mybir.ActivationFunctionType
F32 = mybir.dt.float32
F32R = mybir.dt.float32r
F16 = mybir.dt.float16
BF16 = mybir.dt.bfloat16
I32 = mybir.dt.int32
AX_X = mybir.AxisListType.X

N = 1250
D = 512
E = 21250
L = 4
H = 4
DH = D // H
C = 16
NFREQ = 32
T = 125
NT = N // T
W = 2 * T
NC = NT // 2
KD = D // 128
EC = E // T
QUAD = 4
ECP = EC + QUAD
KC = 96
UNITS = 2 * H
EPS = 1e-5
SCALE = DH ** -0.5
BIG = 1e38
FLOOR = 1e30
MAGIC = 1.5 * 2.0 ** 23
COLS = [(0, 512), (512, 1024), (1024, N)]
PIECES = [(0, 4), (4, 8), (8, NT)]
AHEAD = 1
AHEAD_OF = "sb y yT yTp zC v_e ct ct_t ct_deg ct_e bst_out ttr Te zB k_e Tp cnt_out q_st qg wa vt".split()
LOW_ROWS = 112


def build(nc, x, src, dst, node_vec1, f_w1, f_b1, f_w2, f_b2, s1_w, s1_b, b1_w, b1_b, wq, bq, wk, bk, wv, bv,
          wo, bo, s2_w, s2_b, b2_w, b2_b, m_w1, m_b1, m_w2, m_b2, g_W1, g_b1, g_W2, g_b2, out):
    counts_dram = nc.dram_tensor("counts_scratch", [N, N], F32, kind="Internal").ap()
    q_dram = nc.dram_tensor("q_scratch", [NC, 128, KD * W], F32, kind="Internal").ap()
    bias_dram = nc.dram_tensor("edge_bias_scratch", [N, N], F32, kind="Internal").ap()

    with ExitStack() as ctx:
        at = [(nc.sbuf_base + 31) // 32 * 32]

        def place(name, shape, dt, where):
            return nc.alloc_sbuf_tensor_at(name, shape, dt, offset=where)

        def region(nbytes):
            start = at[0]
            at[0] += (nbytes + 31) // 32 * 32
            assert at[0] <= nc.sbuf_usable_end, at[0]
            return start

        def sb(name, shape, dt=F32):
            n = 1
            for k in shape[1:]:
                n *= k
            return place(name, shape, dt, region(n * (2 if dt in (F16, BF16) else 4)))

        def sem(name):
            return ctx.enter_context(nc.semaphore(name))

        z = sb("z", [T, NT, D])
        r_kv = region(2 * 4 * KD * N + 2 * 4 * NT * D)
        kT = place("kT", [128, 2, KD, N], F32R, r_kv)
        V = place("V", [T, 2, NT, D], F32R, r_kv + 2 * 4 * KD * N)
        pbuf = sb("pbuf", [T, 2 * N])
        P = pbuf[:, :].rearrange("p (b n) -> p b n", b=2)
        xn = pbuf[:, 0:2 * D].rearrange("p (u d) -> p u d", u=2)
        y = pbuf[:, 2 * D:4 * D].rearrange("p (u d) -> p u d", u=2)
        r_pt = region(2 * 2 * 4 * NT * W + 2 * 4 * N)
        PT = place("PT", [T, 2, 2, NT, W], F32R, r_pt)
        wa = place("wa", [128, 3, 2, KD, D], F32R, r_pt)
        WV, WK, WQ = (wa[:, i] for i in range(3))
        r_bt = r_pt + 2 * 2 * 4 * NT * W
        bt = place("bt", [T, 2, N], F32, r_bt)
        r_wm = region(4 * 3 * KD * D)
        wm = place("wm", [128, 3, KD, D], F32, r_wm)
        WO = wm[:, 0]
        wa_raw = place("wa_raw", [128, 3, KD, D], F32, r_kv)
        wmS = place("wmS", [128, 2, 2, KD, D], F32R, r_kv + 4 * 3 * KD * D)
        hT = place("hT", [128, 2, KD, W], F32R, r_kv + 4 * 7 * KD * D)
        lnw = sb("lnw", [KC, 2, D])
        lnS = sb("lnS", [KC, 2, D], F32R)
        bvb = sb("bvb", [T, D])
        bob = sb("bob", [T, D])
        b2b = sb("b2b", [T, D])
        outTg = sb("outTg", [128, KD, W])
        r_qg = region(2 * 4 * KD * W)
        qg = place("qg", [128, 2, KD, W], F32R, r_qg)
        yT = place("yT", [128, 2, KD, W], F32R, r_qg)
        qc = sb("qc", [128, KD, W])
        condS = sb("condS", [KC, N], F32R)
        condc = sb("condc", [KC, W], F32R)
        ident = sb("ident", [128, 128])
        cols = sb("cols", [128, 3 * L * KD + KD])
        eps = sb("eps", [T, 1])
        stats = sb("stats", [T, 2, 6])
        mv = sb("mv", [T, 2, 2])
        lnv = sb("lnv", [T, 2])
        r0 = sb("r0", [T, 2])
        nt_a = sb("nt_a", [T, 2])
        nt_b = sb("nt_b", [T, 2])
        nt_c = sb("nt_c", [T, 2])
        rstd = sb("rstd", [T, 2])
        ztmp = sb("ztmp", [T, 2, D])
        nmx = sb("nmx", [T, 2])
        den = sb("den", [T, 2])
        dmx = sb("dmx", [T, 2])
        rden = sb("rden", [T, 2])
        deg = sb("deg", [T, NT])
        dis = sb("dis", [T, NT])
        dis0 = sb("dis0", [T, NT])
        dis_a = sb("dis_a", [T, NT])
        dis_b = sb("dis_b", [T, NT])
        def packer(start, end):
            cur = [start]

            def pack(name, shape, dt=F32):
                here = cur[0]
                n = 1
                for k in shape[1:]:
                    n *= k
                cur[0] += (n * (2 if dt in (F16, BF16) else 4) + 31) // 32 * 32
                assert cur[0] <= end + 31, (name, cur[0] - start)
                return place(name, shape, dt, here)

            return pack

        kv_end = r_kv + 2 * 4 * (KD * N + NT * D)
        late = packer(r_kv, kv_end)
        counts = late("counts", [T, NT, N])
        disb = late("disb", [128, N])
        aggT = late("aggT", [128, KD, N])
        ones = late("ones", [T, 128])
        hs = place("hs", [T, NT, D], F32, r_wm)
        W2 = place("W2", [128, KD, D], F32, r_pt + 2 * 4 * KD * D)
        late2 = packer(r_bt, r_bt + 2 * 4 * N)
        diags = late2("diags", [T, N])
        xs = late2("xs", [T, 2, D])
        early = packer(r_kv, kv_end)
        early2 = packer(r_bt, r_bt + 2 * 4 * N)
        embT = early2("embT", [2 * NFREQ, N])
        h1T = early("h1T", [C, N])
        oh_src = early("oh_src", [T, QUAD, N], BF16)
        oh_dst = early("oh_dst", [T, QUAD, T + 1], BF16)
        iota16 = early("iota16", [T, N], F16)
        iota_i = early("iota_i", [T, N], I32)
        zeros16 = early("zeros16", [T, D], BF16)
        edge_i = early("edge_i", [128, 4, T], I32)
        edge_f = early("edge_f", [128, 4, T])
        edgeT = early("edgeT", [T, 2, ECP])
        nb = early("nb", [2 * NFREQ, N])
        ph = early("ph", [2 * NFREQ, N])
        phr = early("phr", [2 * NFREQ, N])
        condT = early("condT", [C + 1, N])
        cblk = early("cblk", [T, NT, T])
        blk_max = early("blk_max", [T, NT, T])
        blk_ln = early("blk_ln", [T, NT, T])
        blk_bias = early("blk_bias", [T, NT, T])
        ct = pbuf[:, 0:N]
        fw1 = early("fw1", [2 * NFREQ, C])
        fw2 = early("fw2", [C, C])
        fb = early("fb", [C, 2])
        freq_i = early("freq_i", [2 * NFREQ, 1], I32)
        freq = early("freq", [2 * NFREQ, 1])
        offs = early("offs", [2 * NFREQ, 1])
        brow = early("brow", [3 * L * KD + KD, 128])
        low_i = early("low_i", [128, NT + 1], I32)
        low = early("low", [128, NT + 1])
        mm_ = early("mm_", [128, 2, 6])
        cand = early("cand", [128, 2, 2 * NT])
        rel = early("rel", [128, 2, 2 * NT])
        red = early("red", [2 * NT, 1])
        rtab = early("rtab", [1, 6 * NT])
        tab = early("tab", [1, 3 * NT], I32)
        tab0 = early("tab0", [1, NT], I32)

        ps = ctx.enter_context(nc.psum_tensor("ps", [128, 8, 512], F32))
        psf = ps[:, :, :].rearrange("p b n -> p (b n)")
        ps_S = psf[0:T, 0:N]
        ps_sb = ps[0:T, 0:4, :].rearrange("p (u a) n -> p u a n", u=2)
        ps_T = ps[:, 3:6, :]
        ps_yT = ps[:, 4:6, :]
        ps_q = ps[:, 6:8, :]

        s = {}
        for name in ("x_ld edge_ld small_ld brow_ld ident consts edge_f edge_t edgeT brow_t cols emb_u emb_r emb_f emb emb_h "
                     "h1 cond_mm condT rm rel cand cand_t red red_t tab prefix tabi onehot oh_used ct_mm ct ct_deg ct_t ct_e "
                     "bmax bln bmask bdone bst_out cnt_out condS0 condS lnhi lnS onesr "
                     "bn stats lnv r0 nw xn sb ysc y yTp yT condc condc_used "
                     "ldA ldLN ldO ldM q_mm q_e k_mm k_e v_mm v_e "
                     "S ttr exp dmx rden P Tp Te PV oT wo_mm zt zB st0 st1 qg qgh q_st q_ld khi vt vhi Thi wa_hi wa wm_hi wmS yThi hhi hraw ldG "
                     "h_mm h_e o_mm zct zC "
                     "g_cnt g_x g_xz g_A g_dg g_diag g_bc g_disb g_hs_mm g_hs g_ag g_agd g_agT g_ft g_fin g_fz g_out z0 settled").split():
            s[name] = sem(name)
        block = ctx.enter_context(nc.Block())

        def rows(ap2):
            return ((0, LOW_ROWS), (LOW_ROWS, T))

        def settled(eng):
            eng.sem_inc(s["settled"], 1)

        @block.sync
        def _(sp):
            sp.dma_start(edge_i[0:128, 0, :], src[0:128 * T].rearrange("(j p) -> j p", p=T)).then_inc(s["edge_ld"], 16)
            sp.dma_start(edge_i[0:EC - 128, 1, :], src[128 * T:E].rearrange("(j p) -> j p", p=T)).then_inc(s["edge_ld"], 16)
            sp.dma_start(edge_i[0:128, 2, :], dst[0:128 * T].rearrange("(j p) -> j p", p=T)).then_inc(s["edge_ld"], 16)
            sp.dma_start(edge_i[0:EC - 128, 3, :], dst[128 * T:E].rearrange("(j p) -> j p", p=T)).then_inc(s["edge_ld"], 16)
            sp.dma_start(nb[:, :], node_vec1.rearrange("n a -> a n").to_broadcast([2 * NFREQ, N])).then_inc(s["small_ld"], 16)
            sp.dma_start(fw1[:, :], f_w1).then_inc(s["small_ld"], 16)
            sp.dma_start(fw2[:, :], f_w2).then_inc(s["small_ld"], 16)
            sp.dma_start(fb[:, 0:1], f_b1.rearrange("(c a) -> c a", a=1)).then_inc(s["small_ld"], 16)
            sp.dma_start(fb[:, 1:2], f_b2.rearrange("(c a) -> c a", a=1)).then_inc(s["small_ld"], 16)
            for i, b in enumerate((bq, bk, m_b1)):
                sp.dma_start(brow[i * L * KD:(i + 1) * L * KD, :], b.rearrange("l (k p) -> (l k) p", p=128)).then_inc(s["brow_ld"], 16)
            sp.dma_start(brow[3 * L * KD:3 * L * KD + KD, :], g_b1.rearrange("(k p) -> k p", p=128)).then_inc(s["brow_ld"], 16)
            for t in range(NT):
                sp.dma_start(z[:, t, :], x[t * T:(t + 1) * T, :]).then_inc(s["x_ld"], 16)

            def load_w(slot, w, name):
                sp.dma_start(slot, w.rearrange("(k p) n -> p k n", p=128)).then_inc(s[name], 16)

            def lay(w, l):
                return w[bass.ds(l, 1)].rearrange("a k n -> (a k) n") if not isinstance(l, int) else w[l]

            def row(b, l):
                return b[bass.ds(l, 1), :] if not isinstance(l, int) else b[l:l + 1, :]

            def load_attn(l, to):
                load_w(to[:, 0], lay(wv, l), "ldA")
                load_w(to[:, 1], lay(wk, l), "ldA")
                load_w(to[:, 2], lay(wq, l), "ldA")
                sp.dma_start(bvb[:, :], row(bv, l).to_broadcast([T, D])).then_inc(s["ldA"], 16)

            def load_ln(l, sw, sbias, bw, bbias):
                for q in (0, 32, 64):
                    sp.dma_start(lnw[q:q + C, 0, :], lay(sw, l)).then_inc(s["ldLN"], 16)
                    sp.dma_start(lnw[q + C:q + C + 1, 0, :], row(sbias, l)).then_inc(s["ldLN"], 16)
                    sp.dma_start(lnw[q:q + C, 1, :], lay(bw, l)).then_inc(s["ldLN"], 16)
                    sp.dma_start(lnw[q + C:q + C + 1, 1, :], row(bbias, l)).then_inc(s["ldLN"], 16)

            def load_o(l):
                load_w(WO, lay(wo, l), "ldO")
                sp.dma_start(bob[:, :], row(bo, l).to_broadcast([T, D])).then_inc(s["ldO"], 16)

            def load_m(l):
                load_w(wm[:, 1], lay(m_w1, l), "ldM")
                load_w(wm[:, 2], lay(m_w2, l), "ldM")
                sp.dma_start(b2b[:, :], row(m_b2, l).to_broadcast([T, D])).then_inc(s["ldM"], 16)

            def load_bias(g, u):
                for a, b in ((0, LOW_ROWS), (LOW_ROWS, T)):
                    start = g * W + u * T + a
                    view = bias_dram[bass.ds(start, b - a), :] if not isinstance(g, int) else bias_dram[start:start + b - a, :]
                    sp.dma_start(bt[a:b, u, :], view).then_inc(s[f"st{u}"], 16)

            def q_view(c):
                return q_dram[c] if isinstance(c, int) else q_dram[bass.ds(c, 1)].rearrange("a p n -> (a p) n")

            qc_flat = qc[:, :, :].rearrange("p k n -> p (k n)")

            load_attn(0, wm)
            sp.wait_ge(s["consts"], 14)
            load_ln(0, s1_w, s1_b, b1_w, b1_b)
            sp.wait_ge(s["wa"], AHEAD + 3)
            load_o(0)
            load_m(0)
            by_tile = [d.rearrange("(a p) m -> p a m", p=T) for d in (counts_dram, bias_dram)]
            with sp.Fori(0, NT) as t:
                sp.wait_ge(s["bdone"], t + 1)
                for d, blk, name in zip(by_tile, (cblk, blk_bias), ("cnt_out", "bst_out")):
                    sp.dma_start(d[:, :, bass.ds(t * T, T)], blk[:, :, :]).then_inc(s[name], 16)
            sp.wait_ge(s["bst_out"], AHEAD + 16 * NT)
            def layer(l, last):
                with sp.Fori(0, NC) as c:
                    sp.wait_ge(s["q_e"], KD * (l * NC + c + 1))
                    sp.dma_start(q_view(c), qc_flat).then_inc(s["q_st"], 16)
                sp.wait_ge(s["q_mm"], KD * NC * (l + 1))
                settled(sp)
                for u in range(2):
                    load_bias(0, u)
                sp.wait_ge(s["q_st"], AHEAD + 16 * NC * (l + 1))
                settled(sp)
                sp.dma_start(qc_flat, q_view(0)).then_inc(s["q_ld"], 16)
                sp.wait_ge(s["lnS"], 2 * l + 1)
                settled(sp)
                load_ln(l, s2_w, s2_b, b2_w, b2_b)
                with sp.Fori(0, NC - 1) as g:
                    G = l * NC + g
                    sp.wait_ge(s["qg"], AHEAD + H * (G + 1))
                    sp.dma_start(qc_flat, q_view(g + 1)).then_inc(s["q_ld"], 16)
                    for u in range(2):
                        sp.wait_ge(s["ttr"], AHEAD + (UNITS * G + UNITS - 1 + u))
                        load_bias(g + 1, u)
                sp.wait_ge(s["lnS"], 2 * l + 2)
                settled(sp)
                if not last:
                    load_ln(l + 1, s1_w, s1_b, b1_w, b1_b)
                sp.wait_ge(s["PV"], H * NC * (l + 1))
                settled(sp)
                if not last:
                    load_attn(l + 1, wa_raw)
                else:
                    for i in range(3):
                        load_w(wa_raw[:, i], g_W1, "ldA")
                    sp.dma_start(bvb[:, :], g_b2.rearrange("(a n) -> a n", a=1).to_broadcast([T, D])).then_inc(s["ldA"], 16)
                sp.wait_ge(s["zB"], AHEAD + (2 * NC * (l + 1)))
                settled(sp)
                if not last:
                    load_o(l + 1)
                sp.wait_ge(s["zC"], AHEAD + (2 * NC * (l + 1)))
                if not last:
                    load_m(l + 1)
                else:
                    sp.wait_ge(s["wa"], AHEAD + 3 * (L + 1))
                    load_w(W2[:, :, :], g_W2, "ldG")
                    sp.wait_ge(s["cnt_out"], AHEAD + 16 * NT)
                    for t in range(NT):
                        sp.dma_start(counts[:, t, :], counts_dram[t * T:(t + 1) * T, :]).then_inc(s["g_cnt"], 16)

            with sp.Fori(0, L - 1) as l:
                layer(l, False)
            layer(L - 1, True)
            for c in range(NC):
                if c:
                    sp.wait_ge(s["g_xz"], c)
                for u in range(2):
                    sp.dma_start(xs[:, u, :], x[(2 * c + u) * T:(2 * c + u + 1) * T, :]).then_inc(s["g_x"], 16)
            for t in range(NT):
                sp.wait_ge(s["g_fz"], t + 1)
                sp.dma_start(out[t * T:(t + 1) * T, :], z[:, t, :]).then_inc(s["g_out"], 16)
            sp.wait_ge(s["g_out"], 16 * NT)

        @block.gpsimd
        def _(pool):
            g = nc.gpsimd
            for name in AHEAD_OF:
                pool.sem_inc(s[name], AHEAD)
            g.memset(ident[:, :], 0.0).then_inc(s["ident"], 1)
            pool.wait_ge(s["ident"], 1)
            g.affine_select(out=ident[:, :], in_=ident[:, :], compare_op=ALU.not_equal, fill=1.0, base=0,
                            pattern=[[-1, 128]], channel_multiplier=1).then_inc(s["ident"], 1)
            g.iota(iota_i[:, :], pattern=[[1, N]], base=0, channel_multiplier=0).then_inc(s["consts"], 1)
            pool.wait_ge(s["consts"], 1)
            g.iota(low_i[:, 0:NT], pattern=[[T, NT]], base=0, channel_multiplier=0).then_inc(s["consts"], 1)
            pool.wait_ge(s["consts"], 2)
            g.iota(low_i[:, NT:NT + 1], pattern=[[0, 1]], base=0, channel_multiplier=1).then_inc(s["consts"], 1)
            pool.wait_ge(s["consts"], 3)
            g.iota(freq_i[0:NFREQ, :], pattern=[[0, 1]], base=1, channel_multiplier=1).then_inc(s["consts"], 1)
            pool.wait_ge(s["consts"], 4)
            g.iota(freq_i[NFREQ:2 * NFREQ, :], pattern=[[0, 1]], base=1, channel_multiplier=1).then_inc(s["consts"], 1)
            pool.wait_ge(s["consts"], 5)
            g.memset(offs[0:NFREQ, :], 0.0).then_inc(s["consts"], 1)
            pool.wait_ge(s["consts"], 6)
            g.memset(offs[NFREQ:2 * NFREQ, :], 0.25).then_inc(s["consts"], 1)
            pool.wait_ge(s["consts"], 7)
            g.memset(zeros16[:, :], 0.0).then_inc(s["consts"], 1)
            pool.wait_ge(s["consts"], 8)
            g.memset(eps[:, :], EPS).then_inc(s["consts"], 1)
            pool.wait_ge(s["consts"], 9)
            g.memset(condT[:, :], 1.0).then_inc(s["consts"], 1)
            pool.wait_ge(s["consts"], 10)
            g.memset(edgeT[:, :, EC:ECP], -1.0).then_inc(s["consts"], 1)
            pool.wait_ge(s["consts"], 11)
            g.memset(lnw[:, :, :], 0.0).then_inc(s["consts"], 1)
            pool.wait_ge(s["consts"], 12)
            g.memset(condS[:, :].bitcast(F32), 0.0).then_inc(s["consts"], 1)
            pool.wait_ge(s["consts"], 13)
            g.memset(lnS[:, :, :].bitcast(F32), 0.0).then_inc(s["consts"], 1)
            pool.wait_ge(s["consts"], 14)

            def split_wa(raw, l, i):
                n = 3 * l + i
                pool.wait_ge(s["ldA"], 64 * (l + 1))
                settled(pool)
                g.tensor_copy(wa[:, i, 0], raw[:, i]).then_inc(s["wa_hi"], 1)
                pool.wait_ge(s["wa_hi"], n + 1)
                settled(pool)
                g.tensor_tensor(wa[:, i, 1], raw[:, i], wa[:, i, 0].bitcast(F32), ALU.subtract).then_inc(s["wa"], 1)

            pool.wait_ge(s["emb_h"], len(COLS))
            settled(pool)
            for i in range(3):
                split_wa(wm, 0, i)

            with pool.Fori(0, NT) as t:
                pool.wait_ge(s["ct_e"], AHEAD + 3 * (t + 1))
                settled(pool)
                g.tensor_scalar(blk_max[:, :, :], cblk[:, :, :], 1.0, None, ALU.max).then_inc(s["bmax"], 1)
                pool.wait_ge(s["bst_out"], AHEAD + t * 16)
                settled(pool)
                g.tensor_scalar(blk_bias[:, :, :], cblk[:, :, :], 0.0, -BIG, ALU.is_equal, ALU.mult).then_inc(s["bmask"], 1)
                pool.wait_ge(s["bmask"], t + 1)
                pool.wait_ge(s["bln"], t + 1)
                g.tensor_tensor(blk_bias[:, :, :], blk_bias[:, :, :], blk_ln[:, :, :], ALU.add).then_inc(s["bdone"], 1)

            def split_ln(i):
                pool.wait_ge(s["ldLN"], 192 * (i + 1))
                pool.wait_ge(s["sb"], AHEAD + NC * i)
                settled(pool)
                g.tensor_copy(lnS[:, :, :], lnw[:, :, :]).then_inc(s["lnhi"], 1)
                pool.wait_ge(s["lnhi"], i + 1)
                settled(pool)
                q = slice(32, 32 + C + 1)
                g.tensor_tensor(lnS[q, :, :], lnw[q, :, :], lnS[q, :, :].bitcast(F32), ALU.subtract).then_inc(s["lnS"], 1)
                pool.wait_ge(s["lnS"], i + 1)
                settled(pool)

            def cond_chunk(f, c):
                pool.wait_ge(s["sb"], AHEAD + f)
                settled(pool)
                g.tensor_copy(condc[:, :], condS[:, bass.ds(c * W, W)].bitcast(F32)).then_inc(s["condc"], 1)

            def q_head(G, h):
                pool.wait_ge(s["q_ld"], 16 * (G + 1))
                settled(pool)
                g.tensor_copy(qg[:, 0, h, :], qc[:, h, :]).then_inc(s["qgh"], 1)
                pool.wait_ge(s["qgh"], H * G + h + 1)
                settled(pool)
                g.tensor_tensor(qg[:, 1, h, :], qc[:, h, :], qg[:, 0, h, :].bitcast(F32), ALU.subtract).then_inc(s["qg"], 1)

            def v_split(l, c):
                for u in range(2):
                    i = 2 * (l * NC + c) + u
                    pool.wait_ge(s["vt"], AHEAD + i + 1)
                    settled(pool)
                    vh = V[:, 0, bass.ds(2 * c + u, 1), :].rearrange("p a d -> p (a d)")
                    vl = V[:, 1, bass.ds(2 * c + u, 1), :].rearrange("p a d -> p (a d)")
                    g.tensor_copy(vh, ztmp[:, u, :]).then_inc(s["vhi"], 1)
                    pool.wait_ge(s["vhi"], i + 1)
                    g.tensor_tensor(vl, ztmp[:, u, :], vh.bitcast(F32), ALU.subtract).then_inc(s["v_e"], 1)

            pool.wait_ge(s["condS"], 1)
            with pool.Fori(0, L) as l:
                split_ln(2 * l)
                cond_chunk(2 * NC * l, 0)
                with pool.Fori(0, NC - 1) as c:
                    cond_chunk(2 * NC * l + c + 1, c + 1)
                    v_split(l, c)
                v_split(l, NC - 1)
                pool.wait_ge(s["v_mm"], NC * (l + 1))
                settled(pool)
                for h in range(H):
                    q_head(l * NC, h)
                with pool.Fori(0, NC - 1) as g_:
                    G = l * NC + g_
                    for h in range(H):
                        pool.wait_ge(s["S"], UNITS * G + 2 * h + 2)
                        q_head(G + 1, h)
                split_ln(2 * l + 1)
                for c in range(NC):
                    cond_chunk(2 * NC * l + NC + c, c)
                    if c >= 2:
                        split_wa(wa_raw, l + 1, c - 2)
            pool.wait_ge(s["zC"], AHEAD + 2 * NC * L)
            g.memset(ones[:, :], 1.0).then_inc(s["onesr"], 1)

        @block.scalar
        def _(act):
            sc = nc.scalar
            act.wait_ge(s["consts"], 14)
            act.wait_ge(s["emb_f"], 1)
            sc.activation(embT[:, :], phr[:, :], ACT.Sin, scale=6.2831850).then_inc(s["emb"], 1)
            act.wait_ge(s["emb_h"], 3)
            act.wait_ge(s["small_ld"], 16 * 5)
            sc.activation(h1T[:, :], psf[0:C, 0:N], ACT.Silu, bias=fb[:, 0:1]).then_inc(s["h1"], 1)
            sc.preload_act_table_set("natural_log_exp_and_others")
            for i, (a, b) in enumerate(COLS):
                act.wait_ge(s["cond_mm"], 3)
                sc.activation(condT[0:C, a:b], psf[0:C, 2048 + a:2048 + b], ACT.Identity, bias=fb[:, 1:2]).then_inc(s["condT"], 1)
            with act.Fori(0, NT) as t:
                act.wait_ge(s["ct_mm"], t + 1)
                act.wait_ge(s["ct_t"], AHEAD + 3 * t)
                act.wait_ge(s["ct_deg"], AHEAD + t)
                sc.activation(ct, ps_S, ACT.Copy).then_inc(s["ct"], 1)
                act.wait_ge(s["cnt_out"], AHEAD + 16 * t)
                for p, (a, b) in enumerate(PIECES):
                    act.wait_ge(s["ct_t"], AHEAD + (t * 3 + p + 1))
                    sc.activation(cblk[:, a:b, :], ps_T[0:T, p, 0:(b - a) * T].rearrange("p (t n) -> p t n", n=T),
                                  ACT.Copy).then_inc(s["ct_e"], 1)
                act.wait_ge(s["bmax"], t + 1)
                sc.activation(blk_ln[:, :, :], blk_max[:, :, :], ACT.Ln).then_inc(s["bln"], 1)

            def rsqrt0(f):
                act.wait_ge(s["stats"], f + 1)
                sc.activation(lnv[:, :], mv[:, :, 1], ACT.Ln, bias=eps[:, :]).then_inc(s["lnv"], 1)
                act.wait_ge(s["lnv"], f + 1)
                sc.activation(r0[:, :], lnv[:, :], ACT.Exp, scale=-0.5).then_inc(s["r0"], 1)

            def yT_out(f):
                act.wait_ge(s["yTp"], AHEAD + f + 1)
                sc.activation(yT[:, 0].rearrange("p (a k) n -> p a (k n)", a=2), ps_yT[:, :, 0:2 * W], ACT.Copy).then_inc(s["yThi"], 1)

            def q_out(l, c):
                act.wait_ge(s["q_st"], AHEAD + 16 * (l * NC + c))
                act.wait_ge(s["qg"], AHEAD + H * NC * l)
                for j in range(KD):
                    act.wait_ge(s["q_mm"], KD * (l * NC + c) + (j | 1) + 1)
                    sc.activation(qc[:, j, :], ps_q[:, j // 2, (j % 2) * W:(j % 2 + 1) * W], ACT.Identity,
                                  bias=cols[:, bass.ds(l * KD + j, 1)], scale=SCALE).then_inc(s["q_e"], 1)

            def k_out(l, c):
                for j in range(KD):
                    act.wait_ge(s["k_mm"], KD * (l * NC + c) + (j | 1) + 1)
                    sc.activation(kT[:, 0, j, bass.ds(c * W, W)], ps_yT[:, j // 2, (j % 2) * W:(j % 2 + 1) * W], ACT.Identity,
                                  bias=cols[:, bass.ds(l * KD + (L * KD + j), 1)]).then_inc(s["khi"], 1)

            def h_out(l, c):
                for j in range(KD):
                    act.wait_ge(s["h_mm"], KD * (l * NC + c) + (j | 1) + 1)
                    for o, name in ((hT[:, 0, j, :], "hhi"), (qc[:, j, :], "hraw")):
                        sc.activation(o, ps_q[:, j // 2, (j % 2) * W:(j % 2 + 1) * W], ACT.Relu,
                                      bias=cols[:, bass.ds(2 * L * KD + l * KD + j, 1)]).then_inc(s[name], 1)

            def split_m(l):
                act.wait_ge(s["ldM"], 48 * (l + 1))
                act.wait_ge(s["PV"], H * NC * (l + 1))
                for i in range(2):
                    sc.activation(wmS[:, i, 0], wm[:, 1 + i], ACT.Copy).then_inc(s["wm_hi"], 1)

            def exp_unit(U, u):
                act.wait_ge(s["ttr"], AHEAD + U + 1)
                if u is not None:
                    sc.activation(P[:, u, :], P[:, u, :], ACT.Exp, bias=nmx[:, u:u + 1], scale=-1.0,
                                  accum_out=den[:, u:u + 1]).then_inc(s["exp"], 1)

            def turn_out(U, h, u):
                for i, (a, b) in enumerate(PIECES):
                    act.wait_ge(s["Tp"], AHEAD + 3 * U + i + 1)
                    sc.activation(PT[:, h % 2, 0, a:b, u * T:(u + 1) * T],
                                  ps_T[0:T, i, 0:(b - a) * T].rearrange("p (t n) -> p t n", n=T), ACT.Copy).then_inc(s["Thi"], 1)

            def attn_out(G, h):
                act.wait_ge(s["PV"], H * G + h + 1)
                sc.activation(outTg[:, h, :], ps_q[:, h % 2, 0:W], ACT.Copy).then_inc(s["oT"], 1)

            def attn_group(G, last):
                for k in range(UNITS):
                    h, u = k // 2, k % 2
                    turn_out(UNITS * G + k, h, u)
                    if k + 2 < UNITS or not last:
                        exp_unit(UNITS * G + k + 2, u)
                    if u == 1 and h >= 1:
                        attn_out(G, h - 1)
                attn_out(G, H - 1)

            for c in range(NC):
                rsqrt0(c)

            F0 = NC
            with act.Fori(0, L) as l:
                f = 2 * NC * l
                rsqrt0(F0 + f)
                with act.Fori(0, NC - 1) as c:
                    yT_out(f + c)
                    rsqrt0(F0 + f + c + 1)
                    q_out(l, c)
                    k_out(l, c)
                yT_out(f + NC - 1)
                q_out(l, NC - 1)
                k_out(l, NC - 1)
                exp_unit(UNITS * NC * l, 0)
                exp_unit(UNITS * NC * l + 1, 1)
                with act.Fori(0, NC - 1) as g_:
                    attn_group(l * NC + g_, False)
                attn_group(l * NC + NC - 1, True)
                f2 = 2 * NC * l + NC
                rsqrt0(F0 + f2)
                split_m(l)
                with act.Fori(0, NC - 1) as c:
                    yT_out(f2 + c)
                    rsqrt0(F0 + f2 + c + 1)
                    h_out(l, c)
                yT_out(f2 + NC - 1)
                h_out(l, NC - 1)
            fg = 2 * NC * L
            act.wait_ge(s["g_dg"], 1)
            sc.activation(dis_a[:, :], dis_b[:, :], ACT.Ln).then_inc(s["g_dg"], 1)
            act.wait_ge(s["g_dg"], 2)
            sc.activation(dis0[:, :], dis_a[:, :], ACT.Exp, scale=-0.5).then_inc(s["g_dg"], 1)
            for c in range(NC):
                rsqrt0(F0 + fg + c)
                yT_out(fg + c)
            for j in range(KD):
                act.wait_ge(s["g_agd"], j + 1)
                sc.activation(aggT[:, j, :], aggT[:, j, :], ACT.Relu,
                              bias=cols[:, 3 * L * KD + j:3 * L * KD + j + 1]).then_inc(s["g_agT"], 1)

        @block.vector
        def _(dve):
            v = nc.vector
            dve.wait_ge(s["edge_ld"], 16 * 4)
            for i, r in ((0, 128), (1, EC - 128), (2, 128), (3, EC - 128)):
                e = v.tensor_copy(edge_f[0:r, i, :], edge_i[0:r, i, :])
            e.then_inc(s["edge_f"], 1)
            dve.wait_ge(s["consts"], 14)
            v.tensor_copy(low[:, :], low_i[:, :]).then_inc(s["prefix"], 1)
            v.tensor_copy(iota16[:, :], iota_i[:, :])
            v.tensor_scalar(freq[:, :], freq_i[:, :], 1.0 / 16, None, ALU.mult).then_inc(s["prefix"], 1)
            dve.wait_ge(s["prefix"], 2)
            dve.wait_ge(s["small_ld"], 16 * 5)
            v.tensor_scalar(ph[:, :], nb[:, :], freq[:, 0:1], offs[:, 0:1], ALU.mult, ALU.add).then_inc(s["emb_u"], 1)
            dve.wait_ge(s["emb_u"], 1)
            v.tensor_scalar(phr[:, :], ph[:, :], MAGIC, -MAGIC, ALU.add, ALU.add).then_inc(s["emb_r"], 1)
            dve.wait_ge(s["emb_r"], 1)
            v.tensor_tensor(phr[:, :], ph[:, :], phr[:, :], ALU.subtract).then_inc(s["emb_f"], 1)
            dve.wait_ge(s["edge_f"], 1)
            for hf, r in ((0, 128), (1, EC - 128)):
                v.tensor_reduce(mm_[0:r, hf, 0:1], edge_f[0:r, 2 + hf, :], AX_X, ALU.max)
                v.tensor_reduce(mm_[0:r, hf, 1:2], edge_f[0:r, 2 + hf, :], AX_X, ALU.min)
                v.tensor_scalar(mm_[0:r, hf, 4:5], low[0:r, NT:NT + 1], -1.0, float(ECP - 128 * hf), ALU.mult, ALU.add)
                e = v.tensor_scalar(mm_[0:r, hf, 5:6], low[0:r, NT:NT + 1], float(1 + 128 * hf), None, ALU.add)
            e.then_inc(s["rm"], 1)
            dve.wait_ge(s["rm"], 1)
            for hf, r in ((0, 128), (1, EC - 128)):
                v.tensor_scalar(mm_[0:r, hf, 2:3], mm_[0:r, hf, 1:2], float(-T), None, ALU.add)
                e = v.tensor_scalar(rel[0:r, hf, NT:2 * NT], low[0:r, 0:NT], mm_[0:r, hf, 0:1], None, ALU.is_le)
            e.then_inc(s["rel"], 1)
            dve.wait_ge(s["rel"], 1)
            for hf, r in ((0, 128), (1, EC - 128)):
                e = v.scalar_tensor_tensor(out=rel[0:r, hf, 0:NT], in0=low[0:r, 0:NT], scalar=mm_[0:r, hf, 2:3],
                                           in1=rel[0:r, hf, NT:2 * NT], op0=ALU.is_gt, op1=ALU.mult)
            e.then_inc(s["rel"], 1)
            dve.wait_ge(s["rel"], 2)
            for hf, r in ((0, 128), (1, EC - 128)):
                v.tensor_scalar(cand[0:r, hf, 0:NT], rel[0:r, hf, 0:NT], mm_[0:r, hf, 4:5], None, ALU.mult)
                e = v.tensor_scalar(cand[0:r, hf, NT:2 * NT], rel[0:r, hf, 0:NT], mm_[0:r, hf, 5:6], None, ALU.mult)
            e.then_inc(s["cand"], 1)
            dve.wait_ge(s["edge_t"], 1)
            v.tensor_copy(edgeT[:, :, 0:EC], ps[0:T, 7, 0:2 * EC].rearrange("p (a e) -> p a e", a=2)).then_inc(s["edgeT"], 1)
            dve.wait_ge(s["brow_t"], 1)
            v.tensor_scalar(cols[:, 0:L * KD], ps[:, 6, 0:L * KD], SCALE, None, ALU.mult)
            v.tensor_copy(cols[:, L * KD:], ps[:, 6, L * KD:3 * L * KD + KD]).then_inc(s["cols"], 1)
            dve.wait_ge(s["cand_t"], 1)
            v.tensor_reduce(red[:, :], ps[0:2 * NT, 5, 0:EC], AX_X, ALU.max).then_inc(s["red"], 1)
            dve.wait_ge(s["red_t"], 1)
            n_tab = [0]

            def tab_step(ins):
                n_tab[0] += 1
                ins.then_inc(s["tab"], 1)
                dve.wait_ge(s["tab"], n_tab[0])

            R = [rtab[:, i * NT:(i + 1) * NT] for i in range(6)]
            tab_step(v.tensor_copy(rtab[:, 0:2 * NT], ps[0:1, 5, 256:256 + 2 * NT]))
            tab_step(v.tensor_tensor(R[3], R[0], R[1], ALU.add))
            tab_step(v.tensor_scalar(R[4], R[3], float(-ECP), 1.0, ALU.add, ALU.max))
            tab_step(v.tensor_scalar(R[2], R[0], -1.0, float(ECP), ALU.mult, ALU.add))
            tab_step(v.tensor_scalar(tab[:, 0:NT], R[2], float(ECP - QUAD), None, ALU.min))
            tab_step(v.tensor_scalar(tab0[:, :], R[4], float(QUAD - 1), None, ALU.add))
            tab_step(v.tensor_scalar(tab[:, NT:2 * NT], tab0[:, :], QUAD.bit_length() - 1, None, ALU.arith_shift_right))
            tab_step(v.tensor_copy(R[5], tab[:, NT:2 * NT]))
            tab_step(v.memset(rtab[:, 0:1], 0.0))
            for t in range(1, NT):
                tab_step(v.tensor_tensor(rtab[:, t:t + 1], rtab[:, t - 1:t], R[5][:, t - 1:t], ALU.add))
            v.tensor_copy(tab[:, 2 * NT:3 * NT], R[0]).then_inc(s["tabi"], 1)
            dve.wait_ge(s["tabi"], 1)
            dve.wait_ge(s["edgeT"], 1)

            dve.wait_ge(s["condT"], 3)
            v.tensor_copy(condS[0:C + 1, :], condT[:, :])
            v.tensor_copy(condS[32:32 + C + 1, :], condT[:, :]).then_inc(s["condS0"], 1)
            dve.wait_ge(s["condS0"], 1)
            v.tensor_tensor(condS[64:64 + C + 1, :], condT[:, :], condS[0:C + 1, :].bitcast(F32), ALU.subtract).then_inc(s["condS"], 1)

            with dve.Fori(0, NT) as t:
                first = dve.value_load(tab[0:1, bass.ds(t, 1)], min_val=0, max_val=ECP - QUAD)
                quads = dve.value_load(tab[0:1, bass.ds(t + NT, 1)], min_val=1, max_val=EC // QUAD + 1)
                before = dve.value_load(tab[0:1, bass.ds(t + 2 * NT, 1)], min_val=0, max_val=(EC // QUAD + 1) * NT)
                with dve.Fori(0, quads) as i:
                    used = dve.snap((before + i) * QUAD)
                    chunk0 = dve.snap((first + i * QUAD).with_bounds(min_val=0, max_val=ECP - QUAD))
                    for b in range(QUAD):
                        dve.wait_ge(s["oh_used"], used + (b + 1))
                        v.tensor_scalar(oh_dst[:, b, 0:T], iota16[:, bass.ds(t * T, T)],
                                        edgeT[:, 1, bass.ds(chunk0 + b, 1)], None, ALU.is_equal)
                        v.tensor_scalar(oh_src[:, b, :], iota16[:, :], edgeT[:, 0, bass.ds(chunk0 + b, 1)], None,
                                        ALU.is_equal).then_inc(s["onehot"], 1)
                dve.wait_ge(s["ct"], AHEAD + (t + 1))
                v.tensor_reduce(deg[:, bass.ds(t, 1)], ct, AX_X, ALU.add).then_inc(s["ct_deg"], 1)

            def front_stats(f, c):
                for u in range(2):
                    e = v.bn_stats(stats[:, u, :], tile_of(c, u))
                e.then_inc(s["bn"], 1)
                dve.wait_ge(s["bn"], f + 1)
                settled(dve)
                for u in range(2):
                    e = v.bn_aggr(mv[:, u, :], stats[:, u, :])
                e.then_inc(s["stats"], 1)

            def tile_of(c, u):
                i = 2 * c + u
                return z[:, i, :] if isinstance(i, int) else z[:, bass.ds(i, 1), :].rearrange("p a d -> p (a d)")

            def front_norm(f, c):
                dve.wait_ge(s["r0"], f + 1)
                dve.wait_ge(s["stats"], f + 1)
                v.scalar_tensor_tensor(out=nt_a[:, :], in0=mv[:, :, 1], scalar=EPS, in1=r0[:, :], op0=ALU.add,
                                       op1=ALU.mult).then_inc(s["nw"], 1)
                dve.wait_ge(s["nw"], 4 * f + 1)
                v.tensor_tensor(nt_b[:, :], nt_a[:, :], r0[:, :], ALU.mult).then_inc(s["nw"], 1)
                dve.wait_ge(s["nw"], 4 * f + 2)
                v.tensor_scalar(nt_c[:, :], nt_b[:, :], -0.5, 1.5, ALU.mult, ALU.add).then_inc(s["nw"], 1)
                dve.wait_ge(s["nw"], 4 * f + 3)
                v.tensor_tensor(rstd[:, :], nt_c[:, :], r0[:, :], ALU.mult).then_inc(s["nw"], 1)
                dve.wait_ge(s["nw"], 4 * f + 4)
                for u in range(2):
                    e = v.tensor_scalar(xn[:, u, :], tile_of(c, u), mv[:, u, 0:1], rstd[:, u:u + 1], ALU.subtract, ALU.mult)
                e.then_inc(s["xn"], 1)

            def front_mod(f):
                dve.wait_ge(s["sb"], AHEAD + f + 1)
                dve.wait_ge(s["xn"], F0 + f + 1)
                dve.wait_ge(s["yTp"], AHEAD + f)
                for u in range(2):
                    e = v.scalar_tensor_tensor(out=y[:, u, :], in0=ps_sb[:, u, 0, :], scalar=1.0, in1=xn[:, u, :],
                                               op0=ALU.add, op1=ALU.mult)
                e.then_inc(s["ysc"], 1)
                dve.wait_ge(s["ysc"], f + 1)
                for u in range(2):
                    e = v.tensor_tensor(y[:, u, :], y[:, u, :], ps_sb[:, u, 1, :], ALU.add)
                e.then_inc(s["y"], 1)

            F0 = NC
            dve.wait_ge(s["x_ld"], 16 * NT)
            dve.wait_ge(s["ct_t"], AHEAD + 3 * NT)
            for c in range(NC):
                front_stats(c, c)
                front_norm(c, c)
                dve.wait_ge(s["xn"], c + 1)
                v.tensor_scalar(z[:, 2 * c:2 * c + 2, :], xn, 0.0, None, ALU.max).then_inc(s["z0"], 1)

            def yT_low(f):
                dve.wait_ge(s["yThi"], f + 1)
                v.tensor_tensor(yT[:, 1].rearrange("p (a k) n -> p a (k n)", a=2), ps_yT[:, :, 0:2 * W],
                                yT[:, 0].bitcast(F32).rearrange("p (a k) n -> p a (k n)", a=2), ALU.subtract).then_inc(s["yT"], 1)

            def h_low(l, c):
                for j in range(KD):
                    dve.wait_ge(s["hraw"], KD * (l * NC + c) + j + 1)
                    v.tensor_tensor(hT[:, 1, j, :], qc[:, j, :], hT[:, 0, j, :].bitcast(F32), ALU.subtract).then_inc(s["h_e"], 1)

            def split_m(l, i):
                dve.wait_ge(s["wm_hi"], 2 * l + i + 1)
                v.tensor_tensor(wmS[:, i, 1], wm[:, 1 + i], wmS[:, i, 0].bitcast(F32), ALU.subtract).then_inc(s["wmS"], 1)

            def k_out(l, c):
                for j in range(KD):
                    dve.wait_ge(s["khi"], KD * (l * NC + c) + (j | 1) + 1)
                    v.scalar_tensor_tensor(out=kT[:, 1, j, bass.ds(c * W, W)], in0=ps_yT[:, j // 2, (j % 2) * W:(j % 2 + 1) * W],
                                           scalar=cols[:, bass.ds(l * KD + (L * KD + j), 1)],
                                           in1=kT[:, 0, j, bass.ds(c * W, W)].bitcast(F32), op0=ALU.add,
                                           op1=ALU.subtract).then_inc(s["k_e"], 1)

            def v_out(l, c):
                dve.wait_ge(s["ldA"], 64 * (l + 1))
                dve.wait_ge(s["v_mm"], l * NC + c + 1)
                dve.wait_ge(s["v_e"], AHEAD + 2 * (l * NC + c))
                for u in range(2):
                    v.tensor_tensor(ztmp[:, u, :], ps_q[0:T, u, :], bvb[:, :], ALU.add).then_inc(s["vt"], 1)

            def score_max(G, U, u, first):
                dve.wait_ge(s["S"], U + 1)
                dve.wait_ge(s[f"st{u}"], 32 * (G + 1))
                if not first:
                    dve.wait_ge(s["Tp"], AHEAD + (3 * (U - 1)))
                settled(dve)
                v.tensor_tensor_reduce(out=P[:, u, :], in0=ps_S, in1=bt[:, u, :], scale=-1.0, scalar=FLOOR,
                                       op0=ALU.add, op1=ALU.min, accum_out=nmx[:, u:u + 1]).then_inc(s["ttr"], 1)

            def normalise(U, u):
                dve.wait_ge(s["exp"], U + 1)
                v.tensor_scalar(dmx[:, u:u + 1], den[:, u:u + 1], 1e-30, None, ALU.max).then_inc(s["dmx"], 1)
                dve.wait_ge(s["dmx"], U + 1)
                v.reciprocal(rden[:, u:u + 1], dmx[:, u:u + 1]).then_inc(s["rden"], 1)
                dve.wait_ge(s["rden"], U + 1)
                v.tensor_scalar(P[:, u, :], P[:, u, :], rden[:, u:u + 1], None, ALU.mult).then_inc(s["P"], 1)

            def turn_low(U, h, u):
                for i, (a, b) in enumerate(PIECES):
                    dve.wait_ge(s["Thi"], 3 * U + i + 1)
                    o = PT[:, h % 2, :, a:b, u * T:(u + 1) * T]
                    v.tensor_tensor(o[:, 1], ps_T[0:T, i, 0:(b - a) * T].rearrange("p (t n) -> p t n", n=T),
                                    o[:, 0].bitcast(F32), ALU.subtract).then_inc(s["Te"], 1)

            def attn_add(l, g_):
                dve.wait_ge(s["ldO"], 32 * (l + 1))
                G = l * NC + g_
                for u in range(2):
                    dve.wait_ge(s["wo_mm"], 2 * G + u + 1)
                    v.tensor_tensor(ztmp[:, u, :], ps_q[0:T, u, :], bob[:, :], ALU.add).then_inc(s["zt"], 1)
                for u in range(2):
                    dve.wait_ge(s["zt"], 2 * G + u + 1)
                    v.tensor_tensor(tile_of(g_, u), tile_of(g_, u), ztmp[:, u, :], ALU.add).then_inc(s["zB"], 1)

            def mlp_add(l, c):
                dve.wait_ge(s["ldM"], 48 * (l + 1))
                a = l * NC + c
                for u in range(2):
                    dve.wait_ge(s["o_mm"], 2 * a + u + 1)
                    v.tensor_tensor(ztmp[:, u, :], ps_q[0:T, u, :], b2b[:, :], ALU.add).then_inc(s["zct"], 1)
                for u in range(2):
                    dve.wait_ge(s["zct"], 2 * a + u + 1)
                    v.tensor_tensor(tile_of(c, u), tile_of(c, u), ztmp[:, u, :], ALU.add).then_inc(s["zC"], 1)

            def attn_chunk(l, g_, last):
                G = l * NC + g_
                for k in range(UNITS):
                    n = k + 2
                    if n < UNITS or not last:
                        score_max(G + n // UNITS, UNITS * G + n, n % 2, False)
                    turn_low(UNITS * G + k, k // 2, k % 2)
                    if n < UNITS or not last:
                        normalise(UNITS * G + n, n % 2)
                attn_add(l, g_)

            dve.wait_ge(s["z0"], NC)
            with dve.Fori(0, L) as l:
                f = 2 * NC * l
                dve.wait_ge(s["zC"], AHEAD + f)
                front_stats(F0 + f, 0)
                front_norm(F0 + f, 0)
                front_mod(f)
                with dve.Fori(0, NC - 1) as c:
                    yT_low(f + c)
                    front_stats(F0 + f + c + 1, c + 1)
                    front_norm(F0 + f + c + 1, c + 1)
                    k_out(l, c)
                    front_mod(f + c + 1)
                    v_out(l, c)
                yT_low(f + NC - 1)
                k_out(l, NC - 1)
                v_out(l, NC - 1)
                for u in range(2):
                    score_max(l * NC, UNITS * NC * l + u, u, True)
                    normalise(UNITS * NC * l + u, u)
                with dve.Fori(0, NC - 1) as g_:
                    attn_chunk(l, g_, False)
                attn_chunk(l, NC - 1, True)
                dve.wait_ge(s["zB"], AHEAD + f + 2 * NC)
                dve.wait_ge(s["Tp"], AHEAD + 3 * UNITS * NC * (l + 1))
                f2 = 2 * NC * l + NC
                front_stats(F0 + f2, 0)
                front_norm(F0 + f2, 0)
                front_mod(f2)
                split_m(l, 0)
                split_m(l, 1)
                with dve.Fori(0, NC - 1) as c:
                    yT_low(f2 + c)
                    front_stats(F0 + f2 + c + 1, c + 1)
                    front_norm(F0 + f2 + c + 1, c + 1)
                    h_low(l, c)
                    front_mod(f2 + c + 1)
                    mlp_add(l, c)
                yT_low(f2 + NC - 1)
                h_low(l, NC - 1)
                mlp_add(l, NC - 1)

            v.tensor_scalar(dis_b[:, :], deg[:, :], 1.0, None, ALU.add).then_inc(s["g_dg"], 1)
            dve.wait_ge(s["g_dg"], 3)
            v.tensor_tensor(dis_a[:, :], dis_b[:, :], dis0[:, :], ALU.mult).then_inc(s["g_dg"], 1)
            dve.wait_ge(s["g_dg"], 4)
            v.tensor_tensor(dis_a[:, :], dis_a[:, :], dis0[:, :], ALU.mult).then_inc(s["g_dg"], 1)
            dve.wait_ge(s["g_dg"], 5)
            v.tensor_scalar(dis_b[:, :], dis_a[:, :], -0.5, 1.5, ALU.mult, ALU.add).then_inc(s["g_dg"], 1)
            dve.wait_ge(s["g_dg"], 6)
            v.tensor_tensor(dis[:, :], dis_b[:, :], dis0[:, :], ALU.mult).then_inc(s["g_dg"], 1)
            dve.wait_ge(s["g_dg"], 7)
            dve.wait_ge(s["wa"], AHEAD + 3 * (L + 1))
            for t in range(NT):
                e = v.tensor_scalar(diags[:, t * T:(t + 1) * T], ident[0:T, 0:T], dis[:, t:t + 1], None, ALU.mult)
            e.then_inc(s["g_diag"], 1)
            dve.wait_ge(s["g_cnt"], 16 * NT)
            for t in range(NT):
                e = v.tensor_tensor(counts[:, t, t * T:(t + 1) * T], counts[:, t, t * T:(t + 1) * T], ident[0:T, 0:T], ALU.add)
            e.then_inc(s["g_A"], 1)
            fg = 2 * NC * L
            dve.wait_ge(s["zC"], AHEAD + fg)
            for c in range(NC):
                dve.wait_ge(s["g_x"], 32 * (c + 1))
                v.tensor_tensor(z[:, 2 * c:2 * c + 2, :], z[:, 2 * c:2 * c + 2, :], xs[:, :, :], ALU.add).then_inc(s["g_xz"], 1)
                dve.wait_ge(s["g_xz"], c + 1)
                front_stats(F0 + fg + c, c)
                front_norm(F0 + fg + c, c)
                dve.wait_ge(s["xn"], F0 + fg + c + 1)
                dve.wait_ge(s["yTp"], AHEAD + fg + c)
                v.tensor_scalar(y, xn, 0.0, None, ALU.max).then_inc(s["y"], 1)
                yT_low(fg + c)
                for u in range(2):
                    dve.wait_ge(s["g_hs_mm"], 2 * c + u + 1)
                    v.tensor_scalar(hs[:, 2 * c + u, :], ps_q[0:T, u, :], dis[:, 2 * c + u:2 * c + u + 1], None,
                                    ALU.mult).then_inc(s["g_hs"], 1)
            dve.wait_ge(s["g_bc"], 1)
            v.tensor_copy(disb[:, :], psf[:, 0:N]).then_inc(s["g_disb"], 1)
            dve.wait_ge(s["g_disb"], 1)
            for j in range(KD):
                dve.wait_ge(s["g_ag"], j + 1)
                o = 1536 * (j % 2)
                v.tensor_tensor(aggT[:, j, :], psf[:, o:o + N], disb[:, :], ALU.mult).then_inc(s["g_agd"], 1)
            for t in range(NT):
                dve.wait_ge(s["g_hs_mm"], NT + t + 1)
                v.tensor_scalar(hs[:, t, :], ps_q[0:T, t % 2, :], dis[:, t:t + 1], None, ALU.mult).then_inc(s["g_hs"], 1)
            for t in range(NT):
                dve.wait_ge(s["g_ft"], t + 1)
                v.scalar_tensor_tensor(out=ztmp[:, t % 2, :], in0=ps[0:T, t % 2, :], scalar=dis[:, t:t + 1], in1=bvb[:, :],
                                       op0=ALU.mult, op1=ALU.add).then_inc(s["g_fin"], 1)
                dve.wait_ge(s["g_fin"], t + 1)
                v.tensor_tensor(z[:, t, :], z[:, t, :], ztmp[:, t % 2, :], ALU.add).then_inc(s["g_fz"], 1)

        @block.tensor
        def _(pe):
            mm = nc.tensor.matmul
            turn = nc.tensor.transpose
            pe.wait_ge(s["ident"], 2)
            pe.wait_ge(s["edge_f"], 1)
            off = 0
            for i, r in ((0, 128), (1, EC - 128), (2, 128), (3, EC - 128)):
                e = turn(ps[0:T, 7, off:off + r], edge_f[0:r, i, :], ident[0:r, 0:r])
                off += r
            e.then_inc(s["edge_t"], 1)
            pe.wait_ge(s["brow_ld"], 16 * 4)
            nb_ = 3 * L * KD + KD
            turn(ps[:, 6, 0:nb_], brow[:, :], ident[0:nb_, 0:nb_]).then_inc(s["brow_t"], 1)
            pe.wait_ge(s["cand"], 1)
            turn(ps[0:2 * NT, 5, 0:128], cand[:, 0, :], ident[:, :])
            turn(ps[0:2 * NT, 5, 128:EC], cand[0:EC - 128, 1, :], ident[0:EC - 128, 0:EC - 128]).then_inc(s["cand_t"], 1)
            pe.wait_ge(s["red"], 1)
            turn(ps[0:1, 5, 256:256 + 2 * NT], red[:, 0:1], ident[0:2 * NT, 0:2 * NT]).then_inc(s["red_t"], 1)
            pe.wait_ge(s["emb"], 1)
            pe.wait_ge(s["small_ld"], 16 * 5)
            for a, b in COLS:
                mm(psf[0:C, a:b], fw1[:, :], embT[:, a:b], start=True, stop=True).then_inc(s["emb_h"], 1)
            pe.wait_ge(s["h1"], 1)
            pe.wait_ge(s["cols"], 1)
            pe.wait_ge(s["tabi"], 1)
            pe.wait_ge(s["edgeT"], 1)
            for a, b in COLS:
                mm(psf[0:C, 2048 + a:2048 + b], fw2[:, :], h1T[:, a:b], start=True, stop=True).then_inc(s["cond_mm"], 1)
            pe.wait_ge(s["consts"], 14)
            pe.wait_ge(s["condT"], 3)
            mm(ps[0:T, 7, :], zeros16[:, 0:T], zeros16[:, :], start=True, stop=True).then_inc(s["oh_used"], QUAD)
            with pe.Fori(0, NT) as t:
                quads = pe.value_load(tab[0:1, bass.ds(t + NT, 1)], min_val=1, max_val=EC // QUAD + 1)
                before = pe.value_load(tab[0:1, bass.ds(t + 2 * NT, 1)], min_val=0, max_val=(EC // QUAD + 1) * NT)
                pe.wait_ge(s["ct"], AHEAD + t)
                for a, b in COLS:
                    mm(psf[0:T, a:b], zeros16[:, 0:T], zeros16[:, 0:b - a], start=True, stop=False, skip_group_check=True)
                with pe.Fori(0, quads) as i:
                    done = pe.snap((before + i) * QUAD)
                    for q in range(QUAD):
                        pe.wait_ge(s["onehot"], done + (q + 1))
                        for a, b in COLS:
                            e = mm(psf[0:T, a:b], oh_dst[:, q, 0:T], oh_src[:, q, a:b], start=False, stop=False,
                                   skip_group_check=True)
                        e.then_inc(s["oh_used"], 1)
                for a, b in COLS:
                    e = mm(psf[0:T, a:b], zeros16[:, 0:T], zeros16[:, 0:b - a], start=False, stop=True, skip_group_check=True)
                e.then_inc(s["ct_mm"], 1)
                pe.wait_ge(s["ct"], AHEAD + t + 1)
                pe.wait_ge(s["ct_e"], AHEAD + 3 * t)
                for p, (a, b) in enumerate(PIECES):
                    for m in range(a, b):
                        e = turn(ps_T[0:T, p, (m - a) * T:(m - a + 1) * T], ct[:, m * T:(m + 1) * T], ident[0:T, 0:T])
                    e.then_inc(s["ct_t"], 1)

            def product(out_, lhs, rhs, start, stop):
                for i, (a, b) in enumerate(((0, 0), (0, 1), (1, 0))):
                    e = mm(out_, lhs(a), rhs(b), start=start and i == 0, stop=stop and i == 2)
                return e

            def scale_bias(f, i):
                pe.wait_ge(s["condc"], f + 1)
                pe.wait_ge(s["lnS"], i + 1)
                pe.wait_ge(s["y"], AHEAD + f)
                for u in range(2):
                    for a in range(2):
                        e = mm(ps_sb[:, u, a, :], condc[:, u * T:(u + 1) * T], lnS[:, a, :], start=True, stop=True)
                e.then_inc(s["sb"], 1)

            def turn_y(f, k_e=None):
                pe.wait_ge(s["y"], AHEAD + f + 1)
                pe.wait_ge(s["yT"], AHEAD + f)
                if k_e is not None:
                    pe.wait_ge(s["k_e"], AHEAD + k_e)
                for k in range(KD):
                    for u in range(2):
                        o = (k % 2) * W + u * T
                        e = turn(ps_yT[:, k // 2, o:o + T], y[:, u, k * 128:(k + 1) * 128], ident[0:T, 0:T])
                e.then_inc(s["yTp"], 1)

            def features(out_banks, w, rhs, name):
                for j in range(KD):
                    for k in range(KD):
                        e = product(out_banks[:, j // 2, (j % 2) * W:(j % 2 + 1) * W], lambda i: w[:, i, k, j * 128:(j + 1) * 128],
                                    lambda i: rhs[:, i, k, :], k == 0, k == KD - 1)
                    e.then_inc(s[name], 1)

            def nodes(u, lhs, w):
                for k in range(KD):
                    e = product(ps_q[0:T, u, :], lambda i: lhs[:, i, k, u * T:(u + 1) * T], lambda i: w[:, i, k, :],
                                k == 0, k == KD - 1)
                return e

            def project(l, c, more):
                a, f = l * NC + c, 2 * NC * l + c
                pe.wait_ge(s["yT"], AHEAD + f + 1)
                pe.wait_ge(s["wa"], AHEAD + 3 * (l + 1))
                pe.wait_ge(s["vt"], AHEAD + 2 * a)
                features(ps_q, WQ, yT, "q_mm")
                features(ps_yT, WK, yT, "k_mm")
                if more:
                    scale_bias(f + 1, 2 * l)
                pe.wait_ge(s["q_e"], KD * (a + 1))
                for u in range(2):
                    e = nodes(u, yT, WV)
                e.then_inc(s["v_mm"], 1)
                if more:
                    turn_y(f + 1, KD * (a + 1))

            def mlp(l, c, more):
                a, f = l * NC + c, 2 * NC * l + NC + c
                pe.wait_ge(s["yT"], AHEAD + f + 1)
                pe.wait_ge(s["wmS"], 2 * l + 1)
                pe.wait_ge(s["zC"], AHEAD + 2 * a)
                features(ps_q, wmS[:, 0], yT, "h_mm")
                if more:
                    scale_bias(f + 1, 2 * l + 1)
                pe.wait_ge(s["h_e"], KD * (a + 1))
                pe.wait_ge(s["wmS"], 2 * l + 2)
                for u in range(2):
                    nodes(u, hT, wmS[:, 1]).then_inc(s["o_mm"], 1)
                if more:
                    turn_y(f + 1)

            def scores(G, U, h, u):
                pe.wait_ge(s["qg"], AHEAD + (H * G + h + 1))
                pe.wait_ge(s["ttr"], AHEAD + U)
                for a, b in COLS:
                    e = product(psf[0:T, a:b], lambda i: qg[:, i, h, u * T:(u + 1) * T], lambda i: kT[:, i, h, a:b], True, True)
                e.then_inc(s["S"], 1)

            def turn_probs(U, u):
                pe.wait_ge(s["P"], U + 1)
                pe.wait_ge(s["Te"], AHEAD + 3 * U)
                for p, (a, b) in enumerate(PIECES):
                    for m in range(a, b):
                        e = turn(ps_T[0:T, p, (m - a) * T:(m - a + 1) * T], P[:, u, m * T:(m + 1) * T], ident[0:T, 0:T])
                    e.then_inc(s["Tp"], 1)

            def attend(G, h, part):
                ms = (range(0, NT // 2), range(NT // 2, NT), range(NT))[part]
                if part != 1:
                    pe.wait_ge(s["Te"], AHEAD + 3 * UNITS * G + 3 * (2 * h + 2))
                    if h < 2:
                        pe.wait_ge(s["zB"], AHEAD + 2 * G)
                    else:
                        pe.wait_ge(s["oT"], H * G + h - 1)
                for m in ms:
                    e = product(ps_q[:, h % 2, 0:W], lambda i: V[:, i, m, h * DH:(h + 1) * DH], lambda i: PT[:, h % 2, i, m, :],
                                m == 0, m == NT - 1)
                if part != 0:
                    e.then_inc(s["PV"], 1)

            def attn_group(l, g_, last):
                G = l * NC + g_
                for k in range(UNITS):
                    n = k + 2
                    if n < UNITS or not last:
                        scores(G + n // UNITS, UNITS * G + n, n % UNITS // 2, n % 2)
                    turn_probs(UNITS * G + k, k % 2)
                    if k >= 2:
                        attend(G, k // 2 - 1, k % 2)
                attend(G, H - 1, 2)
                pe.wait_ge(s["oT"], H * (G + 1))
                pe.wait_ge(s["ldO"], 32 * (l + 1))
                for u in range(2):
                    for k in range(KD):
                        e = mm(ps_q[0:T, u, :], outTg[:, k, u * T:(u + 1) * T], WO[:, k, :], start=(k == 0), stop=(k == KD - 1))
                    e.then_inc(s["wo_mm"], 1)

            pe.wait_ge(s["ct_e"], AHEAD + 3 * NT)
            with pe.Fori(0, L) as l:
                scale_bias(2 * NC * l, 2 * l)
                pe.wait_ge(s["zC"], AHEAD + 2 * NC * l)
                settled(pe)
                turn_y(2 * NC * l)
                with pe.Fori(0, NC - 1) as c:
                    project(l, c, True)
                project(l, NC - 1, False)
                pe.wait_ge(s["k_e"], AHEAD + KD * NC * (l + 1))
                pe.wait_ge(s["v_e"], AHEAD + 2 * NC * (l + 1))
                for u in range(2):
                    scores(l * NC, UNITS * NC * l + u, 0, u)
                with pe.Fori(0, NC - 1) as g_:
                    attn_group(l, g_, False)
                attn_group(l, NC - 1, True)
                pe.wait_ge(s["ttr"], AHEAD + UNITS * NC * (l + 1))
                pe.wait_ge(s["Te"], AHEAD + 3 * UNITS * NC * (l + 1))
                scale_bias(2 * NC * l + NC, 2 * l + 1)
                turn_y(2 * NC * l + NC)
                pe.wait_ge(s["zB"], AHEAD + 2 * NC * (l + 1))
                settled(pe)
                with pe.Fori(0, NC - 1) as c:
                    mlp(l, c, True)
                mlp(l, NC - 1, False)

            fg = 2 * NC * L
            pe.wait_ge(s["wa"], AHEAD + 3 * (L + 1))
            pe.wait_ge(s["zC"], AHEAD + 2 * NC * L)
            for c in range(NC):
                turn_y(fg + c)
                pe.wait_ge(s["yT"], AHEAD + fg + c + 1)
                pe.wait_ge(s["g_hs"], 2 * c)
                for u in range(2):
                    nodes(u, yT, WV).then_inc(s["g_hs_mm"], 1)
            pe.wait_ge(s["g_diag"], 1)
            pe.wait_ge(s["onesr"], 1)
            for a, b in COLS:
                e = mm(psf[:, a:b], ones[:, :], diags[:, a:b], start=True, stop=True)
            e.then_inc(s["g_bc"], 1)
            pe.wait_ge(s["g_disb"], 1)
            pe.wait_ge(s["g_A"], 1)
            pe.wait_ge(s["g_hs"], NT)
            for j in range(KD):
                if j >= 2:
                    pe.wait_ge(s["g_agd"], j - 1)
                o = 1536 * (j % 2)
                for a, b in COLS:
                    for m in range(NT):
                        e = mm(psf[:, o + a:o + b], hs[:, m, j * 128:(j + 1) * 128], counts[:, m, a:b],
                               start=(m == 0), stop=(m == NT - 1))
                e.then_inc(s["g_ag"], 1)
            pe.wait_ge(s["g_agT"], KD)
            pe.wait_ge(s["ldG"], 16)
            for t in range(NT):
                if t >= 2:
                    pe.wait_ge(s["g_hs"], NT + t - 1)
                for k in range(KD):
                    e = mm(ps_q[0:T, t % 2, :], aggT[:, k, t * T:(t + 1) * T], W2[:, k, :], start=(k == 0), stop=(k == KD - 1))
                e.then_inc(s["g_hs_mm"], 1)
            pe.wait_ge(s["g_hs"], 2 * NT)
            for t in range(NT):
                if t >= 2:
                    pe.wait_ge(s["g_fin"], t - 1)
                for m in range(NT):
                    e = mm(ps[0:T, t % 2, :], counts[:, m, t * T:(t + 1) * T], hs[:, m, :], start=(m == 0), stop=(m == NT - 1))
                e.then_inc(s["g_ft"], 1)


_P = "L0_gnn_"
_INS = ["x", "src", "dst", "node_vec1"] + [_P + n for n in (
    "f_w1 f_b1 f_w2 f_b2 s1_w s1_b b1_w b1_b wq bq wk bk wv bv wo bo s2_w s2_b b2_w b2_b m_w1 m_b1 m_w2 m_b2").split()] + [
    "L1_gnn_W1", "L1_gnn_b1", "L1_gnn_W2", "L1_gnn_b2"]


def kernel(**inputs):
    import numpy as _np
    import concourse.bacc as _bacc
    from concourse import mybir as _mybir
    from concourse.bass_utils import run_bass_kernel_spmd as _run

    nc = _bacc.Bacc("TRN2", target_bir_lowering=False, num_devices=1, dynamic_dma_scratch_size=1024)
    arrays, args = {}, []
    for name in _INS:
        a = _np.ascontiguousarray(inputs[name])
        arrays[f"in_{name}_dram"] = a
        args.append(nc.dram_tensor(f"in_{name}_dram", a.shape, _mybir.dt.from_np(a.dtype), kind="ExternalInput").ap())
    args.append(nc.dram_tensor("out_0_dram", (N, D), F32, kind="ExternalOutput").ap())
    build(nc, *args)
    r = _run(nc, [arrays], core_ids=[0])
    return r.results[0]["out_0_dram"]
```

```python
from contextlib import ExitStack

import concourse.bass as bass
from concourse import mybir

ALU = mybir.AluOpType
ACT = mybir.ActivationFunctionType
F32 = mybir.dt.float32
F32R = mybir.dt.float32r
F16 = mybir.dt.float16
BF16 = mybir.dt.bfloat16
I32 = mybir.dt.int32
AX_X = mybir.AxisListType.X

N = 1250
D = 512
E = 21250
L = 4
H = 4
DH = D // H
C = 16
NFREQ = 32
T = 125
NT = N // T
W = 2 * T
NC = NT // 2
KD = D // 128
EC = E // T
QUAD = 4
ECP = EC + QUAD
KC = 96
UNITS = 2 * H
EPS = 1e-5
SCALE = DH ** -0.5
BIG = 1e38
FLOOR = 1e30
MAGIC = 1.5 * 2.0 ** 23
COLS = [(0, 512), (512, 1024), (1024, N)]
PIECES = [(0, 4), (4, 8), (8, NT)]
AHEAD = 2
AHEAD_OF = "sb y yT yTp zC v_e ct ct_t ct_e bst_out bmask bdone ttr Te zt zB zct k_e Tp cnt_out q_st qg wa vt".split()
LOW_ROWS = 112


def build(nc, x, src, dst, node_vec1, f_w1, f_b1, f_w2, f_b2, s1_w, s1_b, b1_w, b1_b, wq, bq, wk, bk, wv, bv,
          wo, bo, s2_w, s2_b, b2_w, b2_b, m_w1, m_b1, m_w2, m_b2, g_W1, g_b1, g_W2, g_b2, out):
    counts_dram = nc.dram_tensor("counts_scratch", [N, N], F32, kind="Internal").ap()
    q_dram = nc.dram_tensor("q_scratch", [NC, 128, KD * W], F32, kind="Internal").ap()
    bias_dram = nc.dram_tensor("edge_bias_scratch", [N, N], F32, kind="Internal").ap()

    with ExitStack() as ctx:
        at = [(nc.sbuf_base + 31) // 32 * 32]

        def place(name, shape, dt, where):
            return nc.alloc_sbuf_tensor_at(name, shape, dt, offset=where)

        def region(nbytes):
            start = at[0]
            at[0] += (nbytes + 31) // 32 * 32
            assert at[0] <= nc.sbuf_usable_end, at[0]
            return start

        def sb(name, shape, dt=F32):
            n = 1
            for k in shape[1:]:
                n *= k
            return place(name, shape, dt, region(n * (2 if dt in (F16, BF16) else 4)))

        def sem(name):
            return ctx.enter_context(nc.semaphore(name))

        z = sb("z", [T, NT, D])
        r_kv = region(2 * 4 * KD * N + 2 * 4 * NT * D)
        kT = place("kT", [128, 2, KD, N], F32R, r_kv)
        V = place("V", [T, 2, NT, D], F32R, r_kv + 2 * 4 * KD * N)
        pbuf = sb("pbuf", [T, 2 * N])
        P = pbuf[:, :].rearrange("p (b n) -> p b n", b=2)
        xn = pbuf[:, 0:2 * D].rearrange("p (u d) -> p u d", u=2)
        y = pbuf[:, 2 * D:4 * D].rearrange("p (u d) -> p u d", u=2)
        r_pt = region(2 * 2 * 4 * NT * W + 2 * 4 * N)
        PT = place("PT", [T, 2, 2, NT, W], F32R, r_pt)
        wa = place("wa", [128, 3, 2, KD, D], F32R, r_pt)
        WV, WK, WQ = (wa[:, i] for i in range(3))
        r_bt = r_pt + 2 * 2 * 4 * NT * W
        bt = place("bt", [T, 2, N], F32, r_bt)
        r_wm = region(4 * 3 * KD * D)
        wm = place("wm", [128, 3, KD, D], F32, r_wm)
        WO = wm[:, 0]
        wa_raw = place("wa_raw", [128, 3, KD, D], F32, r_kv)
        wmS = place("wmS", [128, 2, 2, KD, D], F32R, r_kv + 4 * 3 * KD * D)
        hT = place("hT", [128, 2, KD, W], F32R, r_kv + 4 * 7 * KD * D)
        lnw = sb("lnw", [KC, 2, D])
        lnS = sb("lnS", [KC, 2, D], F32R)
        bvb = sb("bvb", [T, D])
        bob = sb("bob", [T, D])
        b2b = sb("b2b", [T, D])
        outTg = sb("outTg", [128, KD, W])
        r_qg = region(2 * 4 * KD * W)
        qg = place("qg", [128, 2, KD, W], F32R, r_qg)
        yT = place("yT", [128, 2, KD, W], F32R, r_qg)
        qc = sb("qc", [128, KD, W])
        condS = sb("condS", [KC, N], F32R)
        condc = sb("condc", [KC, W], F32R)
        ident = sb("ident", [128, 128])
        cols = sb("cols", [128, 3 * L * KD + KD])
        eps = sb("eps", [T, 1])
        stats = sb("stats", [T, 2, 6])
        mv = sb("mv", [T, 2, 2])
        lnv = sb("lnv", [T, 2])
        r0 = sb("r0", [T, 2])
        nt_a = sb("nt_a", [T, 2])
        nt_b = sb("nt_b", [T, 2])
        nt_c = sb("nt_c", [T, 2])
        rstd = sb("rstd", [T, 2])
        ztmp = sb("ztmp", [T, 2, D])
        nmx = sb("nmx", [T, 2])
        den = sb("den", [T, 2])
        dmx = sb("dmx", [T, 2])
        rden = sb("rden", [T, 2])
        deg = sb("deg", [T, NT])
        dis = sb("dis", [T, NT])
        dis0 = sb("dis0", [T, NT])
        dis_a = sb("dis_a", [T, NT])
        dis_b = sb("dis_b", [T, NT])
        def packer(start, end):
            cur = [start]

            def pack(name, shape, dt=F32):
                here = cur[0]
                n = 1
                for k in shape[1:]:
                    n *= k
                cur[0] += (n * (2 if dt in (F16, BF16) else 4) + 31) // 32 * 32
                assert cur[0] <= end + 31, (name, cur[0] - start)
                return place(name, shape, dt, here)

            return pack

        kv_end = r_kv + 2 * 4 * (KD * N + NT * D)
        late = packer(r_kv, kv_end)
        counts = late("counts", [T, NT, N])
        disb = late("disb", [128, N])
        aggT = late("aggT", [128, KD, N])
        ones = late("ones", [T, 128])
        hs = place("hs", [T, NT, D], F32, r_wm)
        W2 = place("W2", [128, KD, D], F32, r_pt + 2 * 4 * KD * D)
        late2 = packer(r_bt, r_bt + 2 * 4 * N)
        diags = late2("diags", [T, N])
        xs = late2("xs", [T, 2, D])
        early = packer(r_kv, kv_end - (4 * N + 24))
        early2 = packer(r_bt, r_bt + 2 * 4 * N)
        embT = early2("embT", [2 * NFREQ, N])
        h1T = early("h1T", [C, N])
        oh_src = early("oh_src", [T, QUAD, N], BF16)
        oh_dst = early("oh_dst", [T, QUAD, T + 1], BF16)
        iota16 = early("iota16", [T, N], F16)
        iota_i = early("iota_i", [T, N], I32)
        zeros16 = early("zeros16", [T, D], BF16)
        edge_i = early("edge_i", [128, 4, T], I32)
        edge_f = early("edge_f", [128, 4, T])
        edgeT = early("edgeT", [T, 2, ECP])
        nb = early("nb", [2 * NFREQ, N])
        ph = early("ph", [2 * NFREQ, N])
        phr = early("phr", [2 * NFREQ, N])
        condT = early("condT", [C + 1, N])
        cblk = place("cblk", [T, NT, T], F32, kv_end - (4 * N + 24))
        early4 = packer(r_wm, r_wm + 4 * 3 * KD * D)
        blk_max = early4("blk_max", [T, NT, T])
        blk_mask = early4("blk_mask", [T, NT, T])
        blk_ln = early4("blk_ln", [T, NT, T])
        blk_bias = early4("blk_bias", [T, NT, T])
        ct = pbuf[:, 0:N]
        early3 = packer(r_qg, r_qg + 2 * 4 * KD * W)
        stats_all = early3("stats_all", [T, NT, 6])
        mv_all = early3("mv_all", [T, NT, 2])
        fw1 = early("fw1", [2 * NFREQ, C])
        fw2 = early("fw2", [C, C])
        fb = early("fb", [C, 2])
        freq_i = early("freq_i", [2 * NFREQ, 1], I32)
        freq = early("freq", [2 * NFREQ, 1])
        offs = early("offs", [2 * NFREQ, 1])
        brow = early("brow", [3 * L * KD + KD, 128])
        low_i = early("low_i", [128, NT + 1], I32)
        low = early("low", [128, NT + 1])
        mm_ = early("mm_", [128, 2, 6])
        cand = early("cand", [128, 2, 2 * NT])
        rel = early("rel", [128, 2, 2 * NT])
        red = early("red", [2 * NT, 1])
        rtab = early("rtab", [1, 6 * NT])
        tab = early("tab", [1, 3 * NT], I32)
        tab0 = early("tab0", [1, NT], I32)

        ps = ctx.enter_context(nc.psum_tensor("ps", [128, 8, 512], F32))
        psf = ps[:, :, :].rearrange("p b n -> p (b n)")
        ps_S = psf[0:T, 0:N]
        ps_sb = ps[0:T, 0:4, :].rearrange("p (u a) n -> p u a n", u=2)
        ps_T = ps[:, 3:6, :]
        ps_yT = ps[:, 4:6, :]
        ps_q = ps[:, 6:8, :]

        s = {}
        for name in ("x_ld edge_ld small_ld brow_ld ident consts edge_f edge_t edgeT brow_t cols emb_u emb_r emb_f emb emb_h "
                     "h1 cond_mm condT rm rel cand cand_t red red_t tab prefix tabi onehot oh_used ct_mm ct ct_t ct_e "
                     "i_st bmax bln bmask bdone bst_out cnt_out condS0 condS lnhi lnS onesr "
                     "bn stats lnv r0 nw xn sb ysc y yTp yT condc "
                     "ldA ldLN ldO ldM q_mm q_e k_mm k_e v_mm v_e "
                     "S ttr exp dmx rden P Tp Te PV oT wo_mm zt zB st0 st1 qg qgh q_st q_ld khi vt vhi Thi wa_hi wa wm_hi wmS yThi hhi hraw ldG "
                     "h_mm h_e o_mm zct zC "
                     "g_cnt g_x g_xz g_A g_dg g_diag g_bc g_disb g_hs_mm g_hs g_ag g_agd g_agT g_ft g_fin g_fz g_out z0 settled").split():
            s[name] = sem(name)
        block = ctx.enter_context(nc.Block())

        def settled(eng):
            eng.sem_inc(s["settled"], 1)

        @block.sync
        def _(sp):
            sp.dma_start(edge_i[0:128, 0, :], src[0:128 * T].rearrange("(j p) -> j p", p=T)).then_inc(s["edge_ld"], 16)
            sp.dma_start(edge_i[0:EC - 128, 1, :], src[128 * T:E].rearrange("(j p) -> j p", p=T)).then_inc(s["edge_ld"], 16)
            sp.dma_start(edge_i[0:128, 2, :], dst[0:128 * T].rearrange("(j p) -> j p", p=T)).then_inc(s["edge_ld"], 16)
            sp.dma_start(edge_i[0:EC - 128, 3, :], dst[128 * T:E].rearrange("(j p) -> j p", p=T)).then_inc(s["edge_ld"], 16)
            sp.dma_start(nb[:, :], node_vec1.rearrange("n a -> a n").to_broadcast([2 * NFREQ, N])).then_inc(s["small_ld"], 16)
            sp.dma_start(fw1[:, :], f_w1).then_inc(s["small_ld"], 16)
            sp.dma_start(fw2[:, :], f_w2).then_inc(s["small_ld"], 16)
            sp.dma_start(fb[:, 0:1], f_b1.rearrange("(c a) -> c a", a=1)).then_inc(s["small_ld"], 16)
            sp.dma_start(fb[:, 1:2], f_b2.rearrange("(c a) -> c a", a=1)).then_inc(s["small_ld"], 16)
            for i, b in enumerate((bq, bk, m_b1)):
                sp.dma_start(brow[i * L * KD:(i + 1) * L * KD, :], b.rearrange("l (k p) -> (l k) p", p=128)).then_inc(s["brow_ld"], 16)
            sp.dma_start(brow[3 * L * KD:3 * L * KD + KD, :], g_b1.rearrange("(k p) -> k p", p=128)).then_inc(s["brow_ld"], 16)
            for t in range(NT):
                sp.dma_start(z[:, t, :], x[t * T:(t + 1) * T, :]).then_inc(s["x_ld"], 16)

            def load_w(slot, w, name):
                sp.dma_start(slot, w.rearrange("(k p) n -> p k n", p=128)).then_inc(s[name], 16)

            def lay(w, l):
                return w[bass.ds(l, 1)].rearrange("a k n -> (a k) n") if not isinstance(l, int) else w[l]

            def row(b, l):
                return b[bass.ds(l, 1), :] if not isinstance(l, int) else b[l:l + 1, :]

            def load_attn(l, to):
                load_w(to[:, 0], lay(wv, l), "ldA")
                load_w(to[:, 1], lay(wk, l), "ldA")
                load_w(to[:, 2], lay(wq, l), "ldA")
                sp.dma_start(bvb[:, :], row(bv, l).to_broadcast([T, D])).then_inc(s["ldA"], 16)

            def load_ln(l, sw, sbias, bw, bbias):
                for q in (0, 32, 64):
                    sp.dma_start(lnw[q:q + C, 0, :], lay(sw, l)).then_inc(s["ldLN"], 16)
                    sp.dma_start(lnw[q + C:q + C + 1, 0, :], row(sbias, l)).then_inc(s["ldLN"], 16)
                    sp.dma_start(lnw[q:q + C, 1, :], lay(bw, l)).then_inc(s["ldLN"], 16)
                    sp.dma_start(lnw[q + C:q + C + 1, 1, :], row(bbias, l)).then_inc(s["ldLN"], 16)

            def load_o(l):
                load_w(WO, lay(wo, l), "ldO")
                sp.dma_start(bob[:, :], row(bo, l).to_broadcast([T, D])).then_inc(s["ldO"], 16)

            def load_m(l):
                load_w(wm[:, 1], lay(m_w1, l), "ldM")
                load_w(wm[:, 2], lay(m_w2, l), "ldM")
                sp.dma_start(b2b[:, :], row(m_b2, l).to_broadcast([T, D])).then_inc(s["ldM"], 16)

            def load_bias(g, u):
                for a, b in ((0, LOW_ROWS), (LOW_ROWS, T)):
                    start = g * W + u * T + a
                    view = bias_dram[bass.ds(start, b - a), :] if not isinstance(g, int) else bias_dram[start:start + b - a, :]
                    sp.dma_start(bt[a:b, u, :], view).then_inc(s[f"st{u}"], 16)

            def q_view(c):
                return q_dram[c] if isinstance(c, int) else q_dram[bass.ds(c, 1)].rearrange("a p n -> (a p) n")

            qc_flat = qc[:, :, :].rearrange("p k n -> p (k n)")

            load_attn(0, wm)
            sp.wait_ge(s["consts"], 14)
            load_ln(0, s1_w, s1_b, b1_w, b1_b)
            by_tile = [d.rearrange("(a p) m -> p a m", p=T) for d in (counts_dram, bias_dram)]
            with sp.Fori(0, NT) as t:
                sp.wait_ge(s["ct_e"], AHEAD + 3 * (t + 1))
                sp.dma_start(by_tile[0][:, :, bass.ds(t * T, T)], cblk[:, :, :]).then_inc(s["cnt_out"], 16)
                sp.wait_ge(s["bdone"], AHEAD + t + 1)
                sp.dma_start(by_tile[1][:, :, bass.ds(t * T, T)], blk_bias[:, :, :]).then_inc(s["bst_out"], 16)
            sp.wait_ge(s["bst_out"], AHEAD + 16 * NT)
            load_o(0)
            load_m(0)

            def load_x(c):
                for u in range(2):
                    sp.dma_start(xs[:, u, :], x[(2 * c + u) * T:(2 * c + u + 1) * T, :]).then_inc(s["g_x"], 16)

            def layer(l, last):
                with sp.Fori(0, NC) as c:
                    sp.wait_ge(s["q_e"], KD * (l * NC + c + 1))
                    sp.dma_start(q_view(c), qc_flat).then_inc(s["q_st"], 16)
                sp.wait_ge(s["q_mm"], KD * NC * (l + 1))
                settled(sp)
                for u in range(2):
                    load_bias(0, u)
                sp.wait_ge(s["q_st"], AHEAD + 16 * NC * (l + 1))
                settled(sp)
                sp.dma_start(qc_flat, q_view(0)).then_inc(s["q_ld"], 16)
                sp.wait_ge(s["lnS"], 2 * l + 1)
                settled(sp)
                load_ln(l, s2_w, s2_b, b2_w, b2_b)
                with sp.Fori(0, NC - 1) as g:
                    G = l * NC + g
                    sp.wait_ge(s["qg"], AHEAD + H * (G + 1))
                    sp.dma_start(qc_flat, q_view(g + 1)).then_inc(s["q_ld"], 16)
                    for u in range(2):
                        sp.wait_ge(s["ttr"], AHEAD + (UNITS * G + UNITS - 1 + u))
                        load_bias(g + 1, u)
                sp.wait_ge(s["lnS"], 2 * l + 2)
                settled(sp)
                if not last:
                    load_ln(l + 1, s1_w, s1_b, b1_w, b1_b)
                sp.wait_ge(s["PV"], H * NC * (l + 1))
                settled(sp)
                if not last:
                    load_attn(l + 1, wa_raw)
                else:
                    load_w(wa_raw[:, 0], g_W1, "ldA")
                    sp.dma_start(bvb[:, :], g_b2.rearrange("(a n) -> a n", a=1).to_broadcast([T, D])).then_inc(s["ldA"], 16)
                    load_x(0)
                sp.wait_ge(s["zB"], AHEAD + (2 * NC * (l + 1)))
                settled(sp)
                if not last:
                    load_o(l + 1)
                sp.wait_ge(s["zC"], AHEAD + (2 * NC * (l + 1)))
                if not last:
                    load_m(l + 1)
                else:
                    sp.wait_ge(s["wa"], AHEAD + 3 * L + 1)
                    load_w(W2[:, :, :], g_W2, "ldG")

            with sp.Fori(0, L - 1) as l:
                layer(l, False)
            layer(L - 1, True)
            for c in range(1, NC):
                sp.wait_ge(s["g_xz"], c)
                load_x(c)
            sp.wait_ge(s["cnt_out"], AHEAD + 16 * NT)
            for t in range(NT):
                sp.dma_start(counts[:, t, :], counts_dram[t * T:(t + 1) * T, :]).then_inc(s["g_cnt"], 16)
            for t in range(NT):
                sp.wait_ge(s["g_fz"], t + 1)
                sp.dma_start(out[t * T:(t + 1) * T, :], z[:, t, :]).then_inc(s["g_out"], 16)
            sp.wait_ge(s["g_out"], 16 * NT)

        @block.gpsimd
        def _(pool):
            g = nc.gpsimd
            for name in AHEAD_OF:
                pool.sem_inc(s[name], AHEAD)
            g.memset(ident[:, :], 0.0).then_inc(s["ident"], 1)
            pool.wait_ge(s["ident"], 1)
            g.affine_select(out=ident[:, :], in_=ident[:, :], compare_op=ALU.not_equal, fill=1.0, base=0,
                            pattern=[[-1, 128]], channel_multiplier=1).then_inc(s["ident"], 1)
            g.iota(iota_i[:, :], pattern=[[1, N]], base=0, channel_multiplier=0).then_inc(s["consts"], 1)
            pool.wait_ge(s["consts"], 1)
            g.iota(low_i[:, 0:NT], pattern=[[T, NT]], base=0, channel_multiplier=0).then_inc(s["consts"], 1)
            pool.wait_ge(s["consts"], 2)
            g.iota(low_i[:, NT:NT + 1], pattern=[[0, 1]], base=0, channel_multiplier=1).then_inc(s["consts"], 1)
            pool.wait_ge(s["consts"], 3)
            g.iota(freq_i[0:NFREQ, :], pattern=[[0, 1]], base=1, channel_multiplier=1).then_inc(s["consts"], 1)
            pool.wait_ge(s["consts"], 4)
            g.iota(freq_i[NFREQ:2 * NFREQ, :], pattern=[[0, 1]], base=1, channel_multiplier=1).then_inc(s["consts"], 1)
            pool.wait_ge(s["consts"], 5)
            g.memset(offs[0:NFREQ, :], 0.0).then_inc(s["consts"], 1)
            pool.wait_ge(s["consts"], 6)
            g.memset(offs[NFREQ:2 * NFREQ, :], 0.25).then_inc(s["consts"], 1)
            pool.wait_ge(s["consts"], 7)
            g.memset(zeros16[:, :], 0.0).then_inc(s["consts"], 1)
            pool.wait_ge(s["consts"], 8)
            g.memset(eps[:, :], EPS).then_inc(s["consts"], 1)
            pool.wait_ge(s["consts"], 9)
            g.memset(condT[:, :], 1.0).then_inc(s["consts"], 1)
            pool.wait_ge(s["consts"], 10)
            g.memset(edgeT[:, :, EC:ECP], -1.0).then_inc(s["consts"], 1)
            pool.wait_ge(s["consts"], 11)
            g.memset(lnw[:, :, :], 0.0).then_inc(s["consts"], 1)
            pool.wait_ge(s["consts"], 12)
            g.memset(condS[:, :].bitcast(F32), 0.0).then_inc(s["consts"], 1)
            pool.wait_ge(s["consts"], 13)
            g.memset(lnS[:, :, :].bitcast(F32), 0.0).then_inc(s["consts"], 1)
            pool.wait_ge(s["consts"], 14)

            def split_wa(raw, l, i, loads=64):
                n = 3 * l + i
                pool.wait_ge(s["ldA"], 64 * l + loads)
                settled(pool)
                g.tensor_copy(wa[:, i, 0], raw[:, i]).then_inc(s["wa_hi"], 1)
                pool.wait_ge(s["wa_hi"], n + 1)
                settled(pool)
                g.tensor_tensor(wa[:, i, 1], raw[:, i], wa[:, i, 0].bitcast(F32), ALU.subtract).then_inc(s["wa"], 1)

            pool.wait_ge(s["emb_h"], len(COLS))
            settled(pool)
            for i in range(3):
                split_wa(wm, 0, i)

            def split_ln(i):
                pool.wait_ge(s["ldLN"], 192 * (i + 1))
                pool.wait_ge(s["sb"], AHEAD + NC * i)
                settled(pool)
                g.tensor_copy(lnS[:, :, :], lnw[:, :, :]).then_inc(s["lnhi"], 1)
                pool.wait_ge(s["lnhi"], i + 1)
                settled(pool)
                q = slice(32, 32 + C + 1)
                g.tensor_tensor(lnS[q, :, :], lnw[q, :, :], lnS[q, :, :].bitcast(F32), ALU.subtract).then_inc(s["lnS"], 1)
                pool.wait_ge(s["lnS"], i + 1)
                settled(pool)

            def cond_chunk(f, c):
                pool.wait_ge(s["sb"], AHEAD + f)
                settled(pool)
                g.tensor_copy(condc[:, :], condS[:, bass.ds(c * W, W)].bitcast(F32)).then_inc(s["condc"], 1)

            pool.wait_ge(s["condS"], 1)
            split_ln(0)
            cond_chunk(0, 0)

            with pool.Fori(0, NT) as t:
                pool.wait_ge(s["ct_e"], AHEAD + 3 * (t + 1))
                settled(pool)
                g.tensor_scalar(blk_max[:, :, :], cblk[:, :, :], 1.0, None, ALU.max).then_inc(s["bmax"], 1)
                pool.wait_ge(s["bdone"], AHEAD + t)
                settled(pool)
                g.tensor_scalar(blk_mask[:, :, :], cblk[:, :, :], 0.0, -BIG, ALU.is_equal, ALU.mult).then_inc(s["bmask"], 1)
                pool.wait_ge(s["bmask"], AHEAD + t + 1)
                pool.wait_ge(s["bln"], t + 1)
                pool.wait_ge(s["bst_out"], AHEAD + t * 16)
                settled(pool)
                g.tensor_tensor(blk_bias[:, :, :], blk_mask[:, :, :], blk_ln[:, :, :], ALU.add).then_inc(s["bdone"], 1)

            def q_head(G, h):
                pool.wait_ge(s["q_ld"], 16 * (G + 1))
                settled(pool)
                g.tensor_copy(qg[:, 0, h, :], qc[:, h, :]).then_inc(s["qgh"], 1)
                pool.wait_ge(s["qgh"], H * G + h + 1)
                settled(pool)
                g.tensor_tensor(qg[:, 1, h, :], qc[:, h, :], qg[:, 0, h, :].bitcast(F32), ALU.subtract).then_inc(s["qg"], 1)

            def v_split(l, c):
                for u in range(2):
                    i = 2 * (l * NC + c) + u
                    pool.wait_ge(s["vt"], AHEAD + i + 1)
                    settled(pool)
                    vh = V[:, 0, bass.ds(2 * c + u, 1), :].rearrange("p a d -> p (a d)")
                    vl = V[:, 1, bass.ds(2 * c + u, 1), :].rearrange("p a d -> p (a d)")
                    g.tensor_copy(vh, ztmp[:, u, :]).then_inc(s["vhi"], 1)
                    pool.wait_ge(s["vhi"], i + 1)
                    g.tensor_tensor(vl, ztmp[:, u, :], vh.bitcast(F32), ALU.subtract).then_inc(s["v_e"], 1)

            def layer(l, last):
                with pool.Fori(0, NC - 1) as c:
                    cond_chunk(2 * NC * l + c + 1, c + 1)
                    v_split(l, c)
                pool.wait_ge(s["v_mm"], NC * (l + 1))
                settled(pool)
                q_head(l * NC, 0)
                v_split(l, NC - 1)
                for h in range(1, H):
                    q_head(l * NC, h)
                with pool.Fori(0, NC - 1) as g_:
                    G = l * NC + g_
                    for h in range(H):
                        pool.wait_ge(s["S"], UNITS * G + 2 * h + 2)
                        q_head(G + 1, h)
                split_ln(2 * l + 1)
                for c in range(NC):
                    cond_chunk(2 * NC * l + NC + c, c)
                    if c >= 2 and not (last and c > 2):
                        split_wa(wa_raw, l + 1, c - 2, 32 if last else 64)
                if not last:
                    split_ln(2 * l + 2)
                    cond_chunk(2 * NC * (l + 1), 0)

            pool.wait_ge(s["cnt_out"], AHEAD + 16 * NT)
            with pool.Fori(0, L - 1) as l:
                layer(l, False)
            layer(L - 1, True)
            pool.wait_ge(s["zC"], AHEAD + 2 * NC * L)
            g.memset(ones[:, :], 1.0).then_inc(s["onesr"], 1)

        @block.scalar
        def _(act):
            sc = nc.scalar
            act.wait_ge(s["consts"], 14)
            act.wait_ge(s["emb_f"], 1)
            sc.activation(embT[:, :], phr[:, :], ACT.Sin, scale=6.2831850).then_inc(s["emb"], 1)
            act.wait_ge(s["emb_h"], 3)
            act.wait_ge(s["small_ld"], 16 * 5)
            sc.activation(h1T[:, :], psf[0:C, 0:N], ACT.Silu, bias=fb[:, 0:1]).then_inc(s["h1"], 1)
            sc.preload_act_table_set("natural_log_exp_and_others")
            for i, (a, b) in enumerate(COLS):
                act.wait_ge(s["cond_mm"], 3)
                sc.activation(condT[0:C, a:b], psf[0:C, 2048 + a:2048 + b], ACT.Identity, bias=fb[:, 1:2]).then_inc(s["condT"], 1)
            act.wait_ge(s["i_st"], 2)
            sc.activation(dis_a[:, :], mv_all[:, :, 1], ACT.Ln, bias=eps[:, :]).then_inc(s["i_st"], 1)
            act.wait_ge(s["i_st"], 3)
            sc.activation(dis0[:, :], dis_a[:, :], ACT.Exp, scale=-0.5).then_inc(s["i_st"], 1)
            act.wait_ge(s["i_st"], 9)
            for t in range(NT):
                sc.activation(z[:, t, :], z[:, t, :], ACT.Relu, bias=dis_b[:, t:t + 1], scale=dis[:, t:t + 1]).then_inc(s["z0"], 1)
            with act.Fori(0, NT) as t:
                act.wait_ge(s["ct_mm"], t + 1)
                act.wait_ge(s["ct_t"], AHEAD + 3 * t)
                sc.activation(ct, ps_S, ACT.Copy, accum_out=deg[:, bass.ds(t, 1)]).then_inc(s["ct"], 1)
                act.wait_ge(s["cnt_out"], AHEAD + 16 * t)
                act.wait_ge(s["bmask"], AHEAD + t)
                for p, (a, b) in enumerate(PIECES):
                    act.wait_ge(s["ct_t"], AHEAD + (t * 3 + p + 1))
                    sc.activation(cblk[:, a:b, :], ps_T[0:T, p, 0:(b - a) * T].rearrange("p (t n) -> p t n", n=T),
                                  ACT.Copy).then_inc(s["ct_e"], 1)
                act.wait_ge(s["bmax"], t + 1)
                sc.activation(blk_ln[:, :, :], blk_max[:, :, :], ACT.Ln).then_inc(s["bln"], 1)

            def rsqrt0(f):
                act.wait_ge(s["stats"], f + 1)
                sc.activation(lnv[:, :], mv[:, :, 1], ACT.Ln, bias=eps[:, :]).then_inc(s["lnv"], 1)
                act.wait_ge(s["lnv"], f + 1)
                sc.activation(r0[:, :], lnv[:, :], ACT.Exp, scale=-0.5).then_inc(s["r0"], 1)

            def yT_out(f):
                for a in range(2):
                    act.wait_ge(s["yTp"], AHEAD + 2 * f + a + 1)
                    sc.activation(yT[:, 0, 2 * a:2 * a + 2].rearrange("p k n -> p (k n)"), ps_yT[:, a, 0:2 * W],
                                  ACT.Copy).then_inc(s["yThi"], 1)

            def q_out(l, c):
                act.wait_ge(s["q_st"], AHEAD + 16 * (l * NC + c))
                act.wait_ge(s["qg"], AHEAD + H * NC * l)
                for j in range(KD):
                    act.wait_ge(s["q_mm"], KD * (l * NC + c) + (j | 1) + 1)
                    sc.activation(qc[:, j, :], ps_q[:, j // 2, (j % 2) * W:(j % 2 + 1) * W], ACT.Identity,
                                  bias=cols[:, bass.ds(l * KD + j, 1)], scale=SCALE).then_inc(s["q_e"], 1)

            def k_out(l, c):
                for j in range(KD):
                    act.wait_ge(s["k_mm"], KD * (l * NC + c) + (j | 1) + 1)
                    sc.activation(kT[:, 0, j, bass.ds(c * W, W)], ps_yT[:, j // 2, (j % 2) * W:(j % 2 + 1) * W], ACT.Identity,
                                  bias=cols[:, bass.ds(l * KD + (L * KD + j), 1)]).then_inc(s["khi"], 1)

            def h_out(l, c):
                for j in range(KD):
                    act.wait_ge(s["h_mm"], KD * (l * NC + c) + (j | 1) + 1)
                    for o, name in ((hT[:, 0, j, :], "hhi"), (qc[:, j, :], "hraw")):
                        sc.activation(o, ps_q[:, j // 2, (j % 2) * W:(j % 2 + 1) * W], ACT.Relu,
                                      bias=cols[:, bass.ds(2 * L * KD + l * KD + j, 1)]).then_inc(s[name], 1)

            def split_m(l):
                act.wait_ge(s["ldM"], 48 * (l + 1))
                act.wait_ge(s["PV"], H * NC * (l + 1))
                for i in range(2):
                    sc.activation(wmS[:, i, 0], wm[:, 1 + i], ACT.Copy).then_inc(s["wm_hi"], 1)

            def exp_unit(U, u):
                act.wait_ge(s["ttr"], AHEAD + U + 1)
                if u is not None:
                    sc.activation(P[:, u, :], P[:, u, :], ACT.Exp, bias=nmx[:, u:u + 1], scale=-1.0,
                                  accum_out=den[:, u:u + 1]).then_inc(s["exp"], 1)

            def turn_out(U, h, u):
                for i, (a, b) in enumerate(PIECES):
                    act.wait_ge(s["Tp"], AHEAD + 3 * U + i + 1)
                    sc.activation(PT[:, h % 2, 0, a:b, u * T:(u + 1) * T],
                                  ps_T[0:T, i, 0:(b - a) * T].rearrange("p (t n) -> p t n", n=T), ACT.Copy).then_inc(s["Thi"], 1)

            def attn_out(G, h):
                act.wait_ge(s["PV"], H * G + h + 1)
                sc.activation(outTg[:, h, :], ps_q[:, h % 2, 0:W], ACT.Copy).then_inc(s["oT"], 1)

            def unit(G, k, last):
                turn_out(UNITS * G + k, k // 2, k % 2)
                if k + 2 < UNITS or not last:
                    exp_unit(UNITS * G + k + 2, k % 2)

            def attn_first(G, before):
                unit(G, 0, False)
                if before:
                    attn_out(G - 1, H - 1)
                unit(G, 1, False)

            def attn_rest(G, last, norm=None):
                for k in range(2, UNITS):
                    unit(G, k, last)
                    if last and k == UNITS - 1:
                        rsqrt0(norm)
                    if k % 2:
                        attn_out(G, k // 2 - 1)

            def layer(l):
                f = 2 * NC * l
                with act.Fori(0, NC - 1) as c:
                    yT_out(f + c)
                    rsqrt0(f + c + 1)
                    q_out(l, c)
                    k_out(l, c)
                yT_out(f + NC - 1)
                q_out(l, NC - 1)
                k_out(l, NC - 1)
                exp_unit(UNITS * NC * l, 0)
                exp_unit(UNITS * NC * l + 1, 1)
                attn_first(l * NC, False)
                with act.Fori(0, NC - 1) as g_:
                    attn_rest(l * NC + g_, False)
                    attn_first(l * NC + g_ + 1, True)
                f2 = 2 * NC * l + NC
                attn_rest(l * NC + NC - 1, True, f2)
                attn_out(l * NC + NC - 1, H - 1)
                split_m(l)
                with act.Fori(0, NC) as c:
                    yT_out(f2 + c)
                    rsqrt0(f2 + c + 1)
                    h_out(l, c)

            rsqrt0(0)
            with act.Fori(0, L) as l:
                layer(l)
            fg = 2 * NC * L
            yT_out(fg)
            act.wait_ge(s["g_dg"], 1)
            sc.activation(dis_a[:, :], dis_b[:, :], ACT.Ln).then_inc(s["g_dg"], 1)
            act.wait_ge(s["g_dg"], 2)
            sc.activation(dis0[:, :], dis_a[:, :], ACT.Exp, scale=-0.5).then_inc(s["g_dg"], 1)
            for c in range(1, NC):
                rsqrt0(fg + c)
                yT_out(fg + c)
            for j in range(KD):
                act.wait_ge(s["g_agd"], j + 1)
                sc.activation(aggT[:, j, :], aggT[:, j, :], ACT.Relu,
                              bias=cols[:, 3 * L * KD + j:3 * L * KD + j + 1]).then_inc(s["g_agT"], 1)

        @block.vector
        def _(dve):
            v = nc.vector
            dve.wait_ge(s["edge_ld"], 16 * 4)
            for i, r in ((0, 128), (1, EC - 128), (2, 128), (3, EC - 128)):
                e = v.tensor_copy(edge_f[0:r, i, :], edge_i[0:r, i, :])
            e.then_inc(s["edge_f"], 1)
            dve.wait_ge(s["consts"], 14)
            v.tensor_copy(low[:, :], low_i[:, :]).then_inc(s["prefix"], 1)
            v.tensor_copy(iota16[:, :], iota_i[:, :])
            v.tensor_scalar(freq[:, :], freq_i[:, :], 1.0 / 16, None, ALU.mult).then_inc(s["prefix"], 1)
            dve.wait_ge(s["prefix"], 2)
            dve.wait_ge(s["small_ld"], 16 * 5)
            v.tensor_scalar(ph[:, :], nb[:, :], freq[:, 0:1], offs[:, 0:1], ALU.mult, ALU.add).then_inc(s["emb_u"], 1)
            dve.wait_ge(s["emb_u"], 1)
            v.tensor_scalar(phr[:, :], ph[:, :], MAGIC, -MAGIC, ALU.add, ALU.add).then_inc(s["emb_r"], 1)
            dve.wait_ge(s["emb_r"], 1)
            v.tensor_tensor(phr[:, :], ph[:, :], phr[:, :], ALU.subtract).then_inc(s["emb_f"], 1)
            dve.wait_ge(s["edge_f"], 1)
            for hf, r in ((0, 128), (1, EC - 128)):
                v.tensor_reduce(mm_[0:r, hf, 0:1], edge_f[0:r, 2 + hf, :], AX_X, ALU.max)
                v.tensor_reduce(mm_[0:r, hf, 1:2], edge_f[0:r, 2 + hf, :], AX_X, ALU.min)
                v.tensor_scalar(mm_[0:r, hf, 4:5], low[0:r, NT:NT + 1], -1.0, float(ECP - 128 * hf), ALU.mult, ALU.add)
                e = v.tensor_scalar(mm_[0:r, hf, 5:6], low[0:r, NT:NT + 1], float(1 + 128 * hf), None, ALU.add)
            e.then_inc(s["rm"], 1)
            dve.wait_ge(s["rm"], 1)
            for hf, r in ((0, 128), (1, EC - 128)):
                v.tensor_scalar(mm_[0:r, hf, 2:3], mm_[0:r, hf, 1:2], float(-T), None, ALU.add)
                e = v.tensor_scalar(rel[0:r, hf, NT:2 * NT], low[0:r, 0:NT], mm_[0:r, hf, 0:1], None, ALU.is_le)
            e.then_inc(s["rel"], 1)
            dve.wait_ge(s["rel"], 1)
            for hf, r in ((0, 128), (1, EC - 128)):
                e = v.scalar_tensor_tensor(out=rel[0:r, hf, 0:NT], in0=low[0:r, 0:NT], scalar=mm_[0:r, hf, 2:3],
                                           in1=rel[0:r, hf, NT:2 * NT], op0=ALU.is_gt, op1=ALU.mult)
            e.then_inc(s["rel"], 1)
            dve.wait_ge(s["rel"], 2)
            for hf, r in ((0, 128), (1, EC - 128)):
                v.tensor_scalar(cand[0:r, hf, 0:NT], rel[0:r, hf, 0:NT], mm_[0:r, hf, 4:5], None, ALU.mult)
                e = v.tensor_scalar(cand[0:r, hf, NT:2 * NT], rel[0:r, hf, 0:NT], mm_[0:r, hf, 5:6], None, ALU.mult)
            e.then_inc(s["cand"], 1)
            dve.wait_ge(s["edge_t"], 1)
            v.tensor_copy(edgeT[:, :, 0:EC], ps[0:T, 7, 0:2 * EC].rearrange("p (a e) -> p a e", a=2)).then_inc(s["edgeT"], 1)
            dve.wait_ge(s["brow_t"], 1)
            v.tensor_scalar(cols[:, 0:L * KD], ps[:, 6, 0:L * KD], SCALE, None, ALU.mult)
            v.tensor_copy(cols[:, L * KD:], ps[:, 6, L * KD:3 * L * KD + KD]).then_inc(s["cols"], 1)
            dve.wait_ge(s["cand_t"], 1)
            v.tensor_reduce(red[:, :], ps[0:2 * NT, 5, 0:EC], AX_X, ALU.max).then_inc(s["red"], 1)
            dve.wait_ge(s["red_t"], 1)
            n_tab = [0]

            def tab_step(ins):
                n_tab[0] += 1
                ins.then_inc(s["tab"], 1)
                dve.wait_ge(s["tab"], n_tab[0])

            R = [rtab[:, i * NT:(i + 1) * NT] for i in range(6)]
            tab_step(v.tensor_copy(rtab[:, 0:2 * NT], ps[0:1, 5, 256:256 + 2 * NT]))
            tab_step(v.tensor_tensor(R[3], R[0], R[1], ALU.add))
            tab_step(v.tensor_scalar(R[4], R[3], float(-ECP), 1.0, ALU.add, ALU.max))
            tab_step(v.tensor_scalar(R[2], R[0], -1.0, float(ECP), ALU.mult, ALU.add))
            tab_step(v.tensor_scalar(tab[:, 0:NT], R[2], float(ECP - QUAD), None, ALU.min))
            tab_step(v.tensor_scalar(tab0[:, :], R[4], float(QUAD - 1), None, ALU.add))
            tab_step(v.tensor_scalar(tab[:, NT:2 * NT], tab0[:, :], QUAD.bit_length() - 1, None, ALU.arith_shift_right))
            tab_step(v.tensor_copy(R[5], tab[:, NT:2 * NT]))
            tab_step(v.memset(rtab[:, 0:1], 0.0))
            for t in range(1, NT):
                tab_step(v.tensor_tensor(rtab[:, t:t + 1], rtab[:, t - 1:t], R[5][:, t - 1:t], ALU.add))
            v.tensor_copy(tab[:, 2 * NT:3 * NT], R[0]).then_inc(s["tabi"], 1)
            dve.wait_ge(s["tabi"], 1)
            dve.wait_ge(s["edgeT"], 1)

            dve.wait_ge(s["condT"], 3)
            v.tensor_copy(condS[0:C + 1, :], condT[:, :])
            v.tensor_copy(condS[32:32 + C + 1, :], condT[:, :]).then_inc(s["condS0"], 1)
            dve.wait_ge(s["condS0"], 1)
            v.tensor_tensor(condS[64:64 + C + 1, :], condT[:, :], condS[0:C + 1, :].bitcast(F32), ALU.subtract).then_inc(s["condS"], 1)

            dve.wait_ge(s["x_ld"], 16 * NT)
            for t in range(NT):
                e = v.bn_stats(stats_all[:, t, :], z[:, t, :])
            e.then_inc(s["i_st"], 1)
            dve.wait_ge(s["i_st"], 1)
            for t in range(NT):
                e = v.bn_aggr(mv_all[:, t, :], stats_all[:, t, :])
            e.then_inc(s["i_st"], 1)
            dve.wait_ge(s["i_st"], 4)
            v.scalar_tensor_tensor(out=dis_a[:, :], in0=mv_all[:, :, 1], scalar=EPS, in1=dis0[:, :], op0=ALU.add,
                                   op1=ALU.mult).then_inc(s["i_st"], 1)
            dve.wait_ge(s["i_st"], 5)
            v.tensor_tensor(dis_b[:, :], dis_a[:, :], dis0[:, :], ALU.mult).then_inc(s["i_st"], 1)
            dve.wait_ge(s["i_st"], 6)
            v.tensor_scalar(dis_a[:, :], dis_b[:, :], -0.5, 1.5, ALU.mult, ALU.add).then_inc(s["i_st"], 1)
            dve.wait_ge(s["i_st"], 7)
            v.tensor_tensor(dis[:, :], dis_a[:, :], dis0[:, :], ALU.mult).then_inc(s["i_st"], 1)
            dve.wait_ge(s["i_st"], 8)
            v.scalar_tensor_tensor(out=dis_b[:, :], in0=mv_all[:, :, 0], scalar=-1.0, in1=dis[:, :], op0=ALU.mult,
                                   op1=ALU.mult).then_inc(s["i_st"], 1)

            with dve.Fori(0, NT) as t:
                first = dve.value_load(tab[0:1, bass.ds(t, 1)], min_val=0, max_val=ECP - QUAD)
                quads = dve.value_load(tab[0:1, bass.ds(t + NT, 1)], min_val=1, max_val=EC // QUAD + 1)
                before = dve.value_load(tab[0:1, bass.ds(t + 2 * NT, 1)], min_val=0, max_val=(EC // QUAD + 1) * NT)
                with dve.Fori(0, quads) as i:
                    used = dve.snap((before + i) * QUAD)
                    chunk0 = dve.snap((first + i * QUAD).with_bounds(min_val=0, max_val=ECP - QUAD))
                    for b in range(QUAD):
                        dve.wait_ge(s["oh_used"], used + (b + 1))
                        v.tensor_scalar(oh_dst[:, b, 0:T], iota16[:, bass.ds(t * T, T)],
                                        edgeT[:, 1, bass.ds(chunk0 + b, 1)], None, ALU.is_equal)
                        v.tensor_scalar(oh_src[:, b, :], iota16[:, :], edgeT[:, 0, bass.ds(chunk0 + b, 1)], None,
                                        ALU.is_equal).then_inc(s["onehot"], 1)

            def front_stats(f, c):
                for u in range(2):
                    e = v.bn_stats(stats[:, u, :], tile_of(c, u))
                e.then_inc(s["bn"], 1)
                dve.wait_ge(s["bn"], f + 1)
                settled(dve)
                for u in range(2):
                    e = v.bn_aggr(mv[:, u, :], stats[:, u, :])
                e.then_inc(s["stats"], 1)

            def tile_of(c, u):
                i = 2 * c + u
                return z[:, i, :] if isinstance(i, int) else z[:, bass.ds(i, 1), :].rearrange("p a d -> p (a d)")

            def front_norm(f, c):
                dve.wait_ge(s["r0"], f + 1)
                dve.wait_ge(s["stats"], f + 1)
                v.scalar_tensor_tensor(out=nt_a[:, :], in0=mv[:, :, 1], scalar=EPS, in1=r0[:, :], op0=ALU.add,
                                       op1=ALU.mult).then_inc(s["nw"], 1)
                dve.wait_ge(s["nw"], 4 * f + 1)
                v.tensor_tensor(nt_b[:, :], nt_a[:, :], r0[:, :], ALU.mult).then_inc(s["nw"], 1)
                dve.wait_ge(s["nw"], 4 * f + 2)
                v.tensor_scalar(nt_c[:, :], nt_b[:, :], -0.5, 1.5, ALU.mult, ALU.add).then_inc(s["nw"], 1)
                dve.wait_ge(s["nw"], 4 * f + 3)
                v.tensor_tensor(rstd[:, :], nt_c[:, :], r0[:, :], ALU.mult).then_inc(s["nw"], 1)
                dve.wait_ge(s["nw"], 4 * f + 4)
                for u in range(2):
                    e = v.tensor_scalar(xn[:, u, :], tile_of(c, u), mv[:, u, 0:1], rstd[:, u:u + 1], ALU.subtract, ALU.mult)
                e.then_inc(s["xn"], 1)

            def front_mod(f):
                dve.wait_ge(s["sb"], AHEAD + f + 1)
                dve.wait_ge(s["xn"], f + 1)
                dve.wait_ge(s["yTp"], AHEAD + 2 * f)
                for u in range(2):
                    e = v.scalar_tensor_tensor(out=y[:, u, :], in0=ps_sb[:, u, 0, :], scalar=1.0, in1=xn[:, u, :],
                                               op0=ALU.add, op1=ALU.mult)
                e.then_inc(s["ysc"], 1)
                dve.wait_ge(s["ysc"], f + 1)
                for u in range(2):
                    e = v.tensor_tensor(y[:, u, :], y[:, u, :], ps_sb[:, u, 1, :], ALU.add)
                e.then_inc(s["y"], 1)

            def yT_low(f):
                for a in range(2):
                    dve.wait_ge(s["yThi"], 2 * f + a + 1)
                    v.tensor_tensor(yT[:, 1, 2 * a:2 * a + 2].rearrange("p k n -> p (k n)"), ps_yT[:, a, 0:2 * W],
                                    yT[:, 0, 2 * a:2 * a + 2].bitcast(F32).rearrange("p k n -> p (k n)"),
                                    ALU.subtract).then_inc(s["yT"], 1)

            def h_low(l, c):
                for j in range(KD):
                    dve.wait_ge(s["hraw"], KD * (l * NC + c) + j + 1)
                    v.tensor_tensor(hT[:, 1, j, :], qc[:, j, :], hT[:, 0, j, :].bitcast(F32), ALU.subtract).then_inc(s["h_e"], 1)

            def split_m(l, i):
                dve.wait_ge(s["wm_hi"], 2 * l + i + 1)
                v.tensor_tensor(wmS[:, i, 1], wm[:, 1 + i], wmS[:, i, 0].bitcast(F32), ALU.subtract).then_inc(s["wmS"], 1)

            def k_out(l, c):
                for j in range(KD):
                    dve.wait_ge(s["khi"], KD * (l * NC + c) + (j | 1) + 1)
                    v.scalar_tensor_tensor(out=kT[:, 1, j, bass.ds(c * W, W)], in0=ps_yT[:, j // 2, (j % 2) * W:(j % 2 + 1) * W],
                                           scalar=cols[:, bass.ds(l * KD + (L * KD + j), 1)],
                                           in1=kT[:, 0, j, bass.ds(c * W, W)].bitcast(F32), op0=ALU.add,
                                           op1=ALU.subtract).then_inc(s["k_e"], 1)

            def v_out(l, c):
                dve.wait_ge(s["ldA"], 64 * (l + 1))
                dve.wait_ge(s["v_mm"], l * NC + c + 1)
                dve.wait_ge(s["v_e"], AHEAD + 2 * (l * NC + c))
                for u in range(2):
                    v.tensor_tensor(ztmp[:, u, :], ps_q[0:T, u, :], bvb[:, :], ALU.add).then_inc(s["vt"], 1)

            def score_max(G, U, u, first):
                dve.wait_ge(s["S"], U + 1)
                dve.wait_ge(s[f"st{u}"], 32 * (G + 1))
                if not first:
                    dve.wait_ge(s["Tp"], AHEAD + (3 * (U - 1)))
                settled(dve)
                v.tensor_tensor_reduce(out=P[:, u, :], in0=ps_S, in1=bt[:, u, :], scale=-1.0, scalar=FLOOR,
                                       op0=ALU.add, op1=ALU.min, accum_out=nmx[:, u:u + 1]).then_inc(s["ttr"], 1)

            def normalise(U, u):
                dve.wait_ge(s["exp"], U + 1)
                v.tensor_scalar(dmx[:, u:u + 1], den[:, u:u + 1], 1e-30, None, ALU.max).then_inc(s["dmx"], 1)
                dve.wait_ge(s["dmx"], U + 1)
                v.reciprocal(rden[:, u:u + 1], dmx[:, u:u + 1]).then_inc(s["rden"], 1)
                dve.wait_ge(s["rden"], U + 1)
                v.tensor_scalar(P[:, u, :], P[:, u, :], rden[:, u:u + 1], None, ALU.mult).then_inc(s["P"], 1)

            def turn_low(U, h, u):
                for i, (a, b) in enumerate(PIECES):
                    dve.wait_ge(s["Thi"], 3 * U + i + 1)
                    o = PT[:, h % 2, :, a:b, u * T:(u + 1) * T]
                    v.tensor_tensor(o[:, 1], ps_T[0:T, i, 0:(b - a) * T].rearrange("p (t n) -> p t n", n=T),
                                    o[:, 0].bitcast(F32), ALU.subtract).then_inc(s["Te"], 1)

            def attn_add(l, g_):
                dve.wait_ge(s["ldO"], 32 * (l + 1))
                G = l * NC + g_
                for u in range(2):
                    dve.wait_ge(s["wo_mm"], 2 * G + u + 1)
                    v.tensor_tensor(ztmp[:, u, :], ps_q[0:T, u, :], bob[:, :], ALU.add).then_inc(s["zt"], 1)
                for u in range(2):
                    dve.wait_ge(s["zt"], AHEAD + 2 * G + u + 1)
                    v.tensor_tensor(tile_of(g_, u), tile_of(g_, u), ztmp[:, u, :], ALU.add).then_inc(s["zB"], 1)

            def mlp_add(l, c):
                dve.wait_ge(s["ldM"], 48 * (l + 1))
                a = l * NC + c
                for u in range(2):
                    dve.wait_ge(s["o_mm"], 2 * a + u + 1)
                    v.tensor_tensor(ztmp[:, u, :], ps_q[0:T, u, :], b2b[:, :], ALU.add).then_inc(s["zct"], 1)
                    if u == 0:
                        yT_low(2 * NC * l + NC + c + 1)
                for u in range(2):
                    dve.wait_ge(s["zct"], AHEAD + 2 * a + u + 1)
                    v.tensor_tensor(tile_of(c, u), tile_of(c, u), ztmp[:, u, :], ALU.add).then_inc(s["zC"], 1)

            def unit(G, k, last):
                n = k + 2
                if n < UNITS or not last:
                    score_max(G + n // UNITS, UNITS * G + n, n % 2, False)
                turn_low(UNITS * G + k, k // 2, k % 2)
                if n < UNITS or not last:
                    normalise(UNITS * G + n, n % 2)

            def attn_first(l, g_, before):
                for k in range(2):
                    unit(l * NC + g_, k, False)
                if before:
                    attn_add(l, g_ - 1)

            def attn_rest(l, g_, last):
                for k in range(2, UNITS):
                    unit(l * NC + g_, k, last)

            def front_relu(c):
                f = 2 * NC * L + c
                dve.wait_ge(s["g_x"], 32 * (c + 1))
                v.tensor_tensor(z[:, 2 * c:2 * c + 2, :], z[:, 2 * c:2 * c + 2, :], xs[:, :, :], ALU.add).then_inc(s["g_xz"], 1)
                dve.wait_ge(s["g_xz"], c + 1)
                front_stats(f, c)
                front_norm(f, c)
                dve.wait_ge(s["xn"], f + 1)
                dve.wait_ge(s["yTp"], AHEAD + 2 * f)
                v.tensor_scalar(y, xn, 0.0, None, ALU.max).then_inc(s["y"], 1)

            def layer(l, last):
                f = 2 * NC * l
                dve.wait_ge(s["zC"], AHEAD + f)
                settled(dve)
                with dve.Fori(0, NC - 1) as c:
                    front_stats(f + c + 1, c + 1)
                    front_norm(f + c + 1, c + 1)
                    k_out(l, c)
                    front_mod(f + c + 1)
                    v_out(l, c)
                    yT_low(f + c + 1)
                k_out(l, NC - 1)
                v_out(l, NC - 1)
                for u in range(2):
                    score_max(l * NC, UNITS * NC * l + u, u, True)
                for u in range(2):
                    normalise(UNITS * NC * l + u, u)
                attn_first(l, 0, False)
                with dve.Fori(0, NC - 1) as g_:
                    attn_rest(l, g_, False)
                    attn_first(l, g_ + 1, True)
                attn_rest(l, NC - 1, True)
                f2 = 2 * NC * l + NC
                dve.wait_ge(s["zB"], AHEAD + f + 2 * (NC - 1))
                dve.wait_ge(s["Tp"], AHEAD + 3 * UNITS * NC * (l + 1))
                front_stats(f2, 0)
                front_norm(f2, 0)
                front_mod(f2)
                split_m(l, 0)
                attn_add(l, NC - 1)
                yT_low(f2)
                split_m(l, 1)
                dve.wait_ge(s["zB"], AHEAD + f + 2 * NC)
                settled(dve)
                with dve.Fori(0, NC - 1) as c:
                    front_stats(f2 + c + 1, c + 1)
                    front_norm(f2 + c + 1, c + 1)
                    h_low(l, c)
                    front_mod(f2 + c + 1)
                    mlp_add(l, c)
                dve.wait_ge(s["zC"], AHEAD + f + 2 * (NC - 1))
                if last:
                    front_relu(0)
                    h_low(l, NC - 1)
                else:
                    front_stats(f2 + NC, 0)
                    front_norm(f2 + NC, 0)
                    h_low(l, NC - 1)
                    front_mod(f2 + NC)
                mlp_add(l, NC - 1)

            dve.wait_ge(s["z0"], NT)
            dve.wait_ge(s["ct_t"], AHEAD + 3 * NT)
            front_stats(0, 0)
            front_norm(0, 0)
            front_mod(0)
            yT_low(0)
            with dve.Fori(0, L - 1) as l:
                layer(l, False)
            layer(L - 1, True)

            v.tensor_scalar(dis_b[:, :], deg[:, :], 1.0, None, ALU.add).then_inc(s["g_dg"], 1)
            dve.wait_ge(s["g_dg"], 3)
            v.tensor_tensor(dis_a[:, :], dis_b[:, :], dis0[:, :], ALU.mult).then_inc(s["g_dg"], 1)
            dve.wait_ge(s["g_dg"], 4)
            v.tensor_tensor(dis_a[:, :], dis_a[:, :], dis0[:, :], ALU.mult).then_inc(s["g_dg"], 1)
            dve.wait_ge(s["g_dg"], 5)
            v.tensor_scalar(dis_b[:, :], dis_a[:, :], -0.5, 1.5, ALU.mult, ALU.add).then_inc(s["g_dg"], 1)
            dve.wait_ge(s["g_dg"], 6)
            v.tensor_tensor(dis[:, :], dis_b[:, :], dis0[:, :], ALU.mult).then_inc(s["g_dg"], 1)
            dve.wait_ge(s["g_dg"], 7)
            fg = 2 * NC * L
            dve.wait_ge(s["zC"], AHEAD + fg)

            for c in range(NC):
                if c + 1 < NC:
                    front_relu(c + 1)
                for u in range(2):
                    dve.wait_ge(s["g_hs_mm"], 2 * c + u + 1)
                    v.tensor_scalar(hs[:, 2 * c + u, :], ps_q[0:T, u, :], dis[:, 2 * c + u:2 * c + u + 1], None,
                                    ALU.mult).then_inc(s["g_hs"], 1)
                if c + 1 < NC:
                    yT_low(fg + c + 1)
            dve.wait_ge(s["wa"], AHEAD + 3 * L + 1)
            for t in range(NT):
                e = v.tensor_scalar(diags[:, t * T:(t + 1) * T], ident[0:T, 0:T], dis[:, t:t + 1], None, ALU.mult)
            e.then_inc(s["g_diag"], 1)
            dve.wait_ge(s["g_cnt"], 16 * NT)
            for t in range(NT):
                e = v.tensor_tensor(counts[:, t, t * T:(t + 1) * T], counts[:, t, t * T:(t + 1) * T], ident[0:T, 0:T], ALU.add)
            e.then_inc(s["g_A"], 1)
            dve.wait_ge(s["g_bc"], 1)
            v.tensor_copy(disb[:, :], psf[:, 0:N]).then_inc(s["g_disb"], 1)
            dve.wait_ge(s["g_disb"], 1)
            for j in range(KD):
                dve.wait_ge(s["g_ag"], j + 1)
                o = 1536 * (j % 2)
                v.tensor_tensor(aggT[:, j, :], psf[:, o:o + N], disb[:, :], ALU.mult).then_inc(s["g_agd"], 1)
            for t in range(NT):
                dve.wait_ge(s["g_hs_mm"], NT + t + 1)
                v.tensor_scalar(hs[:, t, :], ps_q[0:T, t % 2, :], dis[:, t:t + 1], None, ALU.mult).then_inc(s["g_hs"], 1)
            for t in range(NT):
                dve.wait_ge(s["g_ft"], t + 1)
                v.scalar_tensor_tensor(out=ztmp[:, t % 2, :], in0=ps[0:T, t % 2, :], scalar=dis[:, t:t + 1], in1=bvb[:, :],
                                       op0=ALU.mult, op1=ALU.add).then_inc(s["g_fin"], 1)
                dve.wait_ge(s["g_fin"], t + 1)
                v.tensor_tensor(z[:, t, :], z[:, t, :], ztmp[:, t % 2, :], ALU.add).then_inc(s["g_fz"], 1)

        @block.tensor
        def _(pe):
            mm = nc.tensor.matmul
            turn = nc.tensor.transpose
            pe.wait_ge(s["ident"], 2)
            pe.wait_ge(s["edge_f"], 1)
            off = 0
            for i, r in ((0, 128), (1, EC - 128), (2, 128), (3, EC - 128)):
                e = turn(ps[0:T, 7, off:off + r], edge_f[0:r, i, :], ident[0:r, 0:r])
                off += r
            e.then_inc(s["edge_t"], 1)
            pe.wait_ge(s["brow_ld"], 16 * 4)
            nb_ = 3 * L * KD + KD
            turn(ps[:, 6, 0:nb_], brow[:, :], ident[0:nb_, 0:nb_]).then_inc(s["brow_t"], 1)
            pe.wait_ge(s["cand"], 1)
            turn(ps[0:2 * NT, 5, 0:128], cand[:, 0, :], ident[:, :])
            turn(ps[0:2 * NT, 5, 128:EC], cand[0:EC - 128, 1, :], ident[0:EC - 128, 0:EC - 128]).then_inc(s["cand_t"], 1)
            pe.wait_ge(s["red"], 1)
            turn(ps[0:1, 5, 256:256 + 2 * NT], red[:, 0:1], ident[0:2 * NT, 0:2 * NT]).then_inc(s["red_t"], 1)
            pe.wait_ge(s["emb"], 1)
            pe.wait_ge(s["small_ld"], 16 * 5)
            for a, b in COLS:
                mm(psf[0:C, a:b], fw1[:, :], embT[:, a:b], start=True, stop=True).then_inc(s["emb_h"], 1)
            pe.wait_ge(s["h1"], 1)
            pe.wait_ge(s["cols"], 1)
            pe.wait_ge(s["tabi"], 1)
            pe.wait_ge(s["edgeT"], 1)
            for a, b in COLS:
                mm(psf[0:C, 2048 + a:2048 + b], fw2[:, :], h1T[:, a:b], start=True, stop=True).then_inc(s["cond_mm"], 1)
            pe.wait_ge(s["consts"], 14)
            pe.wait_ge(s["condT"], 3)
            mm(ps[0:T, 7, :], zeros16[:, 0:T], zeros16[:, :], start=True, stop=True).then_inc(s["oh_used"], QUAD)
            with pe.Fori(0, NT) as t:
                quads = pe.value_load(tab[0:1, bass.ds(t + NT, 1)], min_val=1, max_val=EC // QUAD + 1)
                before = pe.value_load(tab[0:1, bass.ds(t + 2 * NT, 1)], min_val=0, max_val=(EC // QUAD + 1) * NT)
                pe.wait_ge(s["ct"], AHEAD + t)
                for a, b in COLS:
                    mm(psf[0:T, a:b], zeros16[:, 0:T], zeros16[:, 0:b - a], start=True, stop=False, skip_group_check=True)
                with pe.Fori(0, quads) as i:
                    done = pe.snap((before + i) * QUAD)
                    for q in range(QUAD):
                        pe.wait_ge(s["onehot"], done + (q + 1))
                        for a, b in COLS:
                            e = mm(psf[0:T, a:b], oh_dst[:, q, 0:T], oh_src[:, q, a:b], start=False, stop=False,
                                   skip_group_check=True)
                        e.then_inc(s["oh_used"], 1)
                for a, b in COLS:
                    e = mm(psf[0:T, a:b], zeros16[:, 0:T], zeros16[:, 0:b - a], start=False, stop=True, skip_group_check=True)
                e.then_inc(s["ct_mm"], 1)
                pe.wait_ge(s["ct"], AHEAD + t + 1)
                pe.wait_ge(s["ct_e"], AHEAD + 3 * t)
                for p, (a, b) in enumerate(PIECES):
                    for m in range(a, b):
                        e = turn(ps_T[0:T, p, (m - a) * T:(m - a + 1) * T], ct[:, m * T:(m + 1) * T], ident[0:T, 0:T])
                    e.then_inc(s["ct_t"], 1)

            def product(out_, lhs, rhs, start, stop):
                for i, (a, b) in enumerate(((0, 0), (0, 1), (1, 0))):
                    e = mm(out_, lhs(a), rhs(b), start=start and i == 0, stop=stop and i == 2)
                return e

            def scale_bias(f, i):
                pe.wait_ge(s["condc"], f + 1)
                pe.wait_ge(s["lnS"], i + 1)
                pe.wait_ge(s["y"], AHEAD + f)
                for u in range(2):
                    for a in range(2):
                        e = mm(ps_sb[:, u, a, :], condc[:, u * T:(u + 1) * T], lnS[:, a, :], start=True, stop=True)
                e.then_inc(s["sb"], 1)

            def turn_y(f, k_e=None):
                pe.wait_ge(s["y"], AHEAD + f + 1)
                pe.wait_ge(s["yT"], AHEAD + 2 * f)
                if k_e is not None:
                    pe.wait_ge(s["k_e"], AHEAD + k_e)
                for k in range(KD):
                    for u in range(2):
                        o = (k % 2) * W + u * T
                        e = turn(ps_yT[:, k // 2, o:o + T], y[:, u, k * 128:(k + 1) * 128], ident[0:T, 0:T])
                    if k % 2:
                        e.then_inc(s["yTp"], 1)

            def features(out_banks, w, rhs, name, f=None, free=None):
                for j in range(KD):
                    if free is not None and j % 2 == 0:
                        pe.wait_ge(s[free[0]], AHEAD + free[1] - 1 + j // 2)
                    for k in range(KD):
                        if f is not None and j == 0 and k % 2 == 0:
                            pe.wait_ge(s["yT"], AHEAD + 2 * f + k // 2 + 1)
                        e = product(out_banks[:, j // 2, (j % 2) * W:(j % 2 + 1) * W], lambda i: w[:, i, k, j * 128:(j + 1) * 128],
                                    lambda i: rhs[:, i, k, :], k == 0, k == KD - 1)
                    e.then_inc(s[name], 1)

            def nodes(u, lhs, w, blocks=None):
                for k in range(KD):
                    if blocks is not None:
                        pe.wait_ge(s["h_e"], blocks + k + 1)
                    e = product(ps_q[0:T, u, :], lambda i: lhs[:, i, k, u * T:(u + 1) * T], lambda i: w[:, i, k, :],
                                k == 0, k == KD - 1)
                return e

            def project(l, c, more):
                a, f = l * NC + c, 2 * NC * l + c
                pe.wait_ge(s["wa"], AHEAD + 3 * (l + 1))
                features(ps_q, WQ, yT, "q_mm", f, ("vt", 2 * a))
                features(ps_yT, WK, yT, "k_mm")
                if more:
                    scale_bias(f + 1, 2 * l)
                pe.wait_ge(s["q_e"], KD * (a + 1))
                for u in range(2):
                    e = nodes(u, yT, WV)
                e.then_inc(s["v_mm"], 1)
                if more:
                    turn_y(f + 1, KD * (a + 1))

            def mlp(l, c, next_norm):
                a, f = l * NC + c, 2 * NC * l + NC + c
                pe.wait_ge(s["wmS"], 2 * l + 1)
                features(ps_q, wmS[:, 0], yT, "h_mm", f, ("zct", 2 * a))
                if next_norm is not None:
                    scale_bias(f + 1, next_norm)
                pe.wait_ge(s["hraw"], KD * a + 2)
                pe.wait_ge(s["wmS"], 2 * l + 2)
                nodes(0, hT, wmS[:, 1], KD * a).then_inc(s["o_mm"], 1)
                turn_y(f + 1)
                pe.wait_ge(s["hraw"], KD * (a + 1))
                nodes(1, hT, wmS[:, 1]).then_inc(s["o_mm"], 1)

            def scores(G, U, h, u):
                pe.wait_ge(s["qg"], AHEAD + (H * G + h + 1))
                pe.wait_ge(s["ttr"], AHEAD + U)
                for a, b in COLS:
                    e = product(psf[0:T, a:b], lambda i: qg[:, i, h, u * T:(u + 1) * T], lambda i: kT[:, i, h, a:b], True, True)
                e.then_inc(s["S"], 1)

            def turn_probs(U, u):
                pe.wait_ge(s["P"], U + 1)
                pe.wait_ge(s["Te"], AHEAD + 3 * U)
                for p, (a, b) in enumerate(PIECES):
                    for m in range(a, b):
                        e = turn(ps_T[0:T, p, (m - a) * T:(m - a + 1) * T], P[:, u, m * T:(m + 1) * T], ident[0:T, 0:T])
                    e.then_inc(s["Tp"], 1)

            def attend(G, h, part):
                ms = (range(0, NT // 2), range(NT // 2, NT), range(NT))[part]
                if part != 1:
                    pe.wait_ge(s["Te"], AHEAD + 3 * UNITS * G + 3 * (2 * h + 2))
                    if h < 2:
                        pe.wait_ge(s["zt"], AHEAD + 2 * G)
                    else:
                        pe.wait_ge(s["oT"], H * G + h - 1)
                for m in ms:
                    e = product(ps_q[:, h % 2, 0:W], lambda i: V[:, i, m, h * DH:(h + 1) * DH], lambda i: PT[:, h % 2, i, m, :],
                                m == 0, m == NT - 1)
                if part != 0:
                    e.then_inc(s["PV"], 1)

            def unit(G, k, last):
                n = k + 2
                if n < UNITS or not last:
                    scores(G + n // UNITS, UNITS * G + n, n % UNITS // 2, n % 2)
                turn_probs(UNITS * G + k, k % 2)

            def attn_first(G, before):
                for k in range(2):
                    unit(G, k, False)
                    if before and k == 0:
                        attend(G - 1, H - 1, 2)
                    elif before:
                        attn_project(G - 1)

            def attn_rest(G, last):
                for k in range(2, UNITS):
                    unit(G, k, last)
                    attend(G, k // 2 - 1, k % 2)

            def attn_project(G):
                pe.wait_ge(s["oT"], H * (G + 1))
                for u in range(2):
                    for k in range(KD):
                        e = mm(ps_q[0:T, u, :], outTg[:, k, u * T:(u + 1) * T], WO[:, k, :], start=(k == 0), stop=(k == KD - 1))
                    e.then_inc(s["wo_mm"], 1)

            def layer(l, last):
                pe.wait_ge(s["zct"], AHEAD + 2 * NC * l)
                settled(pe)
                with pe.Fori(0, NC - 1) as c:
                    project(l, c, True)
                project(l, NC - 1, False)
                pe.wait_ge(s["k_e"], AHEAD + KD * NC * (l + 1))
                for u in range(2):
                    scores(l * NC, UNITS * NC * l + u, 0, u)
                pe.wait_ge(s["v_e"], AHEAD + 2 * NC * (l + 1))
                settled(pe)
                attn_first(l * NC, False)
                pe.wait_ge(s["ldO"], 32 * (l + 1))
                settled(pe)
                with pe.Fori(0, NC - 1) as g_:
                    attn_rest(l * NC + g_, False)
                    attn_first(l * NC + g_ + 1, True)
                attn_rest(l * NC + NC - 1, True)
                pe.wait_ge(s["ttr"], AHEAD + UNITS * NC * (l + 1))
                pe.wait_ge(s["Te"], AHEAD + 3 * UNITS * NC * (l + 1))
                scale_bias(2 * NC * l + NC, 2 * l + 1)
                attend(l * NC + NC - 1, H - 1, 2)
                attn_project(l * NC + NC - 1)
                turn_y(2 * NC * l + NC)
                pe.wait_ge(s["zt"], AHEAD + 2 * NC * (l + 1))
                settled(pe)
                with pe.Fori(0, NC - 1) as c:
                    mlp(l, c, 2 * l + 1)
                mlp(l, NC - 1, None if last else 2 * l + 2)

            pe.wait_ge(s["ct_e"], AHEAD + 3 * NT)
            scale_bias(0, 0)
            turn_y(0)
            with pe.Fori(0, L - 1) as l:
                layer(l, False)
            layer(L - 1, True)

            fg = 2 * NC * L
            pe.wait_ge(s["wa"], AHEAD + 3 * L + 1)
            pe.wait_ge(s["zct"], AHEAD + 2 * NC * L)
            for c in range(NC):
                pe.wait_ge(s["yT"], AHEAD + 2 * (fg + c + 1))
                pe.wait_ge(s["g_hs"], 2 * c)
                for u in range(2):
                    nodes(u, yT, WV).then_inc(s["g_hs_mm"], 1)
                if c + 1 < NC:
                    turn_y(fg + c + 1)
            pe.wait_ge(s["g_diag"], 1)
            pe.wait_ge(s["onesr"], 1)
            for a, b in COLS:
                e = mm(psf[:, a:b], ones[:, :], diags[:, a:b], start=True, stop=True)
            e.then_inc(s["g_bc"], 1)
            pe.wait_ge(s["g_disb"], 1)
            pe.wait_ge(s["g_A"], 1)
            pe.wait_ge(s["g_hs"], NT)
            for j in range(KD):
                if j >= 2:
                    pe.wait_ge(s["g_agd"], j - 1)
                o = 1536 * (j % 2)
                for a, b in COLS:
                    for m in range(NT):
                        e = mm(psf[:, o + a:o + b], hs[:, m, j * 128:(j + 1) * 128], counts[:, m, a:b],
                               start=(m == 0), stop=(m == NT - 1))
                e.then_inc(s["g_ag"], 1)
            pe.wait_ge(s["g_agT"], KD)
            pe.wait_ge(s["ldG"], 16)
            for t in range(NT):
                if t >= 2:
                    pe.wait_ge(s["g_hs"], NT + t - 1)
                for k in range(KD):
                    e = mm(ps_q[0:T, t % 2, :], aggT[:, k, t * T:(t + 1) * T], W2[:, k, :], start=(k == 0), stop=(k == KD - 1))
                e.then_inc(s["g_hs_mm"], 1)
            pe.wait_ge(s["g_hs"], 2 * NT)
            for t in range(NT):
                if t >= 2:
                    pe.wait_ge(s["g_fin"], t - 1)
                for m in range(NT):
                    e = mm(ps[0:T, t % 2, :], counts[:, m, t * T:(t + 1) * T], hs[:, m, :], start=(m == 0), stop=(m == NT - 1))
                e.then_inc(s["g_ft"], 1)


_P = "L0_gnn_"
_INS = ["x", "src", "dst", "node_vec1"] + [_P + n for n in (
    "f_w1 f_b1 f_w2 f_b2 s1_w s1_b b1_w b1_b wq bq wk bk wv bv wo bo s2_w s2_b b2_w b2_b m_w1 m_b1 m_w2 m_b2").split()] + [
    "L1_gnn_W1", "L1_gnn_b1", "L1_gnn_W2", "L1_gnn_b2"]


def kernel(**inputs):
    import numpy as _np
    import concourse.bacc as _bacc
    from concourse import mybir as _mybir
    from concourse.bass_utils import run_bass_kernel_spmd as _run

    nc = _bacc.Bacc("TRN2", target_bir_lowering=False, num_devices=1, dynamic_dma_scratch_size=1024)
    arrays, args = {}, []
    for name in _INS:
        a = _np.ascontiguousarray(inputs[name])
        arrays[f"in_{name}_dram"] = a
        args.append(nc.dram_tensor(f"in_{name}_dram", a.shape, _mybir.dt.from_np(a.dtype), kind="ExternalInput").ap())
    args.append(nc.dram_tensor("out_0_dram", (N, D), F32, kind="ExternalOutput").ap())
    build(nc, *args)
    r = _run(nc, [arrays], core_ids=[0])
    return r.results[0]["out_0_dram"]
```
